# Optimizing a Trainium2 kernel written in Bass

```python
import numpy as np
import jax
import jax.numpy as jnp

def _softmax(x, axis=-1):
    return jax.nn.softmax(x, axis=axis)

def _gelu(x):
    return jax.nn.gelu(x, approximate=True)

def _silu(x):
    return jax.nn.silu(x)

def _sigmoid(x):
    return jax.nn.sigmoid(x)

def _layernorm(x, axis=-1, eps=1e-05):
    m = jnp.mean(x, axis=axis, keepdims=True)
    v = jnp.var(x, axis=axis, keepdims=True)
    return (x - m) / jnp.sqrt(v + eps)

def _scatter_add(tgt, idx, src, axis=0):
    return tgt.at[idx].add(src)

def _segment_sum(src, seg, n):
    return jax.ops.segment_sum(src, seg, n)
kernel_name = 'mk_early_fusion_d1_tok_img1024_r4_0a5bd6'

def setup_inputs(seed: int=0):
    np.random.seed(seed)
    _w = jnp.asarray

    def _rec_inputs():
        import jax
        import jax.numpy as jnp
        _rk = jax.random.key(seed)
        x = 7.22013e-05 + 1.00017 * jax.random.normal(jax.random.fold_in(_rk, 1), (32, 64, 256, 4), jnp.float32)
        txt = -1.32754e-10 + 0.999995 * jax.random.normal(jax.random.fold_in(_rk, 2), (32, 128, 256), jnp.float32)
        return (x, txt)
    x, txt = _rec_inputs()

    def _L0_tok_setup():
        import jax, jax.numpy as jnp
        import numpy as np
        B, F, L, H, D = (8, 64, 256, 4, 64)
        MODEL = H * F
        WIN = 128

        def _local_mask():
            m = np.ones((L, L), dtype=bool)
            m = np.tril(m, WIN - 1)
            m = np.triu(m, -(WIN - 1))
            return jnp.asarray(m)

        def _flatten(y):
            n = y.shape[0]
            return y.transpose(0, 2, 3, 1).reshape(n, L, -1)
        key = jax.random.key(seed)
        ks = jax.random.split(key, 12)
        s = lambda n: 1.0 / np.sqrt(n)
        xav = np.sqrt(6.0 / (L + L))
        return {'x': jax.random.normal(ks[0], (B, F, L, H), jnp.float32), 'Wq_w': jax.random.normal(ks[1], (D, F), jnp.float32) * s(F), 'Wq_b': jnp.zeros((D,), jnp.float32), 'Wk_w': jax.random.normal(ks[2], (D, F), jnp.float32) * s(F), 'Wk_b': jnp.zeros((D,), jnp.float32), 'Wv_w': jax.random.normal(ks[3], (D, F), jnp.float32) * s(F), 'Wv_b': jnp.zeros((D,), jnp.float32), 'w_bias': jax.random.uniform(ks[4], (L, L), jnp.float32, -xav, xav), 'out_w': jax.random.normal(ks[5], (H * D, MODEL), jnp.float32) * s(H * D), 'out_b': jnp.zeros((MODEL,), jnp.float32), 'ln_g': jnp.ones((MODEL,), jnp.float32), 'ln_b': jnp.zeros((MODEL,), jnp.float32), 'local_mask': _local_mask()}
    _L0_tok_all = _L0_tok_setup()
    _L0_tok_in = {k: v for k, v in _L0_tok_all.items() if k in ('Wq_w', 'Wq_b', 'Wk_w', 'Wk_b', 'Wv_w', 'Wv_b', 'w_bias', 'out_w', 'out_b', 'ln_g', 'ln_b', 'local_mask')}
    del _L0_tok_all

    def _L0_attn_setup():
        import jax, jax.numpy as jnp
        import numpy as np
        EMBED_DIM = 256
        NUM_HEADS = 16
        HEAD_DIM = EMBED_DIM // NUM_HEADS
        NUM_LANDMARKS = 64
        REG = 1e-06
        BATCH = 2
        SEQ = 2048

        def _sq_dists(X, L):
            Xn = jnp.sum(X * X, axis=-1, keepdims=True)
            Ln = jnp.sum(L * L, axis=-1, keepdims=True)
            XL = jnp.einsum('bhnd,bhkd->bhnk', X, L)
            return jnp.maximum(Xn + jnp.swapaxes(Ln, -2, -1) - 2.0 * XL, 0.0)
        key = jax.random.key(seed)
        ks = jax.random.split(key, 10)
        s = 0.02
        inp = {'query': jax.random.normal(ks[0], (BATCH, SEQ, EMBED_DIM), dtype=jnp.float32), 'Wq': jax.random.normal(ks[1], (EMBED_DIM, EMBED_DIM), dtype=jnp.float32) * s, 'bq': jnp.zeros((EMBED_DIM,), jnp.float32), 'Wk': jax.random.normal(ks[2], (EMBED_DIM, EMBED_DIM), dtype=jnp.float32) * s, 'bk': jnp.zeros((EMBED_DIM,), jnp.float32), 'Wv': jax.random.normal(ks[3], (EMBED_DIM, EMBED_DIM), dtype=jnp.float32) * s, 'bv': jnp.zeros((EMBED_DIM,), jnp.float32), 'Wo': jax.random.normal(ks[4], (EMBED_DIM, EMBED_DIM), dtype=jnp.float32) * s, 'bo': jnp.zeros((EMBED_DIM,), jnp.float32), 'temperature': jnp.asarray(float(HEAD_DIM), jnp.float32), 'landmark_idx': jnp.arange(NUM_LANDMARKS, dtype=jnp.int32) * (SEQ // NUM_LANDMARKS)}
        return inp
    _L0_attn_all = _L0_attn_setup()
    _L0_attn_in = {k: v for k, v in _L0_attn_all.items() if k in ('Wq', 'bq', 'Wk', 'bk', 'Wv', 'bv', 'Wo', 'bo', 'temperature', 'landmark_idx')}
    del _L0_attn_all

    def _L0_ffn_setup():
        import jax, jax.numpy as jnp
        import numpy as np
        B, S, D, H = (8, 256, 256, 1024)
        E, R = (3, 8)
        SCALING = 1.0 / R

        def _mole(x, W, b, A, Bm, Rw):
            gates = jax.nn.softmax(jnp.einsum('bsd,de->bse', x, Rw), axis=-1)
            base = jnp.einsum('bsd,dh->bsh', x, W) + b
            z = jnp.einsum('bsd,edr->ebsr', x, A)
            zg = z * jnp.transpose(gates, (2, 0, 1))[..., None]
            lora = jnp.einsum('ebsr,erh->bsh', zg, Bm)
            return base + SCALING * lora
        key = jax.random.key(seed)
        ks = jax.random.split(key, 12)
        s = lambda k, shape, scale: jax.random.normal(k, shape, dtype=jnp.float32) * scale
        return {'x': s(ks[0], (B, S, D), 1.0), 'W1': s(ks[1], (D, H), D ** (-0.5)), 'b1': jnp.zeros((H,), jnp.float32), 'A1': s(ks[2], (E, D, R), D ** (-0.5)), 'B1': s(ks[3], (E, R, H), 0.0) + s(ks[4], (E, R, H), R ** (-0.5)), 'R1': s(ks[5], (D, E), D ** (-0.5)), 'W2': s(ks[6], (H, D), H ** (-0.5)), 'b2': jnp.zeros((D,), jnp.float32), 'A2': s(ks[7], (E, H, R), H ** (-0.5)), 'B2': s(ks[8], (E, R, D), R ** (-0.5)), 'R2': s(ks[9], (H, E), H ** (-0.5))}
    _L0_ffn_all = _L0_ffn_setup()
    _L0_ffn_in = {k: v for k, v in _L0_ffn_all.items() if k in ('W1', 'b1', 'A1', 'B1', 'R1', 'W2', 'b2', 'A2', 'B2', 'R2')}
    del _L0_ffn_all
    return {'x': x, 'txt': txt, 'L0_tok_Wq_w': _L0_tok_in['Wq_w'], 'L0_tok_Wq_b': _L0_tok_in['Wq_b'], 'L0_tok_Wk_w': _L0_tok_in['Wk_w'], 'L0_tok_Wk_b': _L0_tok_in['Wk_b'], 'L0_tok_Wv_w': _L0_tok_in['Wv_w'], 'L0_tok_Wv_b': _L0_tok_in['Wv_b'], 'L0_tok_w_bias': _L0_tok_in['w_bias'], 'L0_tok_out_w': _L0_tok_in['out_w'], 'L0_tok_out_b': _L0_tok_in['out_b'], 'L0_tok_ln_g': _L0_tok_in['ln_g'], 'L0_tok_ln_b': _L0_tok_in['ln_b'], 'L0_tok_local_mask': _L0_tok_in['local_mask'], 'L0_attn_Wq': _L0_attn_in['Wq'], 'L0_attn_bq': _L0_attn_in['bq'], 'L0_attn_Wk': _L0_attn_in['Wk'], 'L0_attn_bk': _L0_attn_in['bk'], 'L0_attn_Wv': _L0_attn_in['Wv'], 'L0_attn_bv': _L0_attn_in['bv'], 'L0_attn_Wo': _L0_attn_in['Wo'], 'L0_attn_bo': _L0_attn_in['bo'], 'L0_attn_temperature': _L0_attn_in['temperature'], 'L0_attn_landmark_idx': _L0_attn_in['landmark_idx'], 'L0_ffn_W1': _L0_ffn_in['W1'], 'L0_ffn_b1': _L0_ffn_in['b1'], 'L0_ffn_A1': _L0_ffn_in['A1'], 'L0_ffn_B1': _L0_ffn_in['B1'], 'L0_ffn_R1': _L0_ffn_in['R1'], 'L0_ffn_W2': _L0_ffn_in['W2'], 'L0_ffn_b2': _L0_ffn_in['b2'], 'L0_ffn_A2': _L0_ffn_in['A2'], 'L0_ffn_B2': _L0_ffn_in['B2'], 'L0_ffn_R2': _L0_ffn_in['R2']}

def reference(x, txt, L0_tok_Wq_w, L0_tok_Wq_b, L0_tok_Wk_w, L0_tok_Wk_b, L0_tok_Wv_w, L0_tok_Wv_b, L0_tok_w_bias, L0_tok_out_w, L0_tok_out_b, L0_tok_ln_g, L0_tok_ln_b, L0_tok_local_mask, L0_attn_Wq, L0_attn_bq, L0_attn_Wk, L0_attn_bk, L0_attn_Wv, L0_attn_bv, L0_attn_Wo, L0_attn_bo, L0_attn_temperature, L0_attn_landmark_idx, L0_ffn_W1, L0_ffn_b1, L0_ffn_A1, L0_ffn_B1, L0_ffn_R1, L0_ffn_W2, L0_ffn_b2, L0_ffn_A2, L0_ffn_B2, L0_ffn_R2):
    import jax
    import jax.numpy as jnp

    def _L0_tok_ref(x, Wq_w, Wq_b, Wk_w, Wk_b, Wv_w, Wv_b, w_bias, out_w, out_b, ln_g, ln_b, local_mask):
        import jax, jax.numpy as jnp
        import numpy as np
        B, F, L, H, D = (8, 64, 256, 4, 64)
        MODEL = H * F
        WIN = 128

        def _local_mask():
            m = np.ones((L, L), dtype=bool)
            m = np.tril(m, WIN - 1)
            m = np.triu(m, -(WIN - 1))
            return jnp.asarray(m)

        def _flatten(y):
            n = y.shape[0]
            return y.transpose(0, 2, 3, 1).reshape(n, L, -1)

        def proj(w, b):
            y = jnp.einsum('nclh,dc->ndlh', x, w) + b[None, :, None, None]
            return _flatten(y)
        q = proj(Wq_w, Wq_b)
        k = proj(Wk_w, Wk_b)
        v = proj(Wv_w, Wv_b)
        wb = w_bias * local_mask.astype(w_bias.dtype)
        ew = jnp.exp(wb)
        ek = jnp.exp(k)
        num = jnp.einsum('ts,nsd->ntd', ew, ek * v)
        den = jnp.einsum('ts,nsd->ntd', ew, ek)
        y = jax.nn.sigmoid(q) * num / den
        h = y @ out_w + out_b + _flatten(x)
        mu = jnp.mean(h, axis=-1, keepdims=True)
        var = jnp.mean(jnp.square(h - mu), axis=-1, keepdims=True)
        return (h - mu) * jax.lax.rsqrt(var + 1e-05) * ln_g + ln_b

    def _L0_attn_ref(query, Wq, bq, Wk, bk, Wv, bv, Wo, bo, temperature, landmark_idx):
        import jax, jax.numpy as jnp
        import numpy as np
        EMBED_DIM = 256
        NUM_HEADS = 16
        HEAD_DIM = EMBED_DIM // NUM_HEADS
        NUM_LANDMARKS = 64
        REG = 1e-06
        BATCH = 2
        SEQ = 2048

        def _sq_dists(X, L):
            Xn = jnp.sum(X * X, axis=-1, keepdims=True)
            Ln = jnp.sum(L * L, axis=-1, keepdims=True)
            XL = jnp.einsum('bhnd,bhkd->bhnk', X, L)
            return jnp.maximum(Xn + jnp.swapaxes(Ln, -2, -1) - 2.0 * XL, 0.0)
        b, n, _ = query.shape
        Q = (query @ Wq.T + bq).reshape(b, n, NUM_HEADS, HEAD_DIM).transpose(0, 2, 1, 3)
        K = (query @ Wk.T + bk).reshape(b, n, NUM_HEADS, HEAD_DIM).transpose(0, 2, 1, 3)
        V = (query @ Wv.T + bv).reshape(b, n, NUM_HEADS, HEAD_DIM).transpose(0, 2, 1, 3)
        landmarks = K[:, :, landmark_idx, :]
        C_Q = _sq_dists(Q, landmarks)
        C_K = _sq_dists(K, landmarks)
        W_sq = C_K[:, :, landmark_idx, :]
        Phi_Q = jnp.exp(-C_Q / temperature)
        Phi_K = jnp.exp(-C_K / temperature)
        W_kernel = jnp.exp(-W_sq / temperature) + REG * jnp.eye(NUM_LANDMARKS, dtype=query.dtype)
        Z = jnp.einsum('bhnk,bhnd->bhkd', Phi_K, V)
        Y = jnp.linalg.solve(W_kernel, Z)
        out_unnorm = jnp.einsum('bhnk,bhkd->bhnd', Phi_Q, Y)
        Phi_K_sum = jnp.sum(Phi_K, axis=-2)[..., None]
        norm = jnp.einsum('bhnk,bhko->bhno', Phi_Q, jnp.linalg.solve(W_kernel, Phi_K_sum))
        norm = jnp.maximum(norm, 1e-10)
        out = out_unnorm / norm
        out = out.transpose(0, 2, 1, 3).reshape(b, n, EMBED_DIM)
        return out @ Wo.T + bo

    def _L0_ffn_ref(x, W1, b1, A1, B1, R1, W2, b2, A2, B2, R2):
        import jax, jax.numpy as jnp
        import numpy as np
        B, S, D, H = (8, 256, 256, 1024)
        E, R = (3, 8)
        SCALING = 1.0 / R

        def _mole(x, W, b, A, Bm, Rw):
            gates = jax.nn.softmax(jnp.einsum('bsd,de->bse', x, Rw), axis=-1)
            base = jnp.einsum('bsd,dh->bsh', x, W) + b
            z = jnp.einsum('bsd,edr->ebsr', x, A)
            zg = z * jnp.transpose(gates, (2, 0, 1))[..., None]
            lora = jnp.einsum('ebsr,erh->bsh', zg, Bm)
            return base + SCALING * lora
        h = _mole(x, W1, b1, A1, B1, R1)
        h = jax.nn.relu(h)
        return _mole(h, W2, b2, A2, B2, R2)
    h = _L0_tok_ref(x, L0_tok_Wq_w, L0_tok_Wq_b, L0_tok_Wk_w, L0_tok_Wk_b, L0_tok_Wv_w, L0_tok_Wv_b, L0_tok_w_bias, L0_tok_out_w, L0_tok_out_b, L0_tok_ln_g, L0_tok_ln_b, L0_tok_local_mask)
    h = jnp.concatenate([h, txt], axis=1)
    h = h + _L0_attn_ref(_layernorm(h, axis=-1), L0_attn_Wq, L0_attn_bq, L0_attn_Wk, L0_attn_bk, L0_attn_Wv, L0_attn_bv, L0_attn_Wo, L0_attn_bo, L0_attn_temperature, L0_attn_landmark_idx)
    h = h + _L0_ffn_ref(_layernorm(h, axis=-1), L0_ffn_W1, L0_ffn_b1, L0_ffn_A1, L0_ffn_B1, L0_ffn_R1, L0_ffn_W2, L0_ffn_b2, L0_ffn_A2, L0_ffn_B2, L0_ffn_R2)
    return h

_drawn_inputs = setup_inputs


def setup_inputs(seed=0):
    import zlib

    import numpy as np

    out = dict(_drawn_inputs(seed))
    spreads = {'L0_tok_Wq_b': (0.0, 2.0),
     'L0_tok_Wk_b': (0.0, 2.0),
     'L0_tok_Wv_b': (0.0, 0.1),
     'L0_tok_out_b': (0.0, 0.1),
     'L0_tok_ln_g': (1.0, 0.2),
     'L0_tok_ln_b': (0.0, 0.1),
     'L0_attn_bq': (0.0, 0.8),
     'L0_attn_bk': (0.0, 0.8),
     'L0_attn_bv': (0.0, 0.268),
     'L0_attn_bo': (0.0, 0.1),
     'L0_ffn_b1': (0.0, 0.1),
     'L0_ffn_b2': (0.0, 0.1)}
    factors = {'L0_tok_w_bias': 8.0, 'L0_attn_Wq': 8.0, 'L0_attn_Wk': 8.0, 'L0_attn_Wv': 4.573}
    for name, (base, spread) in spreads.items():
        noise = np.random.default_rng([zlib.crc32(name.encode()), seed]).standard_normal(out[name].shape)
        drawn = base * np.exp(spread * noise) if base else spread * noise
        out[name] = jnp.asarray(drawn.astype(out[name].dtype))
    for name, factor in factors.items():
        out[name] = (out[name] * factor).astype(out[name].dtype)
    return out
```

```python
from contextlib import ExitStack

import concourse.bass as bass
import numpy as np
from concourse import mybir

ALU = mybir.AluOpType
ACT = mybir.ActivationFunctionType
F32 = mybir.dt.float32
I32 = mybir.dt.int32
U8 = mybir.dt.uint8
AX_X = mybir.AxisListType.X

P = 128
N = 32
C, L, HT = 64, 256, 4
M = C * HT
NT = 3
T = NT * P
HA, DA = 16, 16
NL = 64
R = DA + 1
F = 1024
FC = F // P
E, RK = 3, 8
ER = E * RK
GATED = ER + E
NB = 8
SMALL = 16
EPS = 1e-5
REG = 1e-6


def constants(slots):
    hpc = P // slots
    chunks = HA // hpc
    p = np.arange(P)
    col = np.arange(P)
    bd = np.zeros((P, chunks // 2, P), np.float32)
    for q in range(chunks // 2):
        bd[:, q, :] = (p[:, None] // DA) == (q * hpc + col[None, :] // slots)
    bz = np.repeat((p[:, None] // slots) == np.arange(hpc)[None, :], R, axis=1).astype(np.float32)
    rd = (p[:, None] % slots == np.arange(slots)[None, :]).astype(np.float32)
    return bd, bz, rd


class Sample:

    def __init__(self, s, pair, par):
        self.s, self.pair, self.par = s, pair, par


class Signal:

    def __init__(self, sem, per=1):
        self.sem, self.per = sem, per


def wait(eng, signal, x, i=None, back=0):
    count = (x.s - back) * signal.per + (signal.per if i is None else i + 1)
    if isinstance(count, int) and count <= 0:
        return
    eng.wait_ge(signal.sem, count)


def wait_dma(eng, sems, x, back=0):
    count = (x.pair + 1 - back // 2) * 16
    if isinstance(count, int) and count <= 0:
        return
    eng.wait_ge(sems[x.par], count)


def idle(block, *engines):
    for name in engines:
        {"tensor": block.tensor, "scalar": block.scalar, "gpsimd": block.gpsimd}[name](lambda eng: None)


def pipeline(eng, stages, peel=4):

    def turn(t, pair, u):
        for skew, step in stages:
            if isinstance(t, int) and not 0 <= t - skew < N:
                continue
            step(Sample(t - skew, pair + (u - skew) // 2, (u - skew) % 2))

    for t in range(peel):
        turn(t, t // 2, t % 2)
    with eng.Fori(peel // 2, N // 2) as pair:
        for u in range(2):
            turn(pair * 2 + u, pair, u)
    for t in range(N, N + peel - 2):
        turn(t, t // 2, t % 2)


class Ring:

    def __init__(self, order, free, banks):
        assert len(order) % NB == 0, len(order)
        self.order, self.free, self.banks = order, free, banks
        self.place = {job[:2]: n for n, job in enumerate(order)}

    def bank(self, stage, i=0):
        return self.banks[self.place[stage, i] % NB]

    def wait(self, eng, stage, i, x, waited=()):
        n = self.place[stage, i]
        own = self.order[n][2]
        turn, back = x.s + own, 0
        while True:
            n -= NB
            if n < 0:
                n += len(self.order)
                back += 1
            before, j, skew = self.order[n]
            s = turn - back - skew
            if isinstance(s, int) and s >= N:
                continue
            if before in waited and own - back - skew <= 0:
                return
            wait(eng, self.free[before], Sample(s, None, None), j)
            return


def landmark_tables(nc, ins, slots, t):
    hpc = P // slots
    with ExitStack() as ctx, nc.Block() as block:
        def sb(name, shape, dt=F32):
            return ctx.enter_context(nc.sbuf_tensor(f"{name}_{slots}", shape, dt))

        idx_row = sb("idx_row", [P, NL], I32)
        idx_col = sb("idx_col", [NL, 1], I32)
        row_f = sb("row_f", [P, NL])
        col_f = sb("col_f", [NL, 1])
        neg_r = sb("neg_r", [P, NL])
        neg_c = sb("neg_c", [NL, 1])
        tri = sb("tri", [NL, 2, NL])
        iota = sb("iota", [NL, T])
        same = sb("same", [NL, 2, NL])
        count = sb("count", [NL, 2])
        first = sb("first", [NL, 1])
        rank = sb("rank", [NL, 1])
        pick = sb("pick", [NL, NL])
        spread = sb("spread", [NL, hpc, slots])
        hot = sb("hot", [NL, T])
        both = sb("both", [NL, 2])
        loaded = t.semaphore("tables_loaded")
        link_sem = t.semaphore("tables_step")
        product = t.semaphore("tables_product")
        loads = [(t.ident[:, :], ins["ident"]), (t.bd[:, :, :], ins[f"bd{slots}"]),
                 (t.bz[:, :, :].rearrange("p h r -> p (h r)"), ins[f"bz{slots}"]),
                 (t.diag[:, :], ins[f"diag{slots}"]), (t.rate[:, 0:1], ins["temperature"].broadcast_to([P, 1])),
                 (idx_row[:, :], ins["idx"].broadcast_to([P, NL])), (idx_col[:, :], ins["idx"].rearrange("a n -> n a")),
                 (tri[:, :, :], ins["tri"]), (iota[:, :], ins["iota"].broadcast_to([NL, T]))]
        idle(block, "scalar", "gpsimd")
        known = {}

        @block.sync
        def _(sy):
            for dst, src in loads:
                sy.dma_start(dst, src).then_inc(loaded, 16)

        @block.vector
        def _(ve):
            n = [0]

            def link(instruction):
                n[0] += 1
                instruction.then_inc(link_sem, 1)
                ve.wait_ge(link_sem, n[0])

            ve.wait_ge(loaded, 16 * len(loads))
            link(ve.memset(t.ones[:, :], 1.0))
            link(ve.reciprocal(t.rate[:, 1:2], t.rate[:, 0:1]))
            link(ve.tensor_scalar(t.rate[:, 0:1], t.rate[:, 1:2], -1.0, None, ALU.mult))
            for raw, f, neg in ((idx_row, row_f, neg_r), (idx_col, col_f, neg_c)):
                link(ve.tensor_copy(f[:, :], raw[:, :]))
                link(ve.tensor_scalar(neg[:, :], f[:, :], 0.0, float(T), ALU.is_lt, ALU.mult))
                link(ve.tensor_tensor(f[:, :], f[:, :], neg[:, :], ALU.add))
                link(ve.tensor_scalar(f[:, :], f[:, :], 0.0, float(T - 1), ALU.max, ALU.min))
            link(ve.tensor_scalar(same[:, 1, :], row_f[0:NL, :], col_f[:, 0:1], None, ALU.is_equal))
            link(ve.tensor_tensor(same[:, 0, :], same[:, 1, :], tri[:, 0, :], ALU.mult))
            link(ve.tensor_reduce(count[:, :], same[:, :, :], AX_X, ALU.add))
            link(ve.tensor_scalar(first[:, :], count[:, 0:1], 0.0, None, ALU.is_equal))
            known["first"] = n[0]
            ve.wait_ge(product, 1)
            link(ve.tensor_copy(rank[:, :], t.banks[0][0:NL, 0:1]))
            link(ve.tensor_scalar(pick[:, :], iota[:, 0:NL], rank[:, 0:1], first[:, 0:1], ALU.is_equal, ALU.mult))
            for h in range(hpc):
                link(ve.tensor_copy(spread[:, h, :], pick[:, 0:slots]))
            link(ve.tensor_scalar(hot[:, :], iota[:, :], col_f[:, 0:1], None, ALU.is_equal))
            link(ve.tensor_copy(both[:, 0:1], count[:, 1:2]))
            link(ve.memset(both[:, 1:2], 1.0))
            known["all"] = n[0]
            ve.wait_ge(product, 2)
            for c in range(NT):
                link(ve.tensor_copy(t.gather[:, c, :], t.banks[1][:, c * slots:(c + 1) * slots]))
            link(ve.tensor_copy(t.reg[:, 0:2], t.banks[2][:, 0:2]))
            link(ve.tensor_scalar(t.reg[:, 2:3], t.reg[:, 0:1], 1.0, None, ALU.max))
            link(ve.reciprocal(t.reg[:, 3:4], t.reg[:, 2:3]))
            link(ve.tensor_scalar(t.reg[:, 2:3], t.reg[:, 3:4], REG, t.reg[:, 1:2], ALU.mult, ALU.mult))
            link(ve.tensor_scalar(t.reg[:, 3:4], t.reg[:, 1:2], -1.0, 1.0, ALU.mult, ALU.add))
            link(ve.tensor_tensor(t.reg[:, 2:3], t.reg[:, 2:3], t.reg[:, 3:4], ALU.add))
            link(ve.tensor_scalar(t.regd[:, :], t.diag[:, :], t.reg[:, 2:3], None, ALU.mult))

        @block.tensor
        def _(pe):
            pe.wait_ge(link_sem, known["first"])
            pe.matmul(t.banks[0][0:NL, 0:1], tri[:, 1, :], first[:, :], start=True, stop=True).then_inc(product, 1)
            pe.wait_ge(link_sem, known["all"])
            pe.matmul(t.banks[2][:, 0:2], spread[:, :, :].rearrange("p h k -> p (h k)"), both[:, :],
                      start=True, stop=True)
            for c in range(NT):
                mm = pe.matmul(t.banks[1][:, c * slots:(c + 1) * slots], hot[:, c * P:(c + 1) * P],
                               pick[:, 0:slots], start=True, stop=True, skip_group_check=True)
            mm.then_inc(product, 1)


def count_tokens(nc, ins, number):
    with ExitStack() as ctx, nc.Block() as block:
        def sb(name, shape, dt=F32):
            return ctx.enter_context(nc.sbuf_tensor(name, shape, dt))

        idx = sb("count_idx", [1, NL], I32)
        f = sb("count_f", [1, NL])
        neg = sb("count_neg", [1, NL])
        lower = sb("count_lower", [1, NL, NL])
        same = sb("count_same", [1, NL, NL])
        earlier = sb("count_earlier", [1, NL])
        first = sb("count_first", [1, NL])
        total = sb("count_total", [1, 1])
        loaded = ctx.enter_context(nc.semaphore("count_loaded"))
        link_sem = ctx.enter_context(nc.semaphore("count_step"))
        idle(block, "tensor", "scalar", "gpsimd")

        @block.sync
        def _(sy):
            sy.dma_start(idx[:, :], ins["idx"]).then_inc(loaded, 16)
            sy.dma_start(lower[:, :, :].rearrange("a i j -> a (i j)"), ins["lower"]).then_inc(loaded, 16)

        @block.vector
        def _(ve):
            n = [0]

            def link(instruction):
                n[0] += 1
                instruction.then_inc(link_sem, 1)
                ve.wait_ge(link_sem, n[0])

            ve.wait_ge(loaded, 32)
            link(ve.tensor_copy(f[:, :], idx[:, :]))
            link(ve.tensor_scalar(neg[:, :], f[:, :], 0.0, float(T), ALU.is_lt, ALU.mult))
            link(ve.tensor_tensor(f[:, :], f[:, :], neg[:, :], ALU.add))
            link(ve.tensor_scalar(f[:, :], f[:, :], 0.0, float(T - 1), ALU.max, ALU.min))
            link(ve.tensor_tensor(same[:, :, :], f[:, :].unsqueeze(2).broadcast_to([1, NL, NL]),
                                  f[:, :].unsqueeze(1).broadcast_to([1, NL, NL]), ALU.is_equal))
            link(ve.tensor_tensor(same[:, :, :], same[:, :, :], lower[:, :, :], ALU.mult))
            link(ve.tensor_reduce(earlier[:, :], same[:, :, :], AX_X, ALU.add))
            link(ve.tensor_scalar(first[:, :], earlier[:, :], 0.0, None, ALU.is_equal))
            link(ve.tensor_reduce(total[:, :], first[:, :], AX_X, ALU.add))
            link(ve.tensor_copy(number[:, :], total[:, :]))


RSQRT_STEPS = 18
RSQRT_SEED = 0x5F3759DF


def inverse_deviation(ve, x, ST, RS, made):
    y, neg, v, w, total, gap = (RS[:, i, :] for i in range(6))
    n = [0]

    def link(instruction):
        instruction.then_inc(made.sem, 1)
        wait(ve, made, x, n[0])
        n[0] += 1

    link(ve.tensor_tensor(total, ST[:, :, 1], ST[:, :, 4], ALU.add))
    link(ve.tensor_tensor(gap, ST[:, :, 1], ST[:, :, 4], ALU.subtract))
    link(ve.tensor_tensor(v, ST[:, :, 2], ST[:, :, 5], ALU.add))
    link(ve.scalar_tensor_tensor(out=gap, in0=gap, scalar=0.25, in1=gap, op0=ALU.mult, op1=ALU.mult))
    link(ve.tensor_scalar(v, v, 1.0 / M, EPS, ALU.mult, ALU.add))
    link(ve.tensor_tensor(v, v, gap, ALU.add))
    link(ve.tensor_scalar(w.bitcast(I32), v.bitcast(I32), 1, None, ALU.logical_shift_right))
    link(ve.tensor_scalar(y.bitcast(I32), w.bitcast(I32), -1, RSQRT_SEED, ALU.mult, ALU.add))
    for _ in range(3):
        link(ve.tensor_tensor(w, y, y, ALU.mult))
        link(ve.scalar_tensor_tensor(out=w, in0=w, scalar=-0.5, in1=v, op0=ALU.mult, op1=ALU.mult))
        link(ve.scalar_tensor_tensor(out=y, in0=w, scalar=1.5, in1=y, op0=ALU.add, op1=ALU.mult))
    ve.scalar_tensor_tensor(out=neg, in0=total, scalar=-0.5, in1=y, op0=ALU.mult, op1=ALU.mult)\
        .then_inc(made.sem, 1)

def systems_phase(nc, ins, t, slots, spill):
    hpc = P // slots
    CH = HA // hpc
    CPO = CH // 2
    TL = T + slots
    TB = max(1, CH * P // 512)
    TW = CH * P // TB
    ZB = 1 if slots == SMALL else 2
    CZ = CH // ZB
    sfx = f"_{slots}"
    with ExitStack() as ctx, nc.Block() as block:
        def sb(name, shape, dt=F32):
            return ctx.enter_context(nc.sbuf_tensor("a_" + name + sfx, shape, dt))

        def sem(name):
            return t.semaphore("a_" + name)

        wkv = sb("wkv", [C + 1, 2 * C])
        wq = sb("wq", [C + 1, C])
        res = sb("res", [C + 1, HT, C])
        ow = sb("ow", [P, 2, M])
        ew = sb("ew", [P, 2, L])
        mask8 = sb("mask8", [P, 2, L // 4], I32)
        maskf = sb("maskf", [P, 2, L])
        ln_g = sb("ln_g", [P, M])
        ln_b = sb("ln_b", [P, M])
        wa = {n: sb("attn_w" + n, [P, 2, M]) for n in "qkv"}
        ba = {n: sb("attn_b" + n, [P, 2]) for n in "qk"}
        bv = sb("bv", [P, M])
        X = sb("x", [C + 1, 2, L, HT])
        EK = sb("ek", [P, 2, 2, 2, M])
        EQ = sb("eq", [P, 2, 2, L])
        DE = sb("de", [P, 2, L])
        YT = sb("yt", [P, 2, 2, L])
        ST1, RS1 = sb("st1", [P, 2, 6]), sb("rs1", [P, 6, 2])
        ST2, RS2 = sb("st2", [P, NT, 6]), sb("rs2", [P, 6, NT])
        H0 = sb("h0", [P, 2, M])
        H = sb("h", [P, 2, NT, M])
        XN = sb("xn", [P, 2, NT, M])
        XT = sb("xt", [P, 2, TL])
        KT, KS = sb("kt", [P, 2, TL]), sb("ks", [P, 2, TL])
        QT, QS = sb("qt", [P, 2, T]), sb("qs", [P, 2, T])
        VA = sb("va", [P, 2, NT, HA, R])
        LL, LS = sb("ll", [P, CH, P]), sb("ls", [P, CH, P])
        LN = sb("ln", [P, CH])
        CK = sb("ck", [P, 2, TL])
        PK = sb("pk", [P, 2, CH, TL])
        PQ = sb("pq", [P, 2, CH, T])
        PN = sb("pn", [P, NT, CH * P])
        ZM = sb("zm", [P, CZ, hpc, R])
        Z = sb("z", [P, 2, CH, R])
        W = sb("w", [P, 2, CH, slots])

        order = ([("kv", 0, 0), ("kv", 1, 0), ("q", 0, 0)] + [("t", i, 2) for i in range(NT * TB)]
                 + [("xt", 0, 1), ("xt", 1, 1), ("den", 0, 0), ("num", 0, 0)] + [("z", i, 2) for i in range(ZB)]
                 + [("ak", 0, 1), ("ak", 1, 1), ("aq", 0, 1), ("aq", 1, 1), ("h", 0, 0)]
                 + [("v", i, 1) for i in range(NT)] + [("ln", 0, 1)]
                 + [("ck", i, 1) for i in range(CH)] + [("cq", i, 1) for i in range(CH)])
        per = {stage: sum(1 for job in order if job[0] == stage) for stage, _, _ in order}
        ready = {s: Signal(sem("ready_" + s), n) for s, n in per.items()}
        free = {s: Signal(sem("free_" + s), n) for s, n in per.items()}
        ring = Ring(order, free, t.banks)
        weights = sem("weights")
        mask_ready = sem("mask_ready")
        ew_ready = sem("ew_ready")
        ones_set = sem("ones_set")
        x_loaded = [sem(f"x_loaded{i}") for i in range(2)]
        txt_loaded = [sem(f"txt_loaded{i}") for i in range(2)]
        h_stored = [sem(f"h_stored{i}") for i in range(2)]
        pq_stored = [sem(f"pq_stored{i}") for i in range(2)]
        z_stored = [sem(f"z_stored{i}") for i in range(2)]
        w_stored = [sem(f"w_stored{i}") for i in range(2)]
        ek_made = Signal(sem("ek_made"), 2)
        de_made = Signal(sem("de_made"), 1)
        stat1 = Signal(sem("stat1"), 2)
        rs1_made = Signal(sem("rs1_made"), RSQRT_STEPS)
        hg_made = Signal(sem("hg_made"), 1)
        h_made = Signal(sem("h_made"), 1)
        stat2 = Signal(sem("stat2"), NT)
        rs2_made = Signal(sem("rs2_made"), RSQRT_STEPS)
        xn_made = Signal(sem("xn_made"), NT)
        k_made = Signal(sem("k_made"), 2)
        ll_made = Signal(sem("ll_made"), CH)
        ls_made = Signal(sem("ls_made"), 1)
        pk_made = Signal(sem("pk_made"), CH)
        pq_made = Signal(sem("pq_made"), CH)
        zr_made = Signal(sem("zr_made"), ZB)
        z_made = Signal(sem("z_made"), ZB)
        w0_made = Signal(sem("w0_made"), 1)
        w_made = Signal(sem("w_made"), 1)
        loads = [(wkv[:, :], ins["wkv"]), (wq[:, :], ins["wq_tok"]), (res[:, :, :], ins["res"]),
                 (ow[:, :, :], ins["ow"]), (ew[:, :, :], ins["w_bias"]), (mask8[:, :, :], ins["mask"]),
                 (ln_g[:, :], ins["ln_g"].broadcast_to([P, M])), (ln_b[:, :], ins["ln_b"].broadcast_to([P, M])),
                 (bv[:, :], ins["bv"].broadcast_to([P, M])), (ba["q"][:, :], ins["bq"]), (ba["k"][:, :], ins["bk"])]
        loads += [(wa[n][:, :, :], ins["wa_" + n]) for n in "qkv"]
        loads += [(X[C:C + 1, u, :, :].rearrange("p l h -> p (l h)"), ins["one_row"]) for u in range(2)]

        @block.sync
        def _(sy):
            for dst, src in loads:
                sy.dma_start(dst, src).then_inc(weights, 16)

            def load(x):
                wait(sy, ready["h"], x, back=2)
                sy.dma_start(X[0:C, x.par, :, :].rearrange("p l h -> p (l h)"),
                             ins["x"][bass.ds(x.s, 1)].rearrange("n c l -> c (n l)")).then_inc(x_loaded[x.par], 16)
                wait_dma(sy, h_stored, x, back=2)
                wait(sy, xn_made, x, back=2)
                sy.dma_start(H[:, x.par, 2, :], ins["txt"][bass.ds(x.s, 1)].rearrange("n p m -> p (n m)"))\
                    .then_inc(txt_loaded[x.par], 16)

            def store_h(x):
                wait(sy, h_made, x)
                sy.dma_start(spill.h[bass.ds(x.s, 1)].rearrange("n p k -> p (n k)"),
                             H[:, x.par, :, :].rearrange("p c m -> p (c m)")).then_inc(h_stored[x.par], 16)

            def store_pq(x):
                wait(sy, pq_made, x)
                sy.dma_start(spill.pq[bass.ds(x.s, 1)].rearrange("n p k -> p (n k)"),
                             PQ[:, x.par, :, :].rearrange("p c m -> p (c m)")).then_inc(pq_stored[x.par], 16)

            def store_system(x):
                rows = bass.ds(x.s * (HA * slots), HA * slots)
                wait(sy, w_made, x)
                sy.dma_start(spill.w[rows, :].rearrange("(q p) k -> p q k", p=P), W[:, x.par, :, :])\
                    .then_inc(w_stored[x.par], 16)
                wait(sy, z_made, x)
                sy.dma_start(spill.z[rows, :].rearrange("(q p) k -> p q k", p=P), Z[:, x.par, :, :])\
                    .then_inc(z_stored[x.par], 16)

            pipeline(sy, [(0, load), (1, store_h), (2, store_pq), (2, store_system)])
            for stored in (h_stored, pq_stored, z_stored, w_stored):
                for i in range(2):
                    sy.wait_ge(stored[i], 16 * N // 2)

        @block.tensor
        def _(pe):
            def kv(i):
                def step(x):
                    wait_dma(pe, x_loaded, x)
                    ring.wait(pe, "kv", i, x)
                    o = ring.bank("kv", i)[:, :].rearrange("p (a n) -> p a n", a=2)
                    for h in range(HT):
                        mm = pe.matmul(o[:, :, h * C:(h + 1) * C], X[:, x.par, i * P:(i + 1) * P, h],
                                       wkv[:, :].rearrange("p (a n) -> p a n", a=2), start=True, stop=True,
                                       skip_group_check=True)
                    mm.then_inc(ready["kv"].sem, 1)
                return step

            def q(i):
                def step(x):
                    ring.wait(pe, "q", i, x)
                    for h in range(HT):
                        mm = pe.matmul(ring.bank("q")[(h % 2) * C:(h % 2 + 1) * C, (h // 2) * L:(h // 2 + 1) * L],
                                       wq[:, :], X[:, x.par, :, h], start=True, stop=True, skip_group_check=True)
                    mm.then_inc(ready["q"].sem, 1)
                return step

            def mix(stage, which):
                def step(x):
                    wait(pe, free["kv"] if which else ek_made, x)
                    ring.wait(pe, stage, 0, x)
                    for hp in range(2):
                        for sc in range(2):
                            mm = pe.matmul(ring.bank(stage)[:, hp * L:(hp + 1) * L],
                                           EK[:, x.par, sc, which, hp * P:(hp + 1) * P], ew[:, sc, :],
                                           start=(sc == 0), stop=(sc == 1), skip_group_check=True)
                    mm.then_inc(ready[stage].sem, 1)
                return step

            def h(i):
                def step(x):
                    wait(pe, free["num"], x)
                    ring.wait(pe, "h", i, x, ("num",))
                    for tc in range(2):
                        o = ring.bank("h")[:, tc * M:(tc + 1) * M]
                        for hp in range(2):
                            pe.matmul(o, YT[:, x.par, hp, tc * P:(tc + 1) * P], ow[:, hp, :],
                                      start=(hp == 0), stop=False, skip_group_check=True)
                        for hh in range(HT):
                            mm = pe.matmul(o[:, hh * C:(hh + 1) * C], X[:, x.par, tc * P:(tc + 1) * P, hh],
                                           res[:, hh, :], start=False, stop=(hh == HT - 1), skip_group_check=True)
                    mm.then_inc(ready["h"].sem, 1)
                return step

            def xt(i):
                def step(x):
                    wait(pe, xn_made, x)
                    ring.wait(pe, "xt", i, x)
                    o = ring.bank("xt", i)
                    for c in range(NT):
                        pe.transpose(o[:, c * P:(c + 1) * P], XN[:, x.par, c, i * P:(i + 1) * P], t.ident[:, :])
                    for c in range(NT):
                        mm = pe.matmul(o[:, T:TL], XN[:, x.par, c, i * P:(i + 1) * P], t.gather[:, c, :],
                                       start=(c == 0), stop=(c == NT - 1), skip_group_check=True)
                    mm.then_inc(ready["xt"].sem, 1)
                return step

            def project(stage, i):
                w, width = (wa["k"], TL) if stage == "ak" else (wa["q"], T)

                def step(x):
                    wait(pe, free["xt"], x)
                    ring.wait(pe, stage, i, x, ("xt",))
                    for kc in range(2):
                        mm = pe.matmul(ring.bank(stage, i)[:, 0:width], w[:, kc, i * P:(i + 1) * P],
                                       XT[:, kc, 0:width], start=(kc == 0), stop=(kc == 1))
                    mm.then_inc(ready[stage].sem, 1)
                return step

            def v(i):
                def step(x):
                    ring.wait(pe, "v", i, x)
                    for kc in range(2):
                        mm = pe.matmul(ring.bank("v", i)[:, 0:M], XT[:, kc, i * P:(i + 1) * P], wa["v"][:, kc, :],
                                       start=(kc == 0), stop=(kc == 1))
                    mm.then_inc(ready["v"].sem, 1)
                return step

            def ln(i):
                def step(x):
                    wait(pe, ls_made, x)
                    ring.wait(pe, "ln", i, x)
                    for c in range(CH):
                        mm = pe.matmul(ring.bank("ln")[:, c:c + 1], LS[:, c, :], t.ones[:, :], start=True,
                                       stop=True, skip_group_check=True)
                    mm.then_inc(ready["ln"].sem, 1)
                return step

            def distance(stage, i):
                src, sq, width, made = (KT, KS, TL, "ak") if stage == "ck" else (QT, QS, T, "aq")

                def step(x):
                    wait(pe, free[made], x)
                    wait(pe, ll_made, x)
                    ring.wait(pe, stage, i, x, (made,))
                    o = ring.bank(stage, i)[:, 0:width]
                    pe.matmul(o, LL[:, i, :], src[:, i // CPO, 0:width], start=True, stop=False)
                    pe.matmul(o, t.bd[:, i % CPO, :], sq[:, i // CPO, 0:width], start=False, stop=True)\
                        .then_inc(ready[stage].sem, 1)
                return step

            def turned(i):
                c, b = i // TB, i % TB

                def step(x):
                    wait(pe, pk_made, x)
                    ring.wait(pe, "t", i, x)
                    for n in range(TW // P):
                        mm = pe.transpose(ring.bank("t", i)[:, n * P:(n + 1) * P],
                                          PK[:, x.par, b * (TW // P) + n, c * P:(c + 1) * P], t.ident[:, :])
                    mm.then_inc(ready["t"].sem, 1)
                return step

            def z(i):
                def step(x):
                    wait(pe, free["t"], x)
                    wait(pe, free["v"], x)
                    ring.wait(pe, "z", i, x, ("v", "t",))
                    for n in range(CZ):
                        c = i * CZ + n
                        for k in range(NT):
                            mm = pe.matmul(ring.bank("z", i)[:, n * hpc * R:(n + 1) * hpc * R],
                                           PN[:, k, c * P:(c + 1) * P],
                                           VA[:, x.par, k, c * hpc:(c + 1) * hpc, :].rearrange("p h r -> p (h r)"),
                                           start=(k == 0), stop=(k == NT - 1), skip_group_check=True)
                    mm.then_inc(ready["z"].sem, 1)
                return step

            step_of = {"kv": kv, "q": q, "h": h, "xt": xt, "v": v, "ln": ln, "t": turned, "z": z,
                       "den": lambda i: mix("den", 0), "num": lambda i: mix("num", 1)}
            step_of |= {s: (lambda i, s=s: project(s, i)) for s in ("ak", "aq")}
            step_of |= {s: (lambda i, s=s: distance(s, i)) for s in ("ck", "cq")}
            pe.wait_ge(weights, 16 * len(loads))
            pe.wait_ge(ew_ready, 1)
            pipeline(pe, [(skew, step_of[stage](i)) for stage, i, skew in order])

        @block.scalar
        def _(act):
            act.wait_ge(weights, 16 * len(loads))
            act.wait_ge(mask_ready, 2)
            act.activation(ew[:, :, :], maskf[:, :, :], ACT.Exp).then_inc(ew_ready, 1)

            def exp_k(x):
                for i in range(2):
                    wait(act, ready["kv"], x, i)
                    wait(act, ready["num"], x, back=2)
                    act.activation(EK[:, x.par, i, 0, :], ring.bank("kv", i)[:, 0:M], ACT.Exp).then_inc(ek_made.sem, 1)

            def exp_q(x):
                wait(act, ready["q"], x)
                wait(act, free["den"], x, back=2)
                act.activation(EQ[:, x.par, :, :].rearrange("p a l -> p (a l)"), ring.bank("q")[:, :], ACT.Exp,
                               scale=-1.0).then_inc(free["q"].sem, 1)

            def norm1(x):
                wait(act, rs1_made, x)
                wait(act, hg_made, x, back=1)
                for i in range(2):
                    o = act.activation(H0[:, i, :], ring.bank("h")[:, i * M:(i + 1) * M], ACT.Identity,
                                       bias=RS1[:, 1, i:i + 1], scale=RS1[:, 0, i:i + 1])
                o.then_inc(free["h"].sem, 1)

            def norm2(x):
                wait(act, rs2_made, x)
                wait(act, ready["xt"], x, back=2)
                for i in range(NT):
                    act.activation(XN[:, x.par, i, :], H[:, x.par, i, :], ACT.Identity,
                                   bias=RS2[:, 1, i:i + 1], scale=RS2[:, 0, i:i + 1]).then_inc(xn_made.sem, 1)

            def take_xt(x):
                for i in range(2):
                    wait(act, ready["xt"], x, i)
                    wait(act, ready["v"], x, back=1)
                    act.activation(XT[:, i, :], ring.bank("xt", i)[:, 0:TL], ACT.Copy).then_inc(free["xt"].sem, 1)

            def take_k(x):
                for i in range(2):
                    wait(act, ready["ak"], x, i)
                    wait(act, ready["ck"], x, back=1)
                    wait(act, ll_made, x, back=1)
                    act.activation(KT[:, i, :], ring.bank("ak", i)[:, 0:TL], ACT.Identity,
                                   bias=ba["k"][:, i:i + 1]).then_inc(k_made.sem, 1)
                    act.activation(KS[:, i, :], ring.bank("ak", i)[:, 0:TL], ACT.Square,
                                   bias=ba["k"][:, i:i + 1]).then_inc(free["ak"].sem, 1)

            def take_q(x):
                for i in range(2):
                    wait(act, ready["aq"], x, i)
                    wait(act, ready["cq"], x, back=1)
                    act.activation(QT[:, i, :], ring.bank("aq", i)[:, 0:T], ACT.Identity, bias=ba["q"][:, i:i + 1])
                    act.activation(QS[:, i, :], ring.bank("aq", i)[:, 0:T], ACT.Square,
                                   bias=ba["q"][:, i:i + 1]).then_inc(free["aq"].sem, 1)

            def square_l(x):
                wait(act, ll_made, x)
                wait(act, ready["ln"], x, back=1)
                act.activation(LS[:, :, :], LL[:, :, :], ACT.Square, scale=0.5).then_inc(ls_made.sem, 1)

            def take_ln(x):
                wait(act, ready["ln"], x)
                wait(act, free["cq"], x, back=1)
                act.activation(LN[:, :], ring.bank("ln")[:, 0:CH], ACT.Copy).then_inc(free["ln"].sem, 1)

            def kernels(x):
                for i in range(CH):
                    wait(act, free["ck"], x, i)
                    wait(act, ready["t"], x, back=2)
                    wait(act, w0_made, x, back=2)
                    act.activation(PK[:, x.par, i, :], CK[:, i % 2, :], ACT.Exp, scale=t.rate[:, 0:1])\
                        .then_inc(pk_made.sem, 1)
                for i in range(CH):
                    wait(act, free["cq"], x, i)
                    wait_dma(act, pq_stored, x, back=2)
                    act.activation(PQ[:, x.par, i, :], CK[:, i % 2, 0:T], ACT.Exp, scale=t.rate[:, 0:1])\
                        .then_inc(pq_made.sem, 1)

            pipeline(act, [(0, exp_k), (0, exp_q), (1, take_xt), (1, take_k), (1, take_q), (1, square_l),
                           (0, norm1), (1, take_ln), (1, kernels), (0, norm2)])

        @block.gpsimd
        def _(po):
            po.memset(VA[:, :, :, :, DA:R], 1.0).then_inc(ones_set, 1)
            po.wait_ge(weights, 16 * len(loads))

            def affine(x):
                wait(po, free["h"], x)
                wait(po, xn_made, x, back=2)
                wait_dma(po, h_stored, x, back=2)
                po.tensor_tensor(H[:, x.par, 0:2, :], H0[:, :, :], ln_g[:, :].unsqueeze(1).broadcast_to([P, 2, M]),
                                 ALU.mult).then_inc(hg_made.sem, 1)
                wait(po, hg_made, x)
                wait_dma(po, txt_loaded, x)
                po.tensor_tensor(H[:, x.par, 0:2, :], H[:, x.par, 0:2, :],
                                 ln_b[:, :].unsqueeze(1).broadcast_to([P, 2, M]), ALU.add).then_inc(h_made.sem, 1)

            def system(x):
                wait(po, pk_made, x)
                wait_dma(po, w_stored, x, back=2)
                po.tensor_tensor(W[:, x.par, :, :], PK[:, x.par, :, T:TL],
                                 t.reg[:, 1:2].unsqueeze(1).broadcast_to([P, CH, slots]), ALU.mult)\
                    .then_inc(w0_made.sem, 1)
                wait(po, w0_made, x)
                po.tensor_tensor(W[:, x.par, :, :], W[:, x.par, :, :],
                                 t.regd[:, :].unsqueeze(1).broadcast_to([P, CH, slots]), ALU.add).then_inc(w_made.sem, 1)

            pipeline(po, [(0, affine), (1, system)])

        @block.vector
        def _(ve):
            ve.wait_ge(weights, 16 * len(loads))
            ve.tensor_copy(maskf[:, :, :], mask8[:, :, :].bitcast(U8)).then_inc(mask_ready, 1)
            ve.wait_ge(mask_ready, 1)
            ve.tensor_tensor(maskf[:, :, :], maskf[:, :, :], ew[:, :, :], ALU.mult).then_inc(mask_ready, 1)
            ve.wait_ge(ones_set, 1)

            def v_exp_k(x):
                for i in range(2):
                    wait(ve, ek_made, x, i)
                    wait(ve, ready["num"], x, back=2)
                    ve.tensor_tensor(EK[:, x.par, i, 1, :], EK[:, x.par, i, 0, :], ring.bank("kv", i)[:, M:2 * M],
                                     ALU.mult).then_inc(free["kv"].sem, 1)

            def y(x):
                wait(ve, ready["den"], x)
                wait(ve, free["q"], x)
                wait(ve, free["num"], x, back=1)
                ve.scalar_tensor_tensor(out=DE[:, :, :], in0=EQ[:, x.par, :, :], scalar=1.0,
                                        in1=ring.bank("den")[:, :].rearrange("p (a l) -> p a l", a=2),
                                        op0=ALU.add, op1=ALU.mult).then_inc(free["den"].sem, 1)
                wait(ve, free["den"], x)
                ve.reciprocal(DE[:, :, :], DE[:, :, :]).then_inc(de_made.sem, 1)
                wait(ve, de_made, x)
                wait(ve, ready["num"], x)
                wait(ve, ready["h"], x, back=2)
                ve.tensor_tensor(YT[:, x.par, :, :], DE[:, :, :],
                                 ring.bank("num")[:, :].rearrange("p (a l) -> p a l", a=2), ALU.mult)\
                    .then_inc(free["num"].sem, 1)

            def stats1(x):
                wait(ve, ready["h"], x)
                for i in range(2):
                    ve.bn_stats(ST1[:, i, :], ring.bank("h")[:, i * M:(i + 1) * M]).then_inc(stat1.sem, 1)
                wait(ve, stat1, x)
                wait(ve, free["h"], x, back=1)
                inverse_deviation(ve, x, ST1, RS1, rs1_made)

            def stats2(x):
                wait(ve, h_made, x)
                for i in range(NT):
                    ve.bn_stats(ST2[:, i, :], H[:, x.par, i, :]).then_inc(stat2.sem, 1)
                wait(ve, stat2, x)
                wait(ve, xn_made, x, back=1)
                inverse_deviation(ve, x, ST2, RS2, rs2_made)

            def landmarks(x):
                wait(ve, k_made, x)
                wait(ve, ready["cq"], x, back=1)
                wait(ve, ls_made, x, back=1)
                for i in range(CH):
                    ve.scalar_tensor_tensor(
                        out=LL[:, i, :].rearrange("p (h k) -> p h k", h=hpc),
                        in0=KT[:, i // CPO, T:TL].unsqueeze(1).broadcast_to([P, hpc, slots]), scalar=-2.0,
                        in1=t.bd[:, i % CPO, :].rearrange("p (h k) -> p h k", h=hpc),
                        op0=ALU.mult, op1=ALU.mult).then_inc(ll_made.sem, 1)

            def take_v(x):
                for i in range(NT):
                    wait(ve, ready["v"], x, i)
                    wait(ve, ready["z"], x, back=2)
                    ve.tensor_tensor(VA[:, x.par, i, :, 0:DA],
                                     ring.bank("v", i)[:, 0:M].rearrange("p (h d) -> p h d", h=HA),
                                     bv[:, :].rearrange("p (h d) -> p h d", h=HA), ALU.add).then_inc(free["v"].sem, 1)

            def clamp(x):
                wait(ve, free["ln"], x)
                for n in range(2 * CH):
                    stage, i = ("ck", "cq")[n // CH], n % CH
                    wait(ve, ready[stage], x, i)
                    if n < 2:
                        wait(ve, pq_made, x, CH - 2 + n, back=1)
                    elif n - 2 < CH:
                        wait(ve, pk_made, x, n - 2)
                    else:
                        wait(ve, pq_made, x, n - 2 - CH)
                    width = (TL, T)[n // CH]
                    ve.tensor_scalar(CK[:, n % 2, 0:width], ring.bank(stage, i)[:, 0:width], LN[:, i:i + 1], 0.0,
                                     ALU.add, ALU.max).then_inc(free[stage].sem, 1)

            def take_turned(x):
                for i in range(NT * TB):
                    wait(ve, ready["t"], x, i)
                    wait(ve, ready["z"], x, back=1)
                    ve.tensor_copy(PN[:, i // TB, i % TB * TW:(i % TB + 1) * TW], ring.bank("t", i)[:, 0:TW])\
                        .then_inc(free["t"].sem, 1)

            def right_sides(x):
                for i in range(ZB):
                    wait(ve, ready["z"], x, i)
                    if i:
                        wait(ve, zr_made, x, i - 1)
                    else:
                        wait(ve, zr_made, x, back=1)
                    ve.tensor_tensor(ZM[:, :, :, :],
                                     ring.bank("z", i)[:, 0:CZ * hpc * R].rearrange("p (c h r) -> p c h r", c=CZ, h=hpc),
                                     t.bz[:, :, :].unsqueeze(1).broadcast_to([P, CZ, hpc, R]), ALU.mult)\
                        .then_inc(free["z"].sem, 1)
                    wait(ve, free["z"], x, i)
                    wait_dma(ve, z_stored, x, back=2)
                    own = Z[:, x.par, i * CZ:(i + 1) * CZ, :]
                    ve.tensor_reduce(own, ZM[:, :, :, :].rearrange("p c h r -> p c r h"), AX_X, ALU.add)\
                        .then_inc(zr_made.sem, 1)
                    wait(ve, zr_made, x, i)
                    ve.tensor_scalar(own, own, t.reg[:, 1:2], None, ALU.mult).then_inc(z_made.sem, 1)

            pipeline(ve, [(0, v_exp_k), (2, take_turned), (0, y), (2, right_sides), (1, landmarks), (0, stats1),
                          (1, take_v), (1, clamp), (0, stats2)])


def solve_phase(nc, t, slots, spill):
    GB = N * HA // P if slots == SMALL else 1
    TURNS = N * HA // P // GB
    rows = slots + R
    sfx = f"_{slots}"
    with ExitStack() as ctx, nc.Block() as block:
        def sb(name, shape, dt=F32):
            return ctx.enter_context(nc.sbuf_tensor("s_" + name + sfx, shape, dt))

        def sem(name):
            return t.semaphore("s_" + name)

        A = sb("a", [P, GB, rows, slots])
        ZL = sb("zl", [P, GB, slots, R])
        YO = sb("yo", [P, GB, slots, R])
        DI = sb("di", [P, GB, slots])
        ROW = sb("row", [P, GB, slots])
        PR = sb("pr", [P, GB, rows, slots]) if slots == SMALL else \
            sb("pr", [P, GB, (rows + 1) * (rows + 1) // 4])
        RD = sb("rd", [P, GB, rows])
        loaded = sem("loaded")
        moved = sem("moved")
        stored = sem("stored")
        link_sem = sem("step")
        idle(block, "tensor", "scalar", "gpsimd")
        STEPS = 9 * slots - 6
        w_sys = spill.w.rearrange("(g p k) j -> p g (k j)", p=P, k=slots)
        z_sys = spill.z.rearrange("(g p k) r -> p g (k r)", p=P, k=slots)
        y_sys = spill.y.rearrange("(g p k) r -> p g (k r)", p=P, k=slots)

        @block.sync
        def _(sy):
            def batch(turn, first=False):
                if not first:
                    sy.wait_ge(stored, turn * 16)
                    sy.wait_ge(moved, turn)
                sy.dma_start(A[:, :, 0:slots, :].rearrange("p g k j -> p g (k j)"),
                             w_sys[:, bass.ds(turn * GB, GB), :]).then_inc(loaded, 16)
                sy.dma_start(ZL[:, :, :, :].rearrange("p g k r -> p g (k r)"),
                             z_sys[:, bass.ds(turn * GB, GB), :]).then_inc(loaded, 16)
                sy.wait_ge(moved, turn + 1)
                sy.dma_start(y_sys[:, bass.ds(turn * GB, GB), :],
                             YO[:, :, :, :].rearrange("p g k r -> p g (k r)")).then_inc(stored, 16)

            batch(0, first=True)
            if TURNS > 1:
                with sy.Fori(1, TURNS) as turn:
                    batch(turn)
            sy.wait_ge(stored, TURNS * 16)

        @block.vector
        def _(ve):
            def batch(turn):
                n = [0]

                def link(instruction):
                    n[0] += 1
                    instruction.then_inc(link_sem, 1)
                    ve.wait_ge(link_sem, turn * STEPS + n[0])

                ve.wait_ge(loaded, turn * 32 + 32)
                link(ve.tensor_copy(A[:, :, slots:rows, :], ZL[:, :, :, :].rearrange("p g k r -> p g r k")))
                for j in range(slots):
                    if j:
                        link(ve.tensor_tensor(ROW[:, :, 0:j], A[:, :, j, 0:j], DI[:, :, 0:j], ALU.mult))
                        m = rows - j
                        if slots == SMALL:
                            pr = PR[:, :, 0:m, 0:j]
                        else:
                            pr = PR[:, :, 0:m * j].rearrange("p g (m j) -> p g m j", j=j)
                        link(ve.tensor_tensor(pr, A[:, :, j:rows, 0:j],
                                              ROW[:, :, 0:j].unsqueeze(2).broadcast_to([P, GB, m, j]), ALU.mult))
                        link(ve.tensor_reduce(RD[:, :, 0:m], pr, AX_X, ALU.add))
                        link(ve.tensor_tensor(A[:, :, j:rows, j], A[:, :, j:rows, j], RD[:, :, 0:m], ALU.subtract))
                    link(ve.reciprocal(DI[:, :, j:j + 1], A[:, :, j, j:j + 1]))
                for i in reversed(range(slots)):
                    z = A[:, :, slots:rows, i]
                    m = slots - 1 - i
                    if m:
                        pr = PR[:, :, 0:R, 0:m] if slots == SMALL else \
                            PR[:, :, 0:R * m].rearrange("p g (c m) -> p g c m", m=m)
                        link(ve.tensor_tensor(pr, A[:, :, slots:rows, i + 1:slots],
                                              A[:, :, i + 1:slots, i].unsqueeze(2).broadcast_to([P, GB, R, m]),
                                              ALU.mult))
                        link(ve.tensor_reduce(RD[:, :, 0:R], pr, AX_X, ALU.add))
                        link(ve.tensor_tensor(z, z, RD[:, :, 0:R], ALU.subtract))
                    link(ve.tensor_tensor(z, z, DI[:, :, i:i + 1].broadcast_to([P, GB, R]), ALU.mult))
                n[0] += 1
                ve.tensor_copy(YO[:, :, :, :], A[:, :, slots:rows, :].rearrange("p g r k -> p g k r"))\
                    .then_inc(moved, 1)
                return n[0]

            if TURNS == 1:
                steps = batch(0)
            else:
                with ve.Fori(0, TURNS) as turn:
                    steps = batch(turn)
            assert steps == STEPS + 1, (steps, STEPS)


def output_phase(nc, ins, out, t, slots, spill):
    hpc = P // slots
    CH = HA // hpc
    sfx = f"_{slots}"
    with ExitStack() as ctx, nc.Block() as block:
        def sb(name, shape, dt=F32):
            return ctx.enter_context(nc.sbuf_tensor("b_" + name + sfx, shape, dt))

        def sem(name):
            return t.semaphore("b_" + name)

        wo = sb("wo", [P, 2, M])
        bo = sb("bo", [P, M])
        w1 = sb("w1", [P, 2, F])
        r1 = sb("r1", [P, 2, GATED])
        b1 = sb("b1", [ER + 1, F])
        w2 = sb("w2", [P, FC, M + GATED])
        b2 = sb("b2", [ER + 1, M])
        PQ = sb("pq", [P, 2, CH, T])
        YL = sb("yl", [P, 2, CH, R])
        YY = sb("yy", [P, 2, CH, hpc, R])
        NM = sb("nm", [P, NT, HA])
        NR = sb("nr", [P, NT, HA])
        O = sb("o", [P, NT, M])
        OT = sb("ot", [P, 2, T])
        H = sb("h", [P, 2, NT, M])
        H2 = sb("h2", [P, 2, NT, M])
        ST, RS = sb("st", [P, NT, 6]), sb("rs", [P, 6, NT])
        XN = sb("xn", [P, NT, M])
        XT = sb("xt", [P, 2, 2, T])
        HID = sb("hid", [P, 2, FC, T])
        gate_buffers = [{n: sb(f"{n}{i}", shape) for n, shape in
                         (("mx", [P, NT]), ("d", [P, NT, E]), ("e", [P, NT, E]), ("sum", [P, NT]),
                          ("rec", [P, NT]), ("gate", [P, NT, E]), ("zg", [P, NT, ER + 1]))} for i in range(2)]
        ZT = [sb(f"zt{i}", [ER + 1, T]) for i in range(2)]
        OUT = sb("out", [P, 2, NT, M])

        order = [("o", 0, 0), ("g2", 0, 2), ("o", 1, 0), ("o", 2, 0), ("even", 0, 1), ("odd", 0, 1),
                 ("ot", 0, 0), ("ot", 1, 0), ("even", 1, 1), ("odd", 1, 1), ("w", 0, 0), ("w", 1, 0), ("w", 2, 0),
                 ("even", 2, 1), ("odd", 2, 1), ("even", 3, 1), ("xt", 0, 0), ("xt", 1, 0), ("odd", 3, 1),
                 ("r", 0, 0), ("y", 0, 1), ("y", 1, 1), ("y", 2, 1), ("g1", 0, 0)]
        per = {stage: sum(1 for job in order if job[0] == stage) for stage, _, _ in order}
        ready = {s: Signal(sem("ready_" + s), n) for s, n in per.items()}
        free = {s: Signal(sem("free_" + s), n) for s, n in per.items()}
        ring = Ring(order, free, t.banks)
        weights = sem("weights")
        ones_set = sem("ones_set")
        pq_loaded = [sem(f"pq_loaded{i}") for i in range(2)]
        y_loaded = [sem(f"y_loaded{i}") for i in range(2)]
        h_loaded = [sem(f"h_loaded{i}") for i in range(2)]
        out_stored = [sem(f"out_stored{i}") for i in range(2)]
        yy_made = Signal(sem("yy_made"), 1)
        hb_made = Signal(sem("hb_made"), 1)
        norm_made = Signal(sem("norm_made"), 2 * NT)
        stat = Signal(sem("stat"), NT)
        rs_made = Signal(sem("rs_made"), RSQRT_STEPS)
        xn_made = Signal(sem("xn_made"), NT)
        lora_added = Signal(sem("lora_added"), NT)
        logits = [Signal(sem("logits0"), 2), Signal(sem("logits1"), 2 * NT)]
        exps = [Signal(sem(f"exps{i}"), 1) for i in range(2)]
        gates = [Signal(sem(f"gates{i}"), 3) for i in range(2)]
        gated = [free["r"], Signal(sem("gated1"), NT)]
        loads = [(wo[:, :, :], ins["wo"]), (bo[:, :], ins["bo"].broadcast_to([P, M])), (w1[:, :, :], ins["w1"]),
                 (r1[:, :, :], ins["r1"]), (b1[:, :], ins["b1"]), (w2[:, :, :], ins["w2"]), (b2[:, :], ins["b2"])]

        @block.sync
        def _(sy):
            for dst, src in loads:
                sy.dma_start(dst, src).then_inc(weights, 16)

            def load(x):
                wait(sy, ready["o"], x, back=2)
                sy.dma_start(PQ[:, x.par, :, :].rearrange("p c m -> p (c m)"),
                             spill.pq[bass.ds(x.s, 1)].rearrange("n p k -> p (n k)")).then_inc(pq_loaded[x.par], 16)
                wait(sy, yy_made, x, back=2)
                sy.dma_start(YL[:, x.par, :, :],
                             spill.y[bass.ds(x.s * (HA * slots), HA * slots), :].rearrange("(q p) r -> p q r", p=P))\
                    .then_inc(y_loaded[x.par], 16)
                wait(sy, free["w"], x, back=2)
                sy.dma_start(H[:, x.par, :, :].rearrange("p c m -> p (c m)"),
                             spill.h[bass.ds(x.s, 1)].rearrange("n p k -> p (n k)")).then_inc(h_loaded[x.par], 16)

            def store(x):
                wait(sy, free["y"], x)
                sy.dma_start(out[bass.ds(x.s, 1)].rearrange("n (c p) m -> p (n c) m", p=P), OUT[:, x.par, :, :])\
                    .then_inc(out_stored[x.par], 16)

            pipeline(sy, [(0, load), (2, store)])
            for i in range(2):
                sy.wait_ge(out_stored[i], 16 * N // 2)

        @block.tensor
        def _(pe):
            def o(i):
                def step(x):
                    wait_dma(pe, pq_loaded, x)
                    wait(pe, yy_made, x)
                    ring.wait(pe, "o", i, x)
                    for c in range(CH):
                        mm = pe.matmul(ring.bank("o", i)[:, c * hpc * R:(c + 1) * hpc * R],
                                       PQ[:, x.par, c, i * P:(i + 1) * P],
                                       YY[:, x.par, c, :, :].rearrange("p h r -> p (h r)"), start=True, stop=True,
                                       skip_group_check=True)
                    mm.then_inc(ready["o"].sem, 1)
                return step

            def turn(stage, i, src, made):
                def step(x):
                    wait(pe, made, x)
                    ring.wait(pe, stage, i, x)
                    for c in range(NT):
                        mm = pe.transpose(ring.bank(stage, i)[:, c * P:(c + 1) * P], src[:, c, i * P:(i + 1) * P],
                                          t.ident[:, :])
                    mm.then_inc(ready[stage].sem, 1)
                return step

            def w(i):
                def step(x):
                    wait(pe, free["ot"], x)
                    ring.wait(pe, "w", i, x, ("ot",))
                    for kc in range(2):
                        mm = pe.matmul(ring.bank("w", i)[:, 0:M], OT[:, kc, i * P:(i + 1) * P], wo[:, kc, :],
                                       start=(kc == 0), stop=(kc == 1))
                    mm.then_inc(ready["w"].sem, 1)
                return step

            def r(i):
                def step(x):
                    wait(pe, free["xt"], x)
                    ring.wait(pe, "r", i, x, ("xt",))
                    for c in range(NT):
                        for kc in range(2):
                            mm = pe.matmul(ring.bank("r")[:, c * GATED:(c + 1) * GATED],
                                           XT[:, x.par, kc, c * P:(c + 1) * P], r1[:, kc, :],
                                           start=(kc == 0), stop=(kc == 1), skip_group_check=True)
                    mm.then_inc(ready["r"].sem, 1)
                return step

            def g(n):
                stage = ("g1", "g2")[n]

                def step(x):
                    wait(pe, gated[n], x)
                    ring.wait(pe, stage, 0, x)
                    for c in range(NT):
                        mm = pe.transpose(ring.bank(stage)[0:ER + 1, c * P:(c + 1) * P],
                                          gate_buffers[n]["zg"][:, c, :], t.ident[:, :])
                    mm.then_inc(ready[stage].sem, 1)
                return step

            def hid(stage, i):
                f = 2 * i + (stage == "odd")

                def step(x):
                    wait(pe, free["xt"], x)
                    ring.wait(pe, stage, i, x, ("xt",))
                    o = ring.bank(stage, i)[:, 0:T]
                    for kc in range(2):
                        pe.matmul(o, w1[:, kc, f * P:(f + 1) * P], XT[:, x.par, kc, :], start=(kc == 0), stop=False)
                    wait(pe, free["g1"], x)
                    pe.matmul(o, b1[:, f * P:(f + 1) * P], ZT[0][:, :], start=False, stop=True)\
                        .then_inc(ready[stage].sem, 1)
                return step

            def y(i):
                def step(x):
                    wait(pe, free["even"], x)
                    wait(pe, free["odd"], x)
                    ring.wait(pe, "y", i, x, ("odd", "even",))
                    for f in range(FC):
                        mm = pe.matmul(ring.bank("y", i)[:, 0:M + GATED], HID[:, x.par, f, i * P:(i + 1) * P],
                                       w2[:, f, :], start=(f == 0), stop=(f == FC - 1))
                    mm.then_inc(ready["y"].sem, 1)
                return step

            def lora(x):
                wait(pe, free["g2"], x)
                for i in range(NT):
                    pe.matmul(ring.bank("y", i)[:, 0:M], ZT[1][:, i * P:(i + 1) * P], b2[:, :], start=False,
                              stop=True, skip_group_check=True).then_inc(lora_added.sem, 1)

            step_of = {"o": o, "ot": lambda i: turn("ot", i, O, free["o"]), "w": w,
                       "xt": lambda i: turn("xt", i, XN, xn_made), "r": r, "y": y,
                       "g1": lambda i: g(0), "g2": lambda i: g(1),
                       "even": lambda i: hid("even", i), "odd": lambda i: hid("odd", i)}
            stages = [(skew, step_of[stage](i)) for stage, i, skew in order]
            stages.insert(4, (2, lora))
            pe.wait_ge(weights, 16 * len(loads))
            pipeline(pe, stages)

        @block.scalar
        def _(act):
            act.wait_ge(weights, 16 * len(loads))

            def take_g(n):
                def step(x):
                    stage = ("g1", "g2")[n]
                    wait(act, ready[stage], x)
                    wait(act, (ready["odd"], lora_added)[n], x, back=1)
                    act.activation(ZT[n][:, :], ring.bank(stage)[0:ER + 1, 0:T], ACT.Copy).then_inc(free[stage].sem, 1)
                return step

            def take_ot(x):
                for i in range(2):
                    wait(act, ready["ot"], x, i)
                    wait(act, ready["w"], x, back=1)
                    act.activation(OT[:, i, :], ring.bank("ot", i)[:, 0:T], ACT.Copy).then_inc(free["ot"].sem, 1)

            def take_xt(x):
                for i in range(2):
                    wait(act, ready["xt"], x, i)
                    wait(act, ready["odd"], x, back=2)
                    act.activation(XT[:, x.par, i, :], ring.bank("xt", i)[:, 0:T], ACT.Copy).then_inc(free["xt"].sem, 1)

            def relu(i):
                def step(x):
                    wait(act, ready["even"], x, i)
                    wait(act, ready["y"], x, back=2)
                    act.activation(HID[:, x.par, 2 * i, :], ring.bank("even", i)[:, 0:T], ACT.Relu)\
                        .then_inc(free["even"].sem, 1)
                return step

            def norm(x):
                wait(act, rs_made, x)
                wait(act, ready["xt"], x, back=1)
                for i in range(NT):
                    act.activation(XN[:, i, :], H2[:, x.par, i, :], ACT.Identity, bias=RS[:, 1, i:i + 1],
                                   scale=RS[:, 0, i:i + 1]).then_inc(xn_made.sem, 1)

            def exp(n):
                def step(x):
                    b = gate_buffers[n]
                    wait(act, logits[n], x)
                    wait(act, gates[n], x, 2, back=1)
                    act.activation(b["e"][:, :, :], b["d"][:, :, :], ACT.Exp).then_inc(exps[n].sem, 1)
                return step

            pipeline(act, [(2, take_g(1)), (1, relu(0)), (0, take_ot), (1, relu(1)), (1, relu(2)), (0, norm),
                           (1, relu(3)), (0, take_xt), (0, exp(0)), (1, exp(1)), (0, take_g(0))])

        @block.gpsimd
        def _(po):
            for n in range(2):
                po.memset(gate_buffers[n]["zg"][:, :, ER:ER + 1], 1.0).then_inc(ones_set, 1)
            po.wait_ge(weights, 16 * len(loads))

            def spread(x):
                wait_dma(po, y_loaded, x)
                wait(po, ready["o"], x, back=2)
                po.tensor_tensor(YY[:, x.par, :, :, :], YL[:, x.par, :, :].unsqueeze(2).broadcast_to([P, CH, hpc, R]),
                                 t.bz[:, :, :].unsqueeze(1).broadcast_to([P, CH, hpc, R]), ALU.mult)\
                    .then_inc(yy_made.sem, 1)

            def add_bias(x):
                wait_dma(po, h_loaded, x)
                po.tensor_tensor(H[:, x.par, :, :], H[:, x.par, :, :], bo[:, :].unsqueeze(1).broadcast_to([P, NT, M]),
                                 ALU.add).then_inc(hb_made.sem, 1)

            pipeline(po, [(0, spread), (0, add_bias)])

        @block.vector
        def _(ve):
            ve.wait_ge(weights, 16 * len(loads))
            ve.wait_ge(ones_set, 2)

            def divide(i):
                def step(x):
                    wait(ve, ready["o"], x, i)
                    b = ring.bank("o", i)[:, 0:HA * R].rearrange("p (h r) -> p h r", h=HA)
                    ve.tensor_scalar(NM[:, i, :], b[:, :, DA], 1e-10, None, ALU.max).then_inc(norm_made.sem, 1)
                    wait(ve, norm_made, x, 2 * i)
                    ve.reciprocal(NR[:, i, :], NM[:, i, :]).then_inc(norm_made.sem, 1)
                    wait(ve, norm_made, x, 2 * i + 1)
                    wait(ve, ready["ot"], x, back=1)
                    ve.tensor_tensor(O[:, i, :].rearrange("p (h d) -> p h d", h=HA), b[:, :, 0:DA],
                                     NR[:, i, :].unsqueeze(2).broadcast_to([P, HA, DA]), ALU.mult)\
                        .then_inc(free["o"].sem, 1)
                return step

            def finish(x):
                for i in range(NT):
                    wait(ve, lora_added, x, i)
                    wait_dma(ve, out_stored, x, back=2)
                    ve.tensor_tensor(OUT[:, x.par, i, :], H2[:, x.par, i, :], ring.bank("y", i)[:, 0:M], ALU.add)\
                        .then_inc(free["y"].sem, 1)

            def relu(i):
                def step(x):
                    wait(ve, ready["odd"], x, i)
                    wait(ve, ready["y"], x, back=2)
                    ve.tensor_scalar(HID[:, x.par, 2 * i + 1, :], ring.bank("odd", i)[:, 0:T], 0.0, None, ALU.max)\
                        .then_inc(free["odd"].sem, 1)
                return step

            def residual(x):
                wait(ve, hb_made, x)
                wait(ve, free["y"], x, back=2)
                for i in range(NT):
                    wait(ve, ready["w"], x, i)
                    ve.tensor_tensor(H2[:, x.par, i, :], H[:, x.par, i, :], ring.bank("w", i)[:, 0:M], ALU.add)\
                        .then_inc(free["w"].sem, 1)
                for i in range(NT):
                    wait(ve, free["w"], x, i)
                    ve.bn_stats(ST[:, i, :], H2[:, x.par, i, :]).then_inc(stat.sem, 1)
                wait(ve, stat, x)
                wait(ve, xn_made, x, back=1)
                inverse_deviation(ve, x, ST, RS, rs_made)

            def shift(n):
                def step(x):
                    b = gate_buffers[n]
                    wait(ve, exps[n], x, back=1)
                    if n == 0:
                        wait(ve, ready["r"], x)
                        p = ring.bank("r")[:, 0:NT * GATED].rearrange("p (c g) -> p c g", c=NT)[:, :, ER:GATED]
                        ve.tensor_reduce(b["mx"][:, :], p, AX_X, ALU.max).then_inc(logits[n].sem, 1)
                        wait(ve, logits[n], x, 0)
                        ve.tensor_tensor(b["d"][:, :, :], p, b["mx"][:, :].unsqueeze(2).broadcast_to([P, NT, E]),
                                         ALU.subtract).then_inc(logits[n].sem, 1)
                        return
                    for i in range(NT):
                        wait(ve, ready["y"], x, i)
                        p = ring.bank("y", i)[:, M + ER:M + GATED]
                        ve.tensor_reduce(b["mx"][:, i:i + 1], p, AX_X, ALU.max).then_inc(logits[n].sem, 1)
                        wait(ve, logits[n], x, 2 * i)
                        ve.tensor_scalar(b["d"][:, i, :], p, b["mx"][:, i:i + 1], None, ALU.subtract)\
                            .then_inc(logits[n].sem, 1)
                return step

            def gate(n):
                def step(x):
                    b = gate_buffers[n]
                    wait(ve, exps[n], x)
                    ve.tensor_reduce(b["sum"][:, :], b["e"][:, :, :], AX_X, ALU.add).then_inc(gates[n].sem, 1)
                    wait(ve, gates[n], x, 0)
                    ve.reciprocal(b["rec"][:, :], b["sum"][:, :]).then_inc(gates[n].sem, 1)
                    wait(ve, gates[n], x, 1)
                    ve.scalar_tensor_tensor(out=b["gate"][:, :, :], in0=b["e"][:, :, :], scalar=1.0 / RK,
                                            in1=b["rec"][:, :].unsqueeze(2).broadcast_to([P, NT, E]),
                                            op0=ALU.mult, op1=ALU.mult).then_inc(gates[n].sem, 1)
                    wait(ve, gates[n], x, 2)
                    wait(ve, ready[("g1", "g2")[n]], x, back=1)
                    if n == 0:
                        p = ring.bank("r")[:, 0:NT * GATED].rearrange("p (c g) -> p c g", c=NT)[:, :, 0:ER]
                        zg = ve.tensor_tensor(b["zg"][:, :, 0:ER].rearrange("p c (e r) -> p c e r", e=E),
                                              p.rearrange("p c (e r) -> p c e r", e=E),
                                              b["gate"][:, :, :].unsqueeze(3).broadcast_to([P, NT, E, RK]), ALU.mult)
                        zg.then_inc(free["r"].sem, 1)
                        return
                    for i in range(NT):
                        zg = ve.tensor_tensor(b["zg"][:, i, 0:ER].rearrange("p (e r) -> p e r", e=E),
                                              ring.bank("y", i)[:, M:M + ER].rearrange("p (e r) -> p e r", e=E),
                                              b["gate"][:, i, :].unsqueeze(2).broadcast_to([P, E, RK]), ALU.mult)
                        zg.then_inc(gated[n].sem, 1)
                return step

            pipeline(ve, [(0, divide(0)), (0, divide(1)), (0, divide(2)), (2, finish), (1, relu(0)), (1, relu(1)),
                          (0, residual), (1, relu(2)), (1, relu(3)), (0, shift(0)), (0, gate(0)),
                          (1, shift(1)), (1, gate(1))])


class Tables:

    def __init__(self, banks, semaphore):
        self.banks, self.semaphore = banks, semaphore


class Spill:
    pass


def computation(nc, ins, out, banks, semaphore, slots):
    hpc = P // slots
    CH = HA // hpc
    with ExitStack() as ctx:
        def sb(name, shape):
            return ctx.enter_context(nc.sbuf_tensor(f"{name}_{slots}", shape, F32))

        t, spill = Tables(banks, semaphore), Spill()
        t.ident = sb("ident", [P, P])
        t.bd = sb("bd", [P, CH // 2, P])
        t.bz = sb("bz", [P, hpc, R])
        t.diag = sb("diag", [P, slots])
        t.gather = sb("gather", [P, NT, slots])
        t.reg = sb("reg", [P, 4])
        t.regd = sb("regd", [P, slots])
        t.rate = sb("rate", [P, 2])
        t.ones = sb("ones", [P, 1])
        spill.h = nc.dram_tensor(f"h_spill_{slots}", (N, P, NT * M), F32, kind="Internal").ap()
        spill.pq = nc.dram_tensor(f"pq_spill_{slots}", (N, P, CH * T), F32, kind="Internal").ap()
        spill.w = nc.dram_tensor(f"w_spill_{slots}", (N * HA * slots, slots), F32, kind="Internal").ap()
        spill.z = nc.dram_tensor(f"z_spill_{slots}", (N * HA * slots, R), F32, kind="Internal").ap()
        spill.y = nc.dram_tensor(f"y_spill_{slots}", (N * HA * slots, R), F32, kind="Internal").ap()
        landmark_tables(nc, ins, slots, t)
        systems_phase(nc, ins, t, slots, spill)
        solve_phase(nc, t, slots, spill)
        output_phase(nc, ins, out, t, slots, spill)


def build(nc, ins, out):
    with ExitStack() as ctx:
        banks = [ctx.enter_context(nc.psum_tensor(f"bank{i}", [P, 512], F32)) for i in range(NB)]
        number = ctx.enter_context(nc.sbuf_tensor("number", [1, 1], I32))
        count_tokens(nc, ins, number)
        semaphores = {}

        def semaphore(name):
            if name not in semaphores:
                semaphores[name] = ctx.enter_context(nc.semaphore(name))
            return semaphores[name]

        tokens = nc.values_load(number[0:1, 0:1], min_val=1, max_val=NL)
        with nc.If(tokens <= SMALL):
            computation(nc, ins, out, banks, semaphore, SMALL)
        with nc.Else():
            computation(nc, ins, out, banks, semaphore, NL)


def kernel(x, txt, L0_tok_Wq_w, L0_tok_Wq_b, L0_tok_Wk_w, L0_tok_Wk_b, L0_tok_Wv_w, L0_tok_Wv_b, L0_tok_w_bias,
           L0_tok_out_w, L0_tok_out_b, L0_tok_ln_g, L0_tok_ln_b, L0_tok_local_mask, L0_attn_Wq, L0_attn_bq,
           L0_attn_Wk, L0_attn_bk, L0_attn_Wv, L0_attn_bv, L0_attn_Wo, L0_attn_bo, L0_attn_temperature,
           L0_attn_landmark_idx, L0_ffn_W1, L0_ffn_b1, L0_ffn_A1, L0_ffn_B1, L0_ffn_R1, L0_ffn_W2, L0_ffn_b2,
           L0_ffn_A2, L0_ffn_B2, L0_ffn_R2):
    import concourse.bacc as _bacc
    from concourse.bass_utils import run_bass_kernel_spmd as _run

    a = np.asarray

    def rows(w):
        w = a(w)
        return w.reshape(w.shape[0] // P, P, w.shape[1]).transpose(1, 0, 2)

    def experts(w):
        w = a(w)
        return w.transpose(1, 0, 2).reshape(w.shape[1], -1)

    one = np.ones((1, L * HT), np.float32)
    eye = np.eye(C, dtype=np.float32)
    low = np.tril(np.ones((NL, NL), np.float32), -1)
    arrays = {
        "x": a(x).reshape(N, C, L * HT),
        "txt": a(txt),
        "wkv": np.concatenate([np.concatenate([a(L0_tok_Wk_w).T, a(L0_tok_Wv_w).T], 1),
                               np.concatenate([a(L0_tok_Wk_b), a(L0_tok_Wv_b)])[None]], 0),
        "wq_tok": np.concatenate([a(L0_tok_Wq_w).T, a(L0_tok_Wq_b)[None]], 0),
        "res": np.concatenate([np.repeat(eye[:, None], HT, 1), a(L0_tok_out_b).reshape(1, HT, C)], 0),
        "ow": rows(L0_tok_out_w),
        "w_bias": rows(a(L0_tok_w_bias).T),
        "mask": rows(a(L0_tok_local_mask).T).copy().view(np.int32),
        "ln_g": a(L0_tok_ln_g)[None], "ln_b": a(L0_tok_ln_b)[None], "one_row": one,
        "wa_q": rows(a(L0_attn_Wq).T), "wa_k": rows(a(L0_attn_Wk).T), "wa_v": rows(a(L0_attn_Wv).T),
        "bq": a(L0_attn_bq).reshape(2, P).T, "bk": a(L0_attn_bk).reshape(2, P).T, "bv": a(L0_attn_bv)[None],
        "wo": rows(a(L0_attn_Wo).T), "bo": a(L0_attn_bo)[None],
        "temperature": a(L0_attn_temperature).reshape(1, 1), "idx": a(L0_attn_landmark_idx).reshape(1, NL),
        "w1": rows(L0_ffn_W1), "r1": rows(np.concatenate([experts(L0_ffn_A1), a(L0_ffn_R1)], 1)),
        "b1": np.concatenate([a(L0_ffn_B1).reshape(ER, F), a(L0_ffn_b1)[None]], 0),
        "w2": rows(np.concatenate([a(L0_ffn_W2), experts(L0_ffn_A2), a(L0_ffn_R2)], 1)),
        "b2": np.concatenate([a(L0_ffn_B2).reshape(ER, M), a(L0_ffn_b2)[None]], 0),
        "ident": np.eye(P, dtype=np.float32), "tri": np.stack([low, low.T], 1),
        "iota": np.arange(T, dtype=np.float32)[None], "lower": low.reshape(1, NL * NL),
    }
    for slots in (SMALL, NL):
        arrays[f"bd{slots}"], arrays[f"bz{slots}"], arrays[f"diag{slots}"] = constants(slots)
    nc = _bacc.Bacc("TRN2", target_bir_lowering=False, num_devices=1)
    ins = {}
    feeds = {}
    for name, array in arrays.items():
        array = np.ascontiguousarray(array)
        feeds[f"in_{name}"] = array
        ins[name] = nc.dram_tensor(f"in_{name}", array.shape, mybir.dt.from_np(array.dtype), kind="ExternalInput").ap()
    out = nc.dram_tensor("out", (N, T, M), F32, kind="ExternalOutput").ap()
    build(nc, ins, out)
    return _run(nc, [feeds], core_ids=[0]).results[0]["out"]
```

```python
from contextlib import ExitStack

import concourse.bass as bass
import numpy as np
from concourse import mybir

ALU = mybir.AluOpType
ACT = mybir.ActivationFunctionType
F32 = mybir.dt.float32
I32 = mybir.dt.int32
FR = mybir.dt.float32r
U8 = mybir.dt.uint8
AX_X = mybir.AxisListType.X

P = 128
N = 32
C, L, HT = 64, 256, 4
M = C * HT
NT = 3
T = NT * P
HA, DA = 16, 16
NL = 64
R = DA + 1
F = 1024
FC = F // P
E, RK = 3, 8
ER = E * RK
GATED = ER + E
GE = GATED + GATED % 2
G3 = 32
NB = 8
SMALL = 16
EPS = 1e-5
REG = 1e-6


def constants(slots):
    hpc = P // slots
    chunks = HA // hpc
    p = np.arange(P)
    col = np.arange(P)
    bd = np.zeros((P, chunks // 2, P), np.float32)
    for q in range(chunks // 2):
        bd[:, q, :] = (p[:, None] // DA) == (q * hpc + col[None, :] // slots)
    bz = np.repeat((p[:, None] // slots) == np.arange(hpc)[None, :], R, axis=1).astype(np.float32)
    rd = (p[:, None] % slots == np.arange(slots)[None, :]).astype(np.float32)
    return bd, bz, rd


class Sample:

    def __init__(self, s, pair, par):
        self.s, self.pair, self.par = s, pair, par


class Signal:

    def __init__(self, sem, per=1):
        self.sem, self.per = sem, per


def wait(eng, signal, x, i=None, back=0):
    count = (x.s - back) * signal.per + (signal.per if i is None else i + 1)
    if isinstance(count, int) and count <= 0:
        return
    eng.wait_ge(signal.sem, count)


def wait_dma(eng, sems, x, back=0):
    count = (x.pair + 1 - back // 2) * 16
    if isinstance(count, int) and count <= 0:
        return
    eng.wait_ge(sems[x.par], count)


def idle(block, *engines):
    for name in engines:
        {"tensor": block.tensor, "scalar": block.scalar, "gpsimd": block.gpsimd}[name](lambda eng: None)


def pipeline(eng, stages, peel=4):

    def turn(t, pair, u):
        for skew, step in stages:
            if isinstance(t, int) and not 0 <= t - skew < N:
                continue
            step(Sample(t - skew, pair + (u - skew) // 2, (u - skew) % 2))

    for t in range(peel):
        turn(t, t // 2, t % 2)
    with eng.Fori(peel // 2, N // 2) as pair:
        for u in range(2):
            turn(pair * 2 + u, pair, u)
    for t in range(N, N + peel - 2):
        turn(t, t // 2, t % 2)


class Ring:

    def __init__(self, order, free, banks, own={}, shared=range(NB)):
        self.order, self.free = order, free
        rest = [job[:2] for job in order if job[0] not in own]
        place = {job: shared[n % len(shared)] for n, job in enumerate(rest)}
        place |= {(stage, i): n for stage, kept in own.items() for i, n in enumerate(kept)}
        self.place = [place[job[:2]] for job in order]
        self.of = {job: banks[n] for job, n in place.items()}

    def bank(self, stage, i=0):
        return self.of[stage, i]

    def wait(self, eng, stage, i, x, waited=()):
        at = next(n for n, job in enumerate(self.order) if job[:2] == (stage, i))
        own = self.order[at][2]
        turn, back, n = x.s + own, 0, at
        while True:
            n -= 1
            if n < 0:
                n += len(self.order)
                back += 1
            if self.place[n] != self.place[at]:
                continue
            before, j, skew = self.order[n]
            s = turn - back - skew
            if isinstance(s, int) and s >= N:
                continue
            if before in waited and own - back - skew <= 0:
                return
            wait(eng, self.free[before], Sample(s, None, None), j)
            return


def landmark_tables(nc, ins, slots, t):
    hpc = P // slots
    with ExitStack() as ctx, nc.Block() as block:
        def sb(name, shape, dt=F32):
            return ctx.enter_context(nc.sbuf_tensor(f"{name}_{slots}", shape, dt))

        idx_row = sb("idx_row", [P, NL], I32)
        idx_col = sb("idx_col", [NL, 1], I32)
        row_f = sb("row_f", [P, NL])
        col_f = sb("col_f", [NL, 1])
        neg_r = sb("neg_r", [P, NL])
        neg_c = sb("neg_c", [NL, 1])
        tri = sb("tri", [NL, 2, NL])
        iota = sb("iota", [NL, T])
        same = sb("same", [NL, 2, NL])
        count = sb("count", [NL, 2])
        first = sb("first", [NL, 1])
        rank = sb("rank", [NL, 1])
        pick = sb("pick", [NL, NL])
        spread = sb("spread", [NL, hpc, slots])
        hot = sb("hot", [NL, T])
        both = sb("both", [NL, 2])
        loaded = t.semaphore("tables_loaded")
        link_sem = t.semaphore("tables_step")
        product = t.semaphore("tables_product")
        loads = [(t.ident[:, :], ins["ident"]), (t.bd[:, :, :], ins[f"bd{slots}"]),
                 (t.bz[:, :, :].rearrange("p h r -> p (h r)"), ins[f"bz{slots}"]),
                 (t.diag[:, :], ins[f"diag{slots}"]), (t.rate[:, 0:1], ins["temperature"].broadcast_to([P, 1])),
                 (idx_row[:, :], ins["idx"].broadcast_to([P, NL])), (idx_col[:, :], ins["idx"].rearrange("a n -> n a")),
                 (tri[:, :, :], ins["tri"]), (iota[:, :], ins["iota"].broadcast_to([NL, T]))]
        idle(block, "scalar", "gpsimd")
        known = {}

        @block.sync
        def _(sy):
            for dst, src in loads:
                sy.dma_start(dst, src).then_inc(loaded, 16)

        @block.vector
        def _(ve):
            n = [0]

            def link(instruction):
                n[0] += 1
                instruction.then_inc(link_sem, 1)
                ve.wait_ge(link_sem, n[0])

            ve.wait_ge(loaded, 16 * len(loads))
            link(ve.memset(t.ones[:, :], 1.0))
            link(ve.memset(t.gather[:, :, :], 0.0))
            link(ve.reciprocal(t.rate[:, 1:2], t.rate[:, 0:1]))
            link(ve.tensor_scalar(t.rate[:, 0:1], t.rate[:, 1:2], -1.0, None, ALU.mult))
            for raw, f, neg in ((idx_row, row_f, neg_r), (idx_col, col_f, neg_c)):
                link(ve.tensor_copy(f[:, :], raw[:, :]))
                link(ve.tensor_scalar(neg[:, :], f[:, :], 0.0, float(T), ALU.is_lt, ALU.mult))
                link(ve.tensor_tensor(f[:, :], f[:, :], neg[:, :], ALU.add))
                link(ve.tensor_scalar(f[:, :], f[:, :], 0.0, float(T - 1), ALU.max, ALU.min))
            link(ve.tensor_scalar(same[:, 1, :], row_f[0:NL, :], col_f[:, 0:1], None, ALU.is_equal))
            link(ve.tensor_tensor(same[:, 0, :], same[:, 1, :], tri[:, 0, :], ALU.mult))
            link(ve.tensor_reduce(count[:, :], same[:, :, :], AX_X, ALU.add))
            link(ve.tensor_scalar(first[:, :], count[:, 0:1], 0.0, None, ALU.is_equal))
            known["first"] = n[0]
            ve.wait_ge(product, 1)
            link(ve.tensor_copy(rank[:, :], t.banks[0][0:NL, 0:1]))
            link(ve.tensor_scalar(pick[:, :], iota[:, 0:NL], rank[:, 0:1], first[:, 0:1], ALU.is_equal, ALU.mult))
            for h in range(hpc):
                link(ve.tensor_copy(spread[:, h, :], pick[:, 0:slots]))
            link(ve.tensor_scalar(hot[:, :], iota[:, :], col_f[:, 0:1], None, ALU.is_equal))
            link(ve.tensor_copy(both[:, 0:1], count[:, 1:2]))
            link(ve.memset(both[:, 1:2], 1.0))
            known["all"] = n[0]
            ve.wait_ge(product, 2)
            for c in range(NT):
                link(ve.tensor_copy(t.gather[:, c, 0:slots], t.banks[1][:, c * slots:(c + 1) * slots]))
            link(ve.tensor_copy(t.reg[:, 0:2], t.banks[2][:, 0:2]))
            link(ve.tensor_scalar(t.reg[:, 2:3], t.reg[:, 0:1], 1.0, None, ALU.max))
            link(ve.reciprocal(t.reg[:, 3:4], t.reg[:, 2:3]))
            link(ve.tensor_scalar(t.reg[:, 2:3], t.reg[:, 3:4], REG, t.reg[:, 1:2], ALU.mult, ALU.mult))
            link(ve.tensor_scalar(t.reg[:, 3:4], t.reg[:, 1:2], -1.0, 1.0, ALU.mult, ALU.add))
            link(ve.tensor_tensor(t.reg[:, 2:3], t.reg[:, 2:3], t.reg[:, 3:4], ALU.add))
            link(ve.tensor_scalar(t.regd[:, :], t.diag[:, :], t.reg[:, 2:3], None, ALU.mult))

        @block.tensor
        def _(pe):
            pe.wait_ge(link_sem, known["first"])
            pe.matmul(t.banks[0][0:NL, 0:1], tri[:, 1, :], first[:, :], start=True, stop=True).then_inc(product, 1)
            pe.wait_ge(link_sem, known["all"])
            pe.matmul(t.banks[2][:, 0:2], spread[:, :, :].rearrange("p h k -> p (h k)"), both[:, :],
                      start=True, stop=True)
            for c in range(NT):
                mm = pe.matmul(t.banks[1][:, c * slots:(c + 1) * slots], hot[:, c * P:(c + 1) * P],
                               pick[:, 0:slots], start=True, stop=True, skip_group_check=True)
            mm.then_inc(product, 1)


def count_tokens(nc, ins, number):
    with ExitStack() as ctx, nc.Block() as block:
        def sb(name, shape, dt=F32):
            return ctx.enter_context(nc.sbuf_tensor(name, shape, dt))

        idx = sb("count_idx", [1, NL], I32)
        f = sb("count_f", [1, NL])
        neg = sb("count_neg", [1, NL])
        lower = sb("count_lower", [1, NL, NL])
        same = sb("count_same", [1, NL, NL])
        earlier = sb("count_earlier", [1, NL])
        first = sb("count_first", [1, NL])
        total = sb("count_total", [1, 1])
        loaded = ctx.enter_context(nc.semaphore("count_loaded"))
        link_sem = ctx.enter_context(nc.semaphore("count_step"))
        idle(block, "tensor", "scalar", "gpsimd")

        @block.sync
        def _(sy):
            sy.dma_start(idx[:, :], ins["idx"]).then_inc(loaded, 16)
            sy.dma_start(lower[:, :, :].rearrange("a i j -> a (i j)"), ins["lower"]).then_inc(loaded, 16)

        @block.vector
        def _(ve):
            n = [0]

            def link(instruction):
                n[0] += 1
                instruction.then_inc(link_sem, 1)
                ve.wait_ge(link_sem, n[0])

            ve.wait_ge(loaded, 32)
            link(ve.tensor_copy(f[:, :], idx[:, :]))
            link(ve.tensor_scalar(neg[:, :], f[:, :], 0.0, float(T), ALU.is_lt, ALU.mult))
            link(ve.tensor_tensor(f[:, :], f[:, :], neg[:, :], ALU.add))
            link(ve.tensor_scalar(f[:, :], f[:, :], 0.0, float(T - 1), ALU.max, ALU.min))
            link(ve.tensor_tensor(same[:, :, :], f[:, :].unsqueeze(2).broadcast_to([1, NL, NL]),
                                  f[:, :].unsqueeze(1).broadcast_to([1, NL, NL]), ALU.is_equal))
            link(ve.tensor_tensor(same[:, :, :], same[:, :, :], lower[:, :, :], ALU.mult))
            link(ve.tensor_reduce(earlier[:, :], same[:, :, :], AX_X, ALU.add))
            link(ve.tensor_scalar(first[:, :], earlier[:, :], 0.0, None, ALU.is_equal))
            link(ve.tensor_reduce(total[:, :], first[:, :], AX_X, ALU.add))
            link(ve.tensor_copy(number[:, :], total[:, :]))


RSQRT_STEPS = 18
RSQRT_SEED = 0x5F3759DF


def inverse_deviation(ve, x, ST, RS, made):
    y, neg, v, w, total, gap = (RS[:, i, :] for i in range(6))
    n = [0]

    def link(instruction):
        instruction.then_inc(made.sem, 1)
        wait(ve, made, x, n[0])
        n[0] += 1

    link(ve.tensor_tensor(total, ST[:, :, 1], ST[:, :, 4], ALU.add))
    link(ve.tensor_tensor(gap, ST[:, :, 1], ST[:, :, 4], ALU.subtract))
    link(ve.tensor_tensor(v, ST[:, :, 2], ST[:, :, 5], ALU.add))
    link(ve.scalar_tensor_tensor(out=gap, in0=gap, scalar=0.25, in1=gap, op0=ALU.mult, op1=ALU.mult))
    link(ve.tensor_scalar(v, v, 1.0 / M, EPS, ALU.mult, ALU.add))
    link(ve.tensor_tensor(v, v, gap, ALU.add))
    link(ve.tensor_scalar(w.bitcast(I32), v.bitcast(I32), 1, None, ALU.logical_shift_right))
    link(ve.tensor_scalar(y.bitcast(I32), w.bitcast(I32), -1, RSQRT_SEED, ALU.mult, ALU.add))
    for _ in range(3):
        link(ve.tensor_tensor(w, y, y, ALU.mult))
        link(ve.scalar_tensor_tensor(out=w, in0=w, scalar=-0.5, in1=v, op0=ALU.mult, op1=ALU.mult))
        link(ve.scalar_tensor_tensor(out=y, in0=w, scalar=1.5, in1=y, op0=ALU.add, op1=ALU.mult))
    ve.scalar_tensor_tensor(out=neg, in0=total, scalar=-0.5, in1=y, op0=ALU.mult, op1=ALU.mult)\
        .then_inc(made.sem, 1)

def systems_phase(nc, ins, t, slots, spill):
    hpc = P // slots
    CH = HA // hpc
    CPO = CH // 2
    TL = T + slots
    TB = max(1, CH * P // 512)
    TW = CH * P // TB
    ZB = 1 if slots == SMALL else 2
    CZ = CH // ZB
    sfx = f"_{slots}"
    with ExitStack() as ctx, nc.Block() as block:
        def sb(name, shape, dt=F32):
            return ctx.enter_context(nc.sbuf_tensor("a_" + name + sfx, shape, dt))

        def sem(name):
            return t.semaphore("a_" + name)

        wkv = sb("wkv", [C + 1, 2 * C])
        wq = sb("wq", [C + 1, C])
        res = sb("res", [C + 1, HT, P])
        ow = sb("ow", [P, 2, M])
        ew = sb("ew", [P, 2, L])
        mask8 = sb("mask8", [P, 2, L // 4], I32)
        maskf = sb("maskf", [P, 2, L])
        ln_g = sb("ln_g", [P, M])
        ln_b = sb("ln_b", [P, M])
        wa = {n: sb("attn_w" + n, [P, 2, M]) for n in "qkv"}
        ba = {n: sb("attn_b" + n, [P, 2]) for n in "qk"}
        bv = sb("bv", [P, M])
        X = sb("x", [C + 1, 2, L, HT])
        EK = sb("ek", [P, 2, 2, 2, M])
        EQ = sb("eq", [P, 2, 2, L])
        DE = sb("de", [P, 2, L])
        YT = sb("yt", [P, 2, 2, L])
        ST1, RS1 = sb("st1", [P, 2, 6]), sb("rs1", [P, 6, 2])
        ST2, RS2 = sb("st2", [P, NT, 6]), sb("rs2", [P, 6, NT])
        H0 = sb("h0", [P, 2, M])
        H = sb("h", [P, 2, NT, M])
        XN = sb("xn", [P, 2, NT, M])
        XT = sb("xt", [P, 2, TL])
        KT, KS = sb("kt", [P, 2, TL]), sb("ks", [P, 2, TL])
        QT, QS = sb("qt", [P, 2, T]), sb("qs", [P, 2, T])
        VA = sb("va", [P, 2, NT, HA, R])
        LL, LS = sb("ll", [P, CH, P]), sb("ls", [P, CH, P])
        LN = sb("ln", [P, CH])
        CK = sb("ck", [P, 2, TL])
        PK = sb("pk", [P, 2, CH, TL])
        PQ = sb("pq", [P, 2, CH, T])
        PN = sb("pn", [P, NT, CH * P])
        ZM = sb("zm", [P, CZ, hpc, R])
        Z = sb("z", [P, 2, CH, R])
        W = sb("w", [P, 2, CH, slots])

        order = ([("kv", 0, 0), ("kv", 1, 0), ("q", 0, 0)] + [("t", i, 2) for i in range(NT * TB)]
                 + [("den", 0, 0), ("num", 0, 0), ("xt", 0, 1), ("xt", 1, 1)] + [("z", i, 2) for i in range(ZB)]
                 + [("ak", 0, 1), ("ak", 1, 1), ("aq", 0, 1), ("aq", 1, 1), ("h", 0, 0)]
                 + [("v", i, 1) for i in range(NT)] + [("ln", 0, 1)]
                 + [("ck", i, 1) for i in range(CH)] + [("cq", i, 1) for i in range(CH)])
        per = {stage: sum(1 for job in order if job[0] == stage) for stage, _, _ in order}
        ready = {s: Signal(sem("ready_" + s), n) for s, n in per.items()}
        free = {s: Signal(sem("free_" + s), n) for s, n in per.items()}
        ring = Ring(order, free, t.banks)
        weights = sem("weights")
        mask_ready = sem("mask_ready")
        ew_ready = sem("ew_ready")
        ones_set = sem("ones_set")
        x_loaded = [sem(f"x_loaded{i}") for i in range(2)]
        txt_loaded = [sem(f"txt_loaded{i}") for i in range(2)]
        h_stored = [sem(f"h_stored{i}") for i in range(2)]
        pq_stored = [sem(f"pq_stored{i}") for i in range(2)]
        z_stored = [sem(f"z_stored{i}") for i in range(2)]
        w_stored = [sem(f"w_stored{i}") for i in range(2)]
        ek_made = Signal(sem("ek_made"), 2)
        de_made = Signal(sem("de_made"), 1)
        stat1 = Signal(sem("stat1"), 2)
        rs1_made = Signal(sem("rs1_made"), RSQRT_STEPS)
        hg_made = Signal(sem("hg_made"), 1)
        h_made = Signal(sem("h_made"), 1)
        stat2 = Signal(sem("stat2"), NT)
        rs2_made = Signal(sem("rs2_made"), RSQRT_STEPS)
        xn_made = Signal(sem("xn_made"), NT)
        k_made = Signal(sem("k_made"), 2)
        ll_made = Signal(sem("ll_made"), CH)
        ls_made = Signal(sem("ls_made"), 1)
        pk_made = Signal(sem("pk_made"), CH)
        pq_made = Signal(sem("pq_made"), CH)
        zr_made = Signal(sem("zr_made"), ZB)
        z_made = Signal(sem("z_made"), ZB)
        w0_made = Signal(sem("w0_made"), 1)
        w_made = Signal(sem("w_made"), 1)
        loads = [(wkv[:, :], ins["wkv"]), (wq[:, :], ins["wq_tok"]), (res[:, :, :], ins["res"]),
                 (ow[:, :, :], ins["ow"]), (ew[:, :, :], ins["w_bias"]), (mask8[:, :, :], ins["mask"]),
                 (ln_g[:, :], ins["ln_g"].broadcast_to([P, M])), (ln_b[:, :], ins["ln_b"].broadcast_to([P, M])),
                 (bv[:, :], ins["bv"].broadcast_to([P, M])), (ba["q"][:, :], ins["bq"]), (ba["k"][:, :], ins["bk"])]
        loads += [(wa[n][:, :, :], ins["wa_" + n]) for n in "qkv"]
        loads += [(X[C:C + 1, u, :, :].rearrange("p l h -> p (l h)"), ins["one_row"]) for u in range(2)]

        @block.sync
        def _(sy):
            for dst, src in loads:
                sy.dma_start(dst, src).then_inc(weights, 16)

            def load(x):
                wait(sy, ready["h"], x, back=2)
                sy.dma_start(X[0:C, x.par, :, :].rearrange("p l h -> p (l h)"),
                             ins["x"][bass.ds(x.s, 1)].rearrange("n c l -> c (n l)")).then_inc(x_loaded[x.par], 16)
                wait_dma(sy, h_stored, x, back=2)
                wait(sy, xn_made, x, back=2)
                sy.dma_start(H[:, x.par, 2, :], ins["txt"][bass.ds(x.s, 1)].rearrange("n p m -> p (n m)"))\
                    .then_inc(txt_loaded[x.par], 16)

            def store_h(x):
                wait(sy, h_made, x)
                sy.dma_start(spill.h[bass.ds(x.s, 1)].rearrange("n p k -> p (n k)"),
                             H[:, x.par, :, :].rearrange("p c m -> p (c m)")).then_inc(h_stored[x.par], 16)

            def store_pq(x):
                wait(sy, pq_made, x)
                sy.dma_start(spill.pq[bass.ds(x.s, 1)].rearrange("n p k -> p (n k)"),
                             PQ[:, x.par, :, :].rearrange("p c m -> p (c m)")).then_inc(pq_stored[x.par], 16)

            def store_system(x):
                rows = bass.ds(x.s * (HA * slots), HA * slots)
                wait(sy, w_made, x)
                sy.dma_start(spill.w[rows, :].rearrange("(q p) k -> p q k", p=P), W[:, x.par, :, :])\
                    .then_inc(w_stored[x.par], 16)
                wait(sy, z_made, x)
                sy.dma_start(spill.z[rows, :].rearrange("(q p) k -> p q k", p=P), Z[:, x.par, :, :])\
                    .then_inc(z_stored[x.par], 16)

            pipeline(sy, [(0, load), (1, store_h), (2, store_pq), (2, store_system)])
            for stored in (h_stored, pq_stored, z_stored, w_stored):
                for i in range(2):
                    sy.wait_ge(stored[i], 16 * N // 2)

        @block.tensor
        def _(pe):
            def kv(i):
                def step(x):
                    wait_dma(pe, x_loaded, x)
                    ring.wait(pe, "kv", i, x)
                    o = ring.bank("kv", i)[:, :].rearrange("p (a n) -> p a n", a=2)
                    for h in range(HT):
                        mm = pe.matmul(o[:, :, h * C:(h + 1) * C], X[:, x.par, i * P:(i + 1) * P, h],
                                       wkv[:, :].rearrange("p (a n) -> p a n", a=2), start=True, stop=True,
                                       skip_group_check=True)
                    mm.then_inc(ready["kv"].sem, 1)
                return step

            def q(i):
                def step(x):
                    ring.wait(pe, "q", i, x)
                    for h in range(HT):
                        mm = pe.matmul(ring.bank("q")[(h % 2) * C:(h % 2 + 1) * C, (h // 2) * L:(h // 2 + 1) * L],
                                       wq[:, :], X[:, x.par, :, h], start=True, stop=True, skip_group_check=True)
                    mm.then_inc(ready["q"].sem, 1)
                return step

            def mix(stage, which):
                def step(x):
                    wait(pe, free["kv"] if which else ek_made, x)
                    ring.wait(pe, stage, 0, x)
                    for hp in range(2):
                        for sc in range(2):
                            mm = pe.matmul(ring.bank(stage)[:, hp * L:(hp + 1) * L],
                                           EK[:, x.par, sc, which, hp * P:(hp + 1) * P], ew[:, sc, :],
                                           start=(sc == 0), stop=(sc == 1), skip_group_check=True)
                    mm.then_inc(ready[stage].sem, 1)
                return step

            def h(i):
                def step(x):
                    wait(pe, free["num"], x)
                    ring.wait(pe, "h", i, x, ("num",))
                    for tc in range(2):
                        o = ring.bank("h")[:, tc * M:(tc + 1) * M]
                        for hp in range(2):
                            pe.matmul(o, YT[:, x.par, hp, tc * P:(tc + 1) * P], ow[:, hp, :],
                                      start=(hp == 0), stop=False, skip_group_check=True)
                        for hh in range(HT):
                            mm = pe.matmul(o[:, hh // 2 * P:(hh // 2 + 1) * P], X[:, x.par, tc * P:(tc + 1) * P, hh],
                                           res[:, hh, :], start=False, stop=(hh == HT - 1), skip_group_check=True)
                    mm.then_inc(ready["h"].sem, 1)
                return step

            def xt(i):
                def step(x):
                    wait(pe, xn_made, x)
                    ring.wait(pe, "xt", i, x)
                    o = ring.bank("xt", i)
                    for c in range(NT):
                        pe.transpose(o[:, c * P:(c + 1) * P], XN[:, x.par, c, i * P:(i + 1) * P], t.ident[:, :])
                    for c in range(NT):
                        mm = pe.matmul(o[:, T:T + P], XN[:, x.par, c, i * P:(i + 1) * P], t.gather[:, c, :],
                                       start=(c == 0), stop=(c == NT - 1), skip_group_check=True)
                    mm.then_inc(ready["xt"].sem, 1)
                return step

            def project(stage, i):
                w, width = (wa["k"], TL) if stage == "ak" else (wa["q"], T)

                def step(x):
                    wait(pe, free["xt"], x)
                    ring.wait(pe, stage, i, x, ("xt",))
                    for kc in range(2):
                        mm = pe.matmul(ring.bank(stage, i)[:, 0:width], w[:, kc, i * P:(i + 1) * P],
                                       XT[:, kc, 0:width], start=(kc == 0), stop=(kc == 1))
                    mm.then_inc(ready[stage].sem, 1)
                return step

            def v(i):
                def step(x):
                    ring.wait(pe, "v", i, x)
                    for kc in range(2):
                        mm = pe.matmul(ring.bank("v", i)[:, 0:M], XT[:, kc, i * P:(i + 1) * P], wa["v"][:, kc, :],
                                       start=(kc == 0), stop=(kc == 1))
                    mm.then_inc(ready["v"].sem, 1)
                return step

            def ln(i):
                def step(x):
                    wait(pe, ls_made, x)
                    ring.wait(pe, "ln", i, x)
                    for c in range(CH):
                        mm = pe.matmul(ring.bank("ln")[:, c:c + 1], LS[:, c, :], t.ones[:, :], start=True,
                                       stop=True, skip_group_check=True)
                    mm.then_inc(ready["ln"].sem, 1)
                return step

            def distance(stage, i):
                src, sq, width, made = (KT, KS, TL, "ak") if stage == "ck" else (QT, QS, T, "aq")

                def step(x):
                    wait(pe, free[made], x)
                    wait(pe, ll_made, x)
                    ring.wait(pe, stage, i, x, (made,))
                    o = ring.bank(stage, i)[:, 0:width]
                    pe.matmul(o, LL[:, i, :], src[:, i // CPO, 0:width], start=True, stop=False)
                    pe.matmul(o, t.bd[:, i % CPO, :], sq[:, i // CPO, 0:width], start=False, stop=True)\
                        .then_inc(ready[stage].sem, 1)
                return step

            def turned(i):
                c, b = i // TB, i % TB

                def step(x):
                    wait(pe, pk_made, x)
                    ring.wait(pe, "t", i, x)
                    for n in range(TW // P):
                        mm = pe.transpose(ring.bank("t", i)[:, n * P:(n + 1) * P],
                                          PK[:, x.par, b * (TW // P) + n, c * P:(c + 1) * P], t.ident[:, :])
                    mm.then_inc(ready["t"].sem, 1)
                return step

            def z(i):
                def step(x):
                    wait(pe, free["t"], x)
                    wait(pe, free["v"], x)
                    ring.wait(pe, "z", i, x, ("v", "t",))
                    for n in range(CZ):
                        c = i * CZ + n
                        for k in range(NT):
                            mm = pe.matmul(ring.bank("z", i)[:, n * hpc * R:(n + 1) * hpc * R],
                                           PN[:, k, c * P:(c + 1) * P],
                                           VA[:, x.par, k, c * hpc:(c + 1) * hpc, :].rearrange("p h r -> p (h r)"),
                                           start=(k == 0), stop=(k == NT - 1), skip_group_check=True)
                    mm.then_inc(ready["z"].sem, 1)
                return step

            step_of = {"kv": kv, "q": q, "h": h, "xt": xt, "v": v, "ln": ln, "t": turned, "z": z,
                       "den": lambda i: mix("den", 0), "num": lambda i: mix("num", 1)}
            step_of |= {s: (lambda i, s=s: project(s, i)) for s in ("ak", "aq")}
            step_of |= {s: (lambda i, s=s: distance(s, i)) for s in ("ck", "cq")}
            pe.wait_ge(weights, 16 * len(loads))
            pe.wait_ge(ew_ready, 1)
            pipeline(pe, [(skew, step_of[stage](i)) for stage, i, skew in order])

        @block.scalar
        def _(act):
            act.wait_ge(weights, 16 * len(loads))
            act.wait_ge(mask_ready, 2)
            act.activation(ew[:, :, :], maskf[:, :, :], ACT.Exp).then_inc(ew_ready, 1)

            def exp_k(x):
                for i in range(2):
                    wait(act, ready["kv"], x, i)
                    wait(act, ready["num"], x, back=2)
                    act.activation(EK[:, x.par, i, 0, :], ring.bank("kv", i)[:, 0:M], ACT.Exp).then_inc(ek_made.sem, 1)

            def exp_q(x):
                wait(act, ready["q"], x)
                wait(act, free["den"], x, back=2)
                act.activation(EQ[:, x.par, :, :].rearrange("p a l -> p (a l)"), ring.bank("q")[:, :], ACT.Exp,
                               scale=-1.0).then_inc(free["q"].sem, 1)

            def norm1(x):
                wait(act, rs1_made, x)
                wait(act, hg_made, x, back=1)
                for i in range(2):
                    o = act.activation(H0[:, i, :], ring.bank("h")[:, i * M:(i + 1) * M], ACT.Identity,
                                       bias=RS1[:, 1, i:i + 1], scale=RS1[:, 0, i:i + 1])
                o.then_inc(free["h"].sem, 1)

            def norm2(x):
                wait(act, rs2_made, x)
                wait(act, ready["xt"], x, back=2)
                for i in range(NT):
                    act.activation(XN[:, x.par, i, :], H[:, x.par, i, :], ACT.Identity,
                                   bias=RS2[:, 1, i:i + 1], scale=RS2[:, 0, i:i + 1]).then_inc(xn_made.sem, 1)

            def take_xt(x):
                for i in range(2):
                    wait(act, ready["xt"], x, i)
                    wait(act, ready["v"], x, back=1)
                    act.activation(XT[:, i, :], ring.bank("xt", i)[:, 0:TL], ACT.Copy).then_inc(free["xt"].sem, 1)

            def take_k(x):
                for i in range(2):
                    wait(act, ready["ak"], x, i)
                    wait(act, ready["ck"], x, back=1)
                    wait(act, ll_made, x, back=1)
                    act.activation(KT[:, i, :], ring.bank("ak", i)[:, 0:TL], ACT.Identity,
                                   bias=ba["k"][:, i:i + 1]).then_inc(k_made.sem, 1)
                    act.activation(KS[:, i, :], ring.bank("ak", i)[:, 0:TL], ACT.Square,
                                   bias=ba["k"][:, i:i + 1]).then_inc(free["ak"].sem, 1)

            def take_q(x):
                for i in range(2):
                    wait(act, ready["aq"], x, i)
                    wait(act, ready["cq"], x, back=1)
                    act.activation(QT[:, i, :], ring.bank("aq", i)[:, 0:T], ACT.Identity, bias=ba["q"][:, i:i + 1])
                    act.activation(QS[:, i, :], ring.bank("aq", i)[:, 0:T], ACT.Square,
                                   bias=ba["q"][:, i:i + 1]).then_inc(free["aq"].sem, 1)

            def square_l(x):
                wait(act, ll_made, x)
                wait(act, ready["ln"], x, back=1)
                act.activation(LS[:, :, :], LL[:, :, :], ACT.Square, scale=0.5).then_inc(ls_made.sem, 1)

            def take_ln(x):
                wait(act, ready["ln"], x)
                wait(act, free["cq"], x, back=1)
                act.activation(LN[:, :], ring.bank("ln")[:, 0:CH], ACT.Copy).then_inc(free["ln"].sem, 1)

            def kernels(x):
                for i in range(CH):
                    wait(act, free["ck"], x, i)
                    wait(act, ready["t"], x, back=2)
                    wait(act, w0_made, x, back=2)
                    act.activation(PK[:, x.par, i, :], CK[:, i % 2, :], ACT.Exp, scale=t.rate[:, 0:1])\
                        .then_inc(pk_made.sem, 1)
                for i in range(CH):
                    wait(act, free["cq"], x, i)
                    wait_dma(act, pq_stored, x, back=2)
                    act.activation(PQ[:, x.par, i, :], CK[:, i % 2, 0:T], ACT.Exp, scale=t.rate[:, 0:1])\
                        .then_inc(pq_made.sem, 1)

            pipeline(act, [(0, exp_k), (0, exp_q), (1, norm2), (1, take_xt), (1, take_k), (1, take_q), (1, square_l),
                           (0, norm1), (1, take_ln), (1, kernels)])

        @block.gpsimd
        def _(po):
            po.memset(VA[:, :, :, :, DA:R], 1.0).then_inc(ones_set, 1)
            po.wait_ge(weights, 16 * len(loads))

            def affine(x):
                wait(po, free["h"], x)
                wait(po, xn_made, x, back=2)
                wait_dma(po, h_stored, x, back=2)
                po.tensor_tensor(H[:, x.par, 0:2, :], H0[:, :, :], ln_g[:, :].unsqueeze(1).broadcast_to([P, 2, M]),
                                 ALU.mult).then_inc(hg_made.sem, 1)
                wait(po, hg_made, x)
                wait_dma(po, txt_loaded, x)
                po.tensor_tensor(H[:, x.par, 0:2, :], H[:, x.par, 0:2, :],
                                 ln_b[:, :].unsqueeze(1).broadcast_to([P, 2, M]), ALU.add).then_inc(h_made.sem, 1)

            def system(x):
                wait(po, pk_made, x)
                wait_dma(po, w_stored, x, back=2)
                po.tensor_tensor(W[:, x.par, :, :], PK[:, x.par, :, T:TL],
                                 t.reg[:, 1:2].unsqueeze(1).broadcast_to([P, CH, slots]), ALU.mult)\
                    .then_inc(w0_made.sem, 1)
                wait(po, w0_made, x)
                po.tensor_tensor(W[:, x.par, :, :], W[:, x.par, :, :],
                                 t.regd[:, :].unsqueeze(1).broadcast_to([P, CH, slots]), ALU.add).then_inc(w_made.sem, 1)

            pipeline(po, [(0, affine), (1, system)])

        @block.vector
        def _(ve):
            ve.wait_ge(weights, 16 * len(loads))
            ve.tensor_copy(maskf[:, :, :], mask8[:, :, :].bitcast(U8)).then_inc(mask_ready, 1)
            ve.wait_ge(mask_ready, 1)
            ve.tensor_tensor(maskf[:, :, :], maskf[:, :, :], ew[:, :, :], ALU.mult).then_inc(mask_ready, 1)
            ve.wait_ge(ones_set, 1)

            def v_exp_k(x):
                for i in range(2):
                    wait(ve, ek_made, x, i)
                    wait(ve, ready["num"], x, back=2)
                    ve.tensor_tensor(EK[:, x.par, i, 1, :], EK[:, x.par, i, 0, :], ring.bank("kv", i)[:, M:2 * M],
                                     ALU.mult).then_inc(free["kv"].sem, 1)

            def y(x):
                wait(ve, ready["den"], x)
                wait(ve, free["q"], x)
                wait(ve, free["num"], x, back=1)
                ve.scalar_tensor_tensor(out=DE[:, :, :], in0=EQ[:, x.par, :, :], scalar=1.0,
                                        in1=ring.bank("den")[:, :].rearrange("p (a l) -> p a l", a=2),
                                        op0=ALU.add, op1=ALU.mult).then_inc(free["den"].sem, 1)
                wait(ve, free["den"], x)
                ve.reciprocal(DE[:, :, :], DE[:, :, :]).then_inc(de_made.sem, 1)
                wait(ve, de_made, x)
                wait(ve, ready["num"], x)
                wait(ve, ready["h"], x, back=2)
                ve.tensor_tensor(YT[:, x.par, :, :], DE[:, :, :],
                                 ring.bank("num")[:, :].rearrange("p (a l) -> p a l", a=2), ALU.mult)\
                    .then_inc(free["num"].sem, 1)

            def stats1(x):
                wait(ve, ready["h"], x)
                for i in range(2):
                    ve.bn_stats(ST1[:, i, :], ring.bank("h")[:, i * M:(i + 1) * M]).then_inc(stat1.sem, 1)
                wait(ve, stat1, x)
                wait(ve, free["h"], x, back=1)
                inverse_deviation(ve, x, ST1, RS1, rs1_made)

            def stats2(x):
                wait(ve, h_made, x)
                for i in range(NT):
                    ve.bn_stats(ST2[:, i, :], H[:, x.par, i, :]).then_inc(stat2.sem, 1)
                wait(ve, stat2, x)
                wait(ve, xn_made, x, back=1)
                inverse_deviation(ve, x, ST2, RS2, rs2_made)

            def landmarks(x):
                wait(ve, k_made, x)
                wait(ve, ready["cq"], x, back=1)
                wait(ve, ls_made, x, back=1)
                for i in range(CH):
                    ve.scalar_tensor_tensor(
                        out=LL[:, i, :].rearrange("p (h k) -> p h k", h=hpc),
                        in0=KT[:, i // CPO, T:TL].unsqueeze(1).broadcast_to([P, hpc, slots]), scalar=-2.0,
                        in1=t.bd[:, i % CPO, :].rearrange("p (h k) -> p h k", h=hpc),
                        op0=ALU.mult, op1=ALU.mult).then_inc(ll_made.sem, 1)

            def take_v(x):
                for i in range(NT):
                    wait(ve, ready["v"], x, i)
                    wait(ve, ready["z"], x, back=2)
                    ve.tensor_tensor(VA[:, x.par, i, :, 0:DA],
                                     ring.bank("v", i)[:, 0:M].rearrange("p (h d) -> p h d", h=HA),
                                     bv[:, :].rearrange("p (h d) -> p h d", h=HA), ALU.add).then_inc(free["v"].sem, 1)

            def clamp(x):
                wait(ve, free["ln"], x)
                for n in range(2 * CH):
                    stage, i = ("ck", "cq")[n // CH], n % CH
                    wait(ve, ready[stage], x, i)
                    if n < 2:
                        wait(ve, pq_made, x, CH - 2 + n, back=1)
                    elif n - 2 < CH:
                        wait(ve, pk_made, x, n - 2)
                    else:
                        wait(ve, pq_made, x, n - 2 - CH)
                    width = (TL, T)[n // CH]
                    ve.tensor_scalar(CK[:, n % 2, 0:width], ring.bank(stage, i)[:, 0:width], LN[:, i:i + 1], 0.0,
                                     ALU.add, ALU.max).then_inc(free[stage].sem, 1)

            def take_turned(x):
                for i in range(NT * TB):
                    wait(ve, ready["t"], x, i)
                    wait(ve, ready["z"], x, back=1)
                    ve.tensor_copy(PN[:, i // TB, i % TB * TW:(i % TB + 1) * TW], ring.bank("t", i)[:, 0:TW])\
                        .then_inc(free["t"].sem, 1)

            def right_sides(x):
                for i in range(ZB):
                    wait(ve, ready["z"], x, i)
                    if i:
                        wait(ve, zr_made, x, i - 1)
                    else:
                        wait(ve, zr_made, x, back=1)
                    ve.tensor_tensor(ZM[:, :, :, :],
                                     ring.bank("z", i)[:, 0:CZ * hpc * R].rearrange("p (c h r) -> p c h r", c=CZ, h=hpc),
                                     t.bz[:, :, :].unsqueeze(1).broadcast_to([P, CZ, hpc, R]), ALU.mult)\
                        .then_inc(free["z"].sem, 1)
                    wait(ve, free["z"], x, i)
                    wait_dma(ve, z_stored, x, back=2)
                    own = Z[:, x.par, i * CZ:(i + 1) * CZ, :]
                    ve.tensor_reduce(own, ZM[:, :, :, :].rearrange("p c h r -> p c r h"), AX_X, ALU.add)\
                        .then_inc(zr_made.sem, 1)
                    wait(ve, zr_made, x, i)
                    ve.tensor_scalar(own, own, t.reg[:, 1:2], None, ALU.mult).then_inc(z_made.sem, 1)

            pipeline(ve, [(0, v_exp_k), (1, stats2), (2, take_turned), (0, y), (2, right_sides), (1, landmarks),
                          (0, stats1), (1, take_v), (1, clamp)])


def product(pe, out, operands, start, stop):
    passes = [(a[:, u], b[:, v]) for a, b in operands for u, v in ((0, 0), (0, 1), (1, 0))]
    for n, (a, b) in enumerate(passes):
        mm = pe.matmul(out, a, b, start=start and n == 0, stop=stop and n == len(passes) - 1)
    return mm


def solve_phase(nc, ins, t, slots, spill):
    GB = N * HA // P if slots == SMALL else 1
    TURNS = N * HA // P // GB
    rows = slots + R
    sfx = f"_{slots}"
    with ExitStack() as ctx, nc.Block() as block:
        def sb(name, shape, dt=F32):
            return ctx.enter_context(nc.sbuf_tensor("s_" + name + sfx, shape, dt))

        def sem(name):
            return t.semaphore("s_" + name)

        A = sb("a", [P, GB, rows, slots])
        ZL = sb("zl", [P, GB, slots, R])
        YO = sb("yo", [P, GB, slots, R])
        DI = sb("di", [P, GB, slots])
        ROW = sb("row", [P, GB, slots])
        PR = sb("pr", [P, GB, rows, slots]) if slots == SMALL else \
            sb("pr", [P, GB, (rows + 1) * (rows + 1) // 4])
        RD = sb("rd", [P, GB, rows])
        loaded = sem("loaded")
        moved = sem("moved")
        stored = sem("stored")
        link_sem = sem("step")
        idle(block, "tensor")
        wo = sb("wo", [P, 2, M])
        w1 = sb("w1", [P, 2, F])
        w2 = sb("w2", [P, FC, M + GE])
        lora_b = sb("lora_b", [3 * G3, F + M])
        weights = sem("weights")
        high = sem("high")
        low_made = sem("low_made")
        loads = [(w1[:, :, :], ins["w1"]), (w2[:, :, :], ins["w2"]), (wo[:, :, :], ins["wo"]),
                 (lora_b[:, :], ins["lora_b"])]
        splits = [(w1[:, :, :], t.w1[:, 0, :, :], t.w1[:, 1, :, :]), (w2[:, :, :], t.w2[:, 0, :, :], t.w2[:, 1, :, :]),
                  (wo[:, :, :], t.wo[:, 0, :, :], t.wo[:, 1, :, :])]
        STEPS = 9 * slots - 6
        w_sys = spill.w.rearrange("(g p k) j -> p g (k j)", p=P, k=slots)
        z_sys = spill.z.rearrange("(g p k) r -> p g (k r)", p=P, k=slots)
        y_sys = spill.y.rearrange("(g p k) r -> p g (k r)", p=P, k=slots)

        @block.sync
        def _(sy):
            def batch(turn, first=False):
                if not first:
                    sy.wait_ge(stored, turn * 16)
                    sy.wait_ge(moved, turn)
                sy.dma_start(A[:, :, 0:slots, :].rearrange("p g k j -> p g (k j)"),
                             w_sys[:, bass.ds(turn * GB, GB), :]).then_inc(loaded, 16)
                sy.dma_start(ZL[:, :, :, :].rearrange("p g k r -> p g (k r)"),
                             z_sys[:, bass.ds(turn * GB, GB), :]).then_inc(loaded, 16)
                sy.wait_ge(moved, turn + 1)
                sy.dma_start(y_sys[:, bass.ds(turn * GB, GB), :],
                             YO[:, :, :, :].rearrange("p g k r -> p g (k r)")).then_inc(stored, 16)

            for dst, src in loads:
                sy.dma_start(dst, src).then_inc(weights, 16)
            batch(0, first=True)
            if TURNS > 1:
                with sy.Fori(1, TURNS) as turn:
                    batch(turn)
            sy.wait_ge(stored, TURNS * 16)

        @block.scalar
        def _(act):
            act.wait_ge(weights, 16 * len(loads))
            for whole, hi, lo in splits:
                act.activation(hi, whole, ACT.Copy).then_inc(high, 1)
            act.activation(t.lora_b[:, :], lora_b[:, :], ACT.Copy).then_inc(high, 1)

        @block.gpsimd
        def _(po):
            for n, (whole, hi, lo) in enumerate(splits):
                po.wait_ge(high, n + 1)
                po.tensor_tensor(lo, whole, hi, ALU.subtract).then_inc(low_made, 1)
                po.wait_ge(low_made, n + 1)
            po.wait_ge(high, len(splits) + 1)
            low = slice(G3, 2 * G3)
            po.tensor_tensor(t.lora_b[low, :], lora_b[low, :], t.lora_b[low, :], ALU.subtract)

        @block.vector
        def _(ve):
            def batch(turn):
                n = [0]

                def link(instruction):
                    n[0] += 1
                    instruction.then_inc(link_sem, 1)
                    ve.wait_ge(link_sem, turn * STEPS + n[0])

                ve.wait_ge(loaded, turn * 32 + 32)
                link(ve.tensor_copy(A[:, :, slots:rows, :], ZL[:, :, :, :].rearrange("p g k r -> p g r k")))
                for j in range(slots):
                    if j:
                        link(ve.tensor_tensor(ROW[:, :, 0:j], A[:, :, j, 0:j], DI[:, :, 0:j], ALU.mult))
                        m = rows - j
                        if slots == SMALL:
                            pr = PR[:, :, 0:m, 0:j]
                        else:
                            pr = PR[:, :, 0:m * j].rearrange("p g (m j) -> p g m j", j=j)
                        link(ve.tensor_tensor(pr, A[:, :, j:rows, 0:j],
                                              ROW[:, :, 0:j].unsqueeze(2).broadcast_to([P, GB, m, j]), ALU.mult))
                        link(ve.tensor_reduce(RD[:, :, 0:m], pr, AX_X, ALU.add))
                        link(ve.tensor_tensor(A[:, :, j:rows, j], A[:, :, j:rows, j], RD[:, :, 0:m], ALU.subtract))
                    link(ve.reciprocal(DI[:, :, j:j + 1], A[:, :, j, j:j + 1]))
                for i in reversed(range(slots)):
                    z = A[:, :, slots:rows, i]
                    m = slots - 1 - i
                    if m:
                        pr = PR[:, :, 0:R, 0:m] if slots == SMALL else \
                            PR[:, :, 0:R * m].rearrange("p g (c m) -> p g c m", m=m)
                        link(ve.tensor_tensor(pr, A[:, :, slots:rows, i + 1:slots],
                                              A[:, :, i + 1:slots, i].unsqueeze(2).broadcast_to([P, GB, R, m]),
                                              ALU.mult))
                        link(ve.tensor_reduce(RD[:, :, 0:R], pr, AX_X, ALU.add))
                        link(ve.tensor_tensor(z, z, RD[:, :, 0:R], ALU.subtract))
                    link(ve.tensor_tensor(z, z, DI[:, :, i:i + 1].broadcast_to([P, GB, R]), ALU.mult))
                n[0] += 1
                ve.tensor_copy(YO[:, :, :, :], A[:, :, slots:rows, :].rearrange("p g r k -> p g k r"))\
                    .then_inc(moved, 1)
                return n[0]

            if TURNS == 1:
                steps = batch(0)
            else:
                with ve.Fori(0, TURNS) as turn:
                    steps = batch(turn)
            assert steps == STEPS + 1, (steps, STEPS)


def output_phase(nc, ins, out, t, slots, spill):
    hpc = P // slots
    CH = HA // hpc
    sfx = f"_{slots}"
    with ExitStack() as ctx, nc.Block() as block:
        def sb(name, shape, dt=F32):
            return ctx.enter_context(nc.sbuf_tensor("b_" + name + sfx, shape, dt))

        def sem(name):
            return t.semaphore("b_" + name)

        wo, w1, w2, lo_b = t.wo, t.w1, t.w2, t.lora_b
        bo = sb("bo", [P, M])
        r1 = sb("r1", [P, 2, P])
        PQ = sb("pq", [P, 2, CH, T])
        YL = sb("yl", [P, 2, CH, R])
        YY = sb("yy", [P, 2, CH, hpc, R])
        NM = sb("nm", [P, NT, HA])
        NR = sb("nr", [P, NT, HA])
        O = sb("o", [P, NT, M])
        OT = sb("ot", [P, 2, 2, T], FR)
        H = sb("h", [P, 2, NT, M])
        H2 = sb("h2", [P, 2, NT, M])
        ST, RS = sb("st", [P, NT, 6]), sb("rs", [P, 6, NT])
        XN = sb("xn", [P, NT, M])
        XF = sb("xf", [P, 2, T])
        XT = sb("xt", [P, 2, 2, 2, T], FR)
        HID = sb("hid", [P, 2, 2, FC, T], FR)
        gate_buffers = [{n: sb(f"{n}{i}", shape) for n, shape in
                         (("mx", [P, NT]), ("d", [P, NT, E]), ("e", [P, NT, E]), ("sum", [P, NT]),
                          ("rec", [P, NT]), ("gate", [P, NT, E]), ("zg", [P, NT, 3, G3]))} for i in range(2)]
        ZT = [sb(f"zt{i}", [3 * G3, T], FR) for i in range(2)]
        OUT = sb("out", [P, 2, NT, M])

        order = ([("o", i, 0) for i in range(NT)] + [("hid", 0, 1), ("hid", 1, 1), ("g2", 0, 2)]
                 + [("ot", 0, 0), ("ot", 1, 0), ("hid", 2, 1), ("hid", 3, 1)] + [("w", i, 0) for i in range(NT)]
                 + [("hid", i, 1) for i in range(4, FC)]
                 + [("y", 0, 1), ("xt", 0, 0), ("xt", 1, 0), ("y", 1, 1), ("r", 0, 0), ("y", 2, 1), ("g1", 0, 0)])
        per = {stage: sum(1 for job in order if job[0] == stage) for stage, _, _ in order}
        ready = {s: Signal(sem("ready_" + s), n) for s, n in per.items()}
        free = {s: Signal(sem("free_" + s), n) for s, n in per.items()}
        ring = Ring(order, free, t.banks, own={"y": (5, 6, 7), "g1": (4,)}, shared=range(5))
        weights = sem("weights")
        ones_set = sem("ones_set")
        pq_loaded = [sem(f"pq_loaded{i}") for i in range(2)]
        y_loaded = [sem(f"y_loaded{i}") for i in range(2)]
        h_loaded = [sem(f"h_loaded{i}") for i in range(2)]
        out_stored = [sem(f"out_stored{i}") for i in range(2)]
        yy_made = Signal(sem("yy_made"), 1)
        hb_made = Signal(sem("hb_made"), 1)
        norm_made = Signal(sem("norm_made"), 2 * NT)
        stat = Signal(sem("stat"), NT)
        rs_made = Signal(sem("rs_made"), RSQRT_STEPS)
        xn_made = Signal(sem("xn_made"), NT)
        ot_high = Signal(sem("ot_high"), 2)
        xf_made = Signal(sem("xf_made"), 2)
        xt_high = Signal(sem("xt_high"), 2)
        hid_high = Signal(sem("hid_high"), FC)
        zt_high = [Signal(sem(f"zt_high{i}"), 1) for i in range(2)]
        lora_added = Signal(sem("lora_added"), NT)
        logits = [Signal(sem("logits0"), 2), Signal(sem("logits1"), 2 * NT)]
        exps = [Signal(sem(f"exps{i}"), 1) for i in range(2)]
        gates = [Signal(sem(f"gates{i}"), 3) for i in range(2)]
        gated = [free["r"], Signal(sem("gated1"), NT)]
        loads = [(bo[:, :], ins["bo"].broadcast_to([P, M])), (r1[:, :, :], ins["r1"])]

        @block.sync
        def _(sy):
            for dst, src in loads:
                sy.dma_start(dst, src).then_inc(weights, 16)

            def load(x):
                wait(sy, ready["o"], x, back=2)
                sy.dma_start(PQ[:, x.par, :, :].rearrange("p c m -> p (c m)"),
                             spill.pq[bass.ds(x.s, 1)].rearrange("n p k -> p (n k)")).then_inc(pq_loaded[x.par], 16)
                wait(sy, yy_made, x, back=2)
                sy.dma_start(YL[:, x.par, :, :],
                             spill.y[bass.ds(x.s * (HA * slots), HA * slots), :].rearrange("(q p) r -> p q r", p=P))\
                    .then_inc(y_loaded[x.par], 16)
                wait(sy, free["w"], x, back=2)
                sy.dma_start(H[:, x.par, :, :].rearrange("p c m -> p (c m)"),
                             spill.h[bass.ds(x.s, 1)].rearrange("n p k -> p (n k)")).then_inc(h_loaded[x.par], 16)

            def store(x):
                wait(sy, free["y"], x)
                sy.dma_start(out[bass.ds(x.s, 1)].rearrange("n (c p) m -> p (n c) m", p=P), OUT[:, x.par, :, :])\
                    .then_inc(out_stored[x.par], 16)

            pipeline(sy, [(0, load), (2, store)])
            for i in range(2):
                sy.wait_ge(out_stored[i], 16 * N // 2)

        @block.tensor
        def _(pe):
            def o(i):
                def step(x):
                    wait_dma(pe, pq_loaded, x)
                    wait(pe, yy_made, x)
                    ring.wait(pe, "o", i, x)
                    for c in range(CH):
                        mm = pe.matmul(ring.bank("o", i)[:, c * hpc * R:(c + 1) * hpc * R],
                                       PQ[:, x.par, c, i * P:(i + 1) * P],
                                       YY[:, x.par, c, :, :].rearrange("p h r -> p (h r)"), start=True, stop=True,
                                       skip_group_check=True)
                    mm.then_inc(ready["o"].sem, 1)
                return step

            def turn(stage, i, src, made):
                def step(x):
                    wait(pe, made, x)
                    ring.wait(pe, stage, i, x)
                    for c in range(NT):
                        mm = pe.transpose(ring.bank(stage, i)[:, c * P:(c + 1) * P], src[:, c, i * P:(i + 1) * P],
                                          t.ident[:, :])
                    mm.then_inc(ready[stage].sem, 1)
                return step

            def w(i):
                def step(x):
                    wait(pe, free["ot"], x)
                    ring.wait(pe, "w", i, x, ("ot",))
                    mm = product(pe, ring.bank("w", i)[:, 0:M],
                                 [(OT[:, :, kc, i * P:(i + 1) * P], wo[:, :, kc, :]) for kc in range(2)], True, True)
                    mm.then_inc(ready["w"].sem, 1)
                return step

            def r(i):
                def step(x):
                    wait(pe, free["xt"], x)
                    ring.wait(pe, "r", i, x, ("xt",))
                    for c in range(NT):
                        for kc in range(2):
                            mm = pe.matmul(ring.bank("r")[:, c * P:(c + 1) * P],
                                           XF[:, kc, c * P:(c + 1) * P], r1[:, kc, :],
                                           start=(kc == 0), stop=(kc == 1), skip_group_check=True)
                    mm.then_inc(ready["r"].sem, 1)
                return step

            def g(n):
                stage = ("g1", "g2")[n]

                def step(x):
                    wait(pe, gated[n], x)
                    ring.wait(pe, stage, 0, x)
                    for c in range(NT):
                        mm = pe.matmul(ring.bank(stage)[0:3 * G3, c * P:(c + 1) * P],
                                       gate_buffers[n]["zg"][:, c, :, :].rearrange("p u g -> p (u g)"),
                                       t.ident[:, :], start=True, stop=True, skip_group_check=True)
                    mm.then_inc(ready[stage].sem, 1)
                return step

            def hid(i):
                def step(x):
                    wait(pe, free["xt"], x)
                    ring.wait(pe, "hid", i, x, ("xt",))
                    own = slice(i * P, (i + 1) * P)
                    product(pe, ring.bank("hid", i)[:, 0:T],
                            [(w1[:, :, kc, own], XT[:, x.par, :, kc, :]) for kc in range(2)], True, False)
                    wait(pe, free["g1"], x)
                    pe.matmul(ring.bank("hid", i)[:, 0:T], lo_b[:, own], ZT[0][:, :], start=False, stop=True)\
                        .then_inc(ready["hid"].sem, 1)
                return step

            def y(i):
                def step(x):
                    ring.wait(pe, "y", i, x)
                    for f in range(FC):
                        if i == 0:
                            wait(pe, free["hid"], x, f)
                        mm = product(pe, ring.bank("y", i)[:, 0:M + GE],
                                     [(HID[:, x.par, :, f, i * P:(i + 1) * P], w2[:, :, f, :])],
                                     f == 0, f == FC - 1)
                    mm.then_inc(ready["y"].sem, 1)
                return step

            def lora(x):
                wait(pe, free["g2"], x)
                for i in range(NT):
                    pe.matmul(ring.bank("y", i)[:, 0:M], ZT[1][:, i * P:(i + 1) * P], lo_b[:, F:F + M], start=False,
                              stop=True, skip_group_check=True).then_inc(lora_added.sem, 1)

            step_of = {"o": o, "ot": lambda i: turn("ot", i, O, free["o"]), "w": w,
                       "xt": lambda i: turn("xt", i, XN, xn_made), "r": r, "y": y,
                       "g1": lambda i: g(0), "g2": lambda i: g(1), "hid": hid}
            stages = [(skew, step_of[stage](i)) for stage, i, skew in order]
            stages.insert(8, (2, lora))
            pe.wait_ge(weights, 16 * len(loads))
            pipeline(pe, stages)

        @block.scalar
        def _(act):
            act.wait_ge(weights, 16 * len(loads))

            def take_g(n):
                def step(x):
                    stage = ("g1", "g2")[n]
                    wait(act, ready[stage], x)
                    wait(act, (ready["hid"], lora_added)[n], x, back=1)
                    act.activation(ZT[n][:, :], ring.bank(stage)[0:3 * G3, 0:T], ACT.Copy).then_inc(zt_high[n].sem, 1)
                return step

            def take_ot(x):
                for i in range(2):
                    wait(act, ready["ot"], x, i)
                    wait(act, ready["w"], x, back=1)
                    act.activation(OT[:, 0, i, :], ring.bank("ot", i)[:, 0:T], ACT.Copy).then_inc(ot_high.sem, 1)

            def take_xt(x):
                for i in range(2):
                    wait(act, ready["xt"], x, i)
                    wait(act, ready["hid"], x, back=2)
                    act.activation(XT[:, x.par, 0, i, :], ring.bank("xt", i)[:, 0:T], ACT.Copy)\
                        .then_inc(xt_high.sem, 1)
                for i in range(2):
                    wait(act, ready["r"], x, back=1)
                    act.activation(XF[:, i, :], ring.bank("xt", i)[:, 0:T], ACT.Copy).then_inc(xf_made.sem, 1)

            def relu(i):
                def step(x):
                    wait(act, ready["hid"], x, i)
                    wait(act, ready["y"], x, back=2)
                    act.activation(HID[:, x.par, 0, i, :], ring.bank("hid", i)[:, 0:T], ACT.Relu)\
                        .then_inc(hid_high.sem, 1)
                return step

            def norm(x):
                wait(act, rs_made, x)
                wait(act, ready["xt"], x, back=1)
                for i in range(NT):
                    act.activation(XN[:, i, :], H2[:, x.par, i, :], ACT.Identity, bias=RS[:, 1, i:i + 1],
                                   scale=RS[:, 0, i:i + 1]).then_inc(xn_made.sem, 1)

            def exp(n):
                def step(x):
                    b = gate_buffers[n]
                    wait(act, logits[n], x)
                    wait(act, gates[n], x, 2, back=1)
                    act.activation(b["e"][:, :, :], b["d"][:, :, :], ACT.Exp).then_inc(exps[n].sem, 1)
                return step

            pipeline(act, [(1, relu(0)), (1, relu(1)), (2, take_g(1)), (0, take_ot), (1, relu(2)), (1, relu(3)),
                           (1, relu(4)), (1, relu(5)), (1, relu(6)), (0, norm), (1, relu(7)), (0, take_xt),
                           (0, exp(0)), (1, exp(1)), (0, take_g(0))])

        @block.gpsimd
        def _(po):
            for n in range(2):
                po.memset(gate_buffers[n]["zg"][:, :, :, ER + 1:G3], 0.0).then_inc(ones_set, 1)
                po.memset(gate_buffers[n]["zg"][:, :, :, ER:ER + 1], 1.0).then_inc(ones_set, 1)
            po.wait_ge(weights, 16 * len(loads))

            def spread(x):
                wait_dma(po, y_loaded, x)
                wait(po, ready["o"], x, back=2)
                po.tensor_tensor(YY[:, x.par, :, :, :], YL[:, x.par, :, :].unsqueeze(2).broadcast_to([P, CH, hpc, R]),
                                 t.bz[:, :, :].unsqueeze(1).broadcast_to([P, CH, hpc, R]), ALU.mult)\
                    .then_inc(yy_made.sem, 1)

            def add_bias(x):
                wait_dma(po, h_loaded, x)
                po.tensor_tensor(H[:, x.par, :, :], H[:, x.par, :, :], bo[:, :].unsqueeze(1).broadcast_to([P, NT, M]),
                                 ALU.add).then_inc(hb_made.sem, 1)

            pipeline(po, [(0, spread), (0, add_bias)])

        @block.vector
        def _(ve):
            ve.wait_ge(weights, 16 * len(loads))
            ve.wait_ge(ones_set, 4)

            def divide(i):
                def step(x):
                    wait(ve, ready["o"], x, i)
                    b = ring.bank("o", i)[:, 0:HA * R].rearrange("p (h r) -> p h r", h=HA)
                    ve.tensor_scalar(NM[:, i, :], b[:, :, DA], 1e-10, None, ALU.max).then_inc(norm_made.sem, 1)
                    wait(ve, norm_made, x, 2 * i)
                    ve.reciprocal(NR[:, i, :], NM[:, i, :]).then_inc(norm_made.sem, 1)
                    wait(ve, norm_made, x, 2 * i + 1)
                    wait(ve, ready["ot"], x, back=1)
                    ve.tensor_tensor(O[:, i, :].rearrange("p (h d) -> p h d", h=HA), b[:, :, 0:DA],
                                     NR[:, i, :].unsqueeze(2).broadcast_to([P, HA, DA]), ALU.mult)\
                        .then_inc(free["o"].sem, 1)
                return step

            def finish(x):
                for i in range(NT):
                    wait(ve, lora_added, x, i)
                    wait_dma(ve, out_stored, x, back=2)
                    ve.tensor_tensor(OUT[:, x.par, i, :], H2[:, x.par, i, :], ring.bank("y", i)[:, 0:M], ALU.add)\
                        .then_inc(free["y"].sem, 1)

            def low_hid(i):
                def step(x):
                    wait(ve, hid_high, x, i)
                    wait(ve, ready["y"], x, back=2)
                    ve.scalar_tensor_tensor(out=HID[:, x.par, 1, i, :], in0=ring.bank("hid", i)[:, 0:T], scalar=0.0,
                                            in1=HID[:, x.par, 0, i, :], op0=ALU.max, op1=ALU.subtract)\
                        .then_inc(free["hid"].sem, 1)
                return step

            def low_ot(x):
                for i in range(2):
                    wait(ve, ot_high, x, i)
                    wait(ve, ready["w"], x, back=1)
                    ve.tensor_tensor(OT[:, 1, i, :], ring.bank("ot", i)[:, 0:T], OT[:, 0, i, :], ALU.subtract)\
                        .then_inc(free["ot"].sem, 1)

            def low_xt(x):
                for i in range(2):
                    wait(ve, xf_made, x, i)
                    wait(ve, xt_high, x, i)
                    wait(ve, ready["hid"], x, back=2)
                    ve.tensor_tensor(XT[:, x.par, 1, i, :], ring.bank("xt", i)[:, 0:T], XT[:, x.par, 0, i, :],
                                     ALU.subtract).then_inc(free["xt"].sem, 1)

            def low_zt(n):
                def step(x):
                    stage = ("g1", "g2")[n]
                    wait(ve, zt_high[n], x)
                    ve.tensor_tensor(ZT[n][2 * G3:3 * G3, :], ring.bank(stage)[2 * G3:3 * G3, 0:T],
                                     ZT[n][2 * G3:3 * G3, :], ALU.subtract).then_inc(free[stage].sem, 1)
                return step

            def residual(x):
                wait(ve, hb_made, x)
                wait(ve, free["y"], x, back=2)
                for i in range(NT):
                    wait(ve, ready["w"], x, i)
                    ve.tensor_tensor(H2[:, x.par, i, :], H[:, x.par, i, :], ring.bank("w", i)[:, 0:M], ALU.add)\
                        .then_inc(free["w"].sem, 1)
                for i in range(NT):
                    wait(ve, free["w"], x, i)
                    ve.bn_stats(ST[:, i, :], H2[:, x.par, i, :]).then_inc(stat.sem, 1)
                wait(ve, stat, x)
                wait(ve, xn_made, x, back=1)
                inverse_deviation(ve, x, ST, RS, rs_made)

            def shift(n):
                def step(x):
                    b = gate_buffers[n]
                    wait(ve, exps[n], x, back=1)
                    if n == 0:
                        wait(ve, ready["r"], x)
                        p = ring.bank("r")[:, 0:NT * P].rearrange("p (c g) -> p c g", c=NT)[:, :, ER:GATED]
                        ve.tensor_reduce(b["mx"][:, :], p, AX_X, ALU.max).then_inc(logits[n].sem, 1)
                        wait(ve, logits[n], x, 0)
                        ve.tensor_tensor(b["d"][:, :, :], p, b["mx"][:, :].unsqueeze(2).broadcast_to([P, NT, E]),
                                         ALU.subtract).then_inc(logits[n].sem, 1)
                        return
                    for i in range(NT):
                        wait(ve, ready["y"], x, i)
                        p = ring.bank("y", i)[:, M + ER:M + GATED]
                        ve.tensor_reduce(b["mx"][:, i:i + 1], p, AX_X, ALU.max).then_inc(logits[n].sem, 1)
                        wait(ve, logits[n], x, 2 * i)
                        ve.tensor_scalar(b["d"][:, i, :], p, b["mx"][:, i:i + 1], None, ALU.subtract)\
                            .then_inc(logits[n].sem, 1)
                return step

            def gate(n):
                def step(x):
                    b = gate_buffers[n]
                    wait(ve, exps[n], x)
                    ve.tensor_reduce(b["sum"][:, :], b["e"][:, :, :], AX_X, ALU.add).then_inc(gates[n].sem, 1)
                    wait(ve, gates[n], x, 0)
                    ve.reciprocal(b["rec"][:, :], b["sum"][:, :]).then_inc(gates[n].sem, 1)
                    wait(ve, gates[n], x, 1)
                    ve.scalar_tensor_tensor(out=b["gate"][:, :, :], in0=b["e"][:, :, :], scalar=1.0 / RK,
                                            in1=b["rec"][:, :].unsqueeze(2).broadcast_to([P, NT, E]),
                                            op0=ALU.mult, op1=ALU.mult).then_inc(gates[n].sem, 1)
                    wait(ve, gates[n], x, 2)
                    wait(ve, ready[("g1", "g2")[n]], x, back=1)
                    for i in range(NT):
                        p = ring.bank("r")[:, i * P:i * P + ER] if n == 0 else ring.bank("y", i)[:, M:M + ER]
                        zg = ve.tensor_tensor(
                            b["zg"][:, i, :, 0:ER].rearrange("p u (e r) -> p u e r", e=E),
                            p.rearrange("p (e r) -> p e r", e=E).unsqueeze(1).broadcast_to([P, 3, E, RK]),
                            b["gate"][:, i, :].unsqueeze(1).unsqueeze(3).broadcast_to([P, 3, E, RK]), ALU.mult)
                        if n or i == NT - 1:
                            zg.then_inc(gated[n].sem, 1)
                return step

            pipeline(ve, [(0, divide(0)), (0, divide(1)), (0, divide(2)), (1, low_hid(0)), (1, low_hid(1)),
                          (2, low_zt(1)), (0, low_ot), (2, finish), (1, low_hid(2)), (1, low_hid(3)),
                          (0, residual), (1, low_hid(4)), (1, low_hid(5)), (1, low_hid(6)), (1, low_hid(7)),
                          (0, low_xt), (0, shift(0)), (0, gate(0)), (1, shift(1)), (0, low_zt(0)), (1, gate(1))])


class Tables:

    def __init__(self, banks, semaphore):
        self.banks, self.semaphore = banks, semaphore


class Spill:
    pass


def computation(nc, ins, out, banks, semaphore, slots):
    hpc = P // slots
    CH = HA // hpc
    with ExitStack() as ctx:
        def sb(name, shape):
            return ctx.enter_context(nc.sbuf_tensor(f"{name}_{slots}", shape, F32))

        t, spill = Tables(banks, semaphore), Spill()
        t.ident = sb("ident", [P, P])
        t.bd = sb("bd", [P, CH // 2, P])
        t.bz = sb("bz", [P, hpc, R])
        t.diag = sb("diag", [P, slots])
        t.gather = sb("gather", [P, NT, P])
        t.reg = sb("reg", [P, 4])
        t.regd = sb("regd", [P, slots])
        t.rate = sb("rate", [P, 2])
        t.ones = sb("ones", [P, 1])
        spill.h = nc.dram_tensor(f"h_spill_{slots}", (N, P, NT * M), F32, kind="Internal").ap()
        spill.pq = nc.dram_tensor(f"pq_spill_{slots}", (N, P, CH * T), F32, kind="Internal").ap()
        spill.w = nc.dram_tensor(f"w_spill_{slots}", (N * HA * slots, slots), F32, kind="Internal").ap()
        spill.z = nc.dram_tensor(f"z_spill_{slots}", (N * HA * slots, R), F32, kind="Internal").ap()
        spill.y = nc.dram_tensor(f"y_spill_{slots}", (N * HA * slots, R), F32, kind="Internal").ap()
        landmark_tables(nc, ins, slots, t)
        systems_phase(nc, ins, t, slots, spill)

        def parts(name, shape):
            return ctx.enter_context(nc.sbuf_tensor(f"{name}_{slots}", shape, FR))

        t.wo = parts("wo", [P, 2, 2, M])
        t.w1 = parts("w1", [P, 2, 2, F])
        t.w2 = parts("w2", [P, 2, FC, M + GE])
        t.lora_b = parts("lora_b", [3 * G3, F + M])
        solve_phase(nc, ins, t, slots, spill)
        output_phase(nc, ins, out, t, slots, spill)


def build(nc, ins, out):
    with ExitStack() as ctx:
        banks = [ctx.enter_context(nc.psum_tensor(f"bank{i}", [P, 512], F32)) for i in range(NB)]
        number = ctx.enter_context(nc.sbuf_tensor("number", [1, 1], I32))
        count_tokens(nc, ins, number)
        semaphores = {}

        def semaphore(name):
            if name not in semaphores:
                semaphores[name] = ctx.enter_context(nc.semaphore(name))
            return semaphores[name]

        tokens = nc.values_load(number[0:1, 0:1], min_val=1, max_val=NL)
        with nc.If(tokens <= SMALL):
            computation(nc, ins, out, banks, semaphore, SMALL)
        with nc.Else():
            computation(nc, ins, out, banks, semaphore, NL)


def kernel(x, txt, L0_tok_Wq_w, L0_tok_Wq_b, L0_tok_Wk_w, L0_tok_Wk_b, L0_tok_Wv_w, L0_tok_Wv_b, L0_tok_w_bias,
           L0_tok_out_w, L0_tok_out_b, L0_tok_ln_g, L0_tok_ln_b, L0_tok_local_mask, L0_attn_Wq, L0_attn_bq,
           L0_attn_Wk, L0_attn_bk, L0_attn_Wv, L0_attn_bv, L0_attn_Wo, L0_attn_bo, L0_attn_temperature,
           L0_attn_landmark_idx, L0_ffn_W1, L0_ffn_b1, L0_ffn_A1, L0_ffn_B1, L0_ffn_R1, L0_ffn_W2, L0_ffn_b2,
           L0_ffn_A2, L0_ffn_B2, L0_ffn_R2):
    import concourse.bacc as _bacc
    from concourse.bass_utils import run_bass_kernel_spmd as _run

    a = np.asarray

    def rows(w):
        w = a(w)
        return w.reshape(w.shape[0] // P, P, w.shape[1]).transpose(1, 0, 2)

    def experts(w):
        w = a(w)
        return w.transpose(1, 0, 2).reshape(w.shape[1], -1)

    one = np.ones((1, L * HT), np.float32)
    res = np.zeros((C + 1, HT, P), np.float32)
    for h in range(HT):
        own = slice(h % 2 * C, (h % 2 + 1) * C)
        res[:C, h, own], res[C, h, own] = np.eye(C), a(L0_tok_out_b)[h * C:(h + 1) * C]
    low = np.tril(np.ones((NL, NL), np.float32), -1)
    arrays = {
        "x": a(x).reshape(N, C, L * HT),
        "txt": a(txt),
        "wkv": np.concatenate([np.concatenate([a(L0_tok_Wk_w).T, a(L0_tok_Wv_w).T], 1),
                               np.concatenate([a(L0_tok_Wk_b), a(L0_tok_Wv_b)])[None]], 0),
        "wq_tok": np.concatenate([a(L0_tok_Wq_w).T, a(L0_tok_Wq_b)[None]], 0),
        "res": res,
        "ow": rows(L0_tok_out_w),
        "w_bias": rows(a(L0_tok_w_bias).T),
        "mask": rows(a(L0_tok_local_mask).T).copy().view(np.int32),
        "ln_g": a(L0_tok_ln_g)[None], "ln_b": a(L0_tok_ln_b)[None], "one_row": one,
        "wa_q": rows(a(L0_attn_Wq).T), "wa_k": rows(a(L0_attn_Wk).T), "wa_v": rows(a(L0_attn_Wv).T),
        "bq": a(L0_attn_bq).reshape(2, P).T, "bk": a(L0_attn_bk).reshape(2, P).T, "bv": a(L0_attn_bv)[None],
        "wo": rows(a(L0_attn_Wo).T), "bo": a(L0_attn_bo)[None],
        "temperature": a(L0_attn_temperature).reshape(1, 1), "idx": a(L0_attn_landmark_idx).reshape(1, NL),
        "w1": rows(L0_ffn_W1), "r1": rows(np.concatenate([experts(L0_ffn_A1), a(L0_ffn_R1), np.zeros((M, P - GATED), np.float32)], 1)),
        "w2": rows(np.concatenate([a(L0_ffn_W2), experts(L0_ffn_A2), a(L0_ffn_R2),
                                   np.zeros((F, GE - GATED), np.float32)], 1)),
        "lora_b": np.tile(np.concatenate([np.concatenate([a(L0_ffn_B1).reshape(ER, F), a(L0_ffn_B2).reshape(ER, M)], 1),
                                          np.concatenate([a(L0_ffn_b1), a(L0_ffn_b2)])[None],
                                          np.zeros((G3 - ER - 1, F + M), np.float32)], 0), (3, 1)),
        "ident": np.eye(P, dtype=np.float32), "tri": np.stack([low, low.T], 1),
        "iota": np.arange(T, dtype=np.float32)[None], "lower": low.reshape(1, NL * NL),
    }
    for slots in (SMALL, NL):
        arrays[f"bd{slots}"], arrays[f"bz{slots}"], arrays[f"diag{slots}"] = constants(slots)
    nc = _bacc.Bacc("TRN2", target_bir_lowering=False, num_devices=1)
    ins = {}
    feeds = {}
    for name, array in arrays.items():
        array = np.ascontiguousarray(array)
        feeds[f"in_{name}"] = array
        ins[name] = nc.dram_tensor(f"in_{name}", array.shape, mybir.dt.from_np(array.dtype), kind="ExternalInput").ap()
    out = nc.dram_tensor("out", (N, T, M), F32, kind="ExternalOutput").ap()
    build(nc, ins, out)
    return _run(nc, [feeds], core_ids=[0]).results[0]["out"]
```

```python
from contextlib import ExitStack

import concourse.bass as bass
import numpy as np
from concourse import mybir

ALU = mybir.AluOpType
ACT = mybir.ActivationFunctionType
F32 = mybir.dt.float32
I32 = mybir.dt.int32
FR = mybir.dt.float32r
U8 = mybir.dt.uint8
AX_X = mybir.AxisListType.X

P = 128
N = 32
C, L, HT = 64, 256, 4
M = C * HT
NT = 3
T = NT * P
HA, DA = 16, 16
NL = 64
R = DA + 1
F = 1024
FC = F // P
E, RK = 3, 8
ER = E * RK
GATED = ER + E
GE = GATED + GATED % 2
G3 = 32
NB = 8
SMALL = 16
EPS = 1e-5
REG = 1e-6


def constants(slots):
    hpc = P // slots
    chunks = HA // hpc
    p = np.arange(P)
    col = np.arange(P)
    bd = np.zeros((P, chunks // 2, P), np.float32)
    for q in range(chunks // 2):
        bd[:, q, :] = (p[:, None] // DA) == (q * hpc + col[None, :] // slots)
    bz = np.repeat((p[:, None] // slots) == np.arange(hpc)[None, :], R, axis=1).astype(np.float32)
    rd = (p[:, None] % slots == np.arange(slots)[None, :]).astype(np.float32)
    return bd, bz, rd


class Sample:

    def __init__(self, s, pair, par):
        self.s, self.pair, self.par = s, pair, par

    def follows(self, back):
        return not isinstance(self.s, int) or self.s >= back


class Signal:

    def __init__(self, sem, per=1):
        self.sem, self.per = sem, per

    def upto(self, x, i=None, back=0):
        return (x.s - back) * self.per + (self.per if i is None else i + 1)


def dma_count(x, back=0):
    return (x.pair + 1 - back // 2) * 16


def idle(block, *engines):
    for name in engines:
        {"tensor": block.tensor, "scalar": block.scalar, "gpsimd": block.gpsimd}[name](lambda eng: None)


def pipeline(eng, stages, peel=4):

    def turn(t, pair, u):
        for skew, step, *more in stages:
            if isinstance(t, int) and not 0 <= t - skew < N + sum(more):
                continue
            step(Sample(t - skew, pair + (u - skew) // 2, (u - skew) % 2))

    for t in range(peel):
        turn(t, t // 2, t % 2)
    with eng.Fori(peel // 2, N // 2) as pair:
        for u in range(2):
            turn(pair * 2 + u, pair, u)
    for t in range(N, N + peel - 2):
        turn(t, t // 2, t % 2)


class Ring:

    def __init__(self, order, free, banks, own={}, shared=range(NB)):
        self.order, self.free = order, free
        rest = [job[:2] for job in order if job[0] not in own]
        place = {job: shared[n % len(shared)] for n, job in enumerate(rest)}
        place |= {(stage, i): n for stage, kept in own.items() for i, n in enumerate(kept)}
        self.place = [place[job[:2]] for job in order]
        self.of = {job: banks[n] for job, n in place.items()}

    def bank(self, stage, i=0):
        return self.of[stage, i]

    def wait(self, eng, stage, i, x, waited=()):
        at = next(n for n, job in enumerate(self.order) if job[:2] == (stage, i))
        own = self.order[at][2]
        turn, back, n = x.s + own, 0, at
        while True:
            n -= 1
            if n < 0:
                n += len(self.order)
                back += 1
            if self.place[n] != self.place[at]:
                continue
            before, j, skew = self.order[n]
            s = turn - back - skew
            if isinstance(s, int) and s >= N:
                continue
            if before in waited and own - back - skew <= 0 or isinstance(s, int) and s < 0:
                return
            jobs = sum(1 for job in self.order if job[0] == before)
            free = self.free[before]
            eng.wait_ge(free.sem, free.upto(Sample(s, None, None), j if free.per == jobs else None))
            return


def landmark_tables(nc, ins, slots, t):
    hpc = P // slots
    with ExitStack() as ctx, nc.Block() as block:
        def sb(name, shape, dt=F32):
            return ctx.enter_context(nc.sbuf_tensor(f"{name}_{slots}", shape, dt))

        iota = sb("iota", [NL, T])
        token, count, first, rank = (t.marks[n] for n in ("token", "count", "first", "rank"))
        pick = sb("pick", [NL, NL])
        spread = sb("spread", [NL, hpc, slots])
        hot = sb("hot", [NL, T])
        both = sb("both", [NL, 2])
        loaded = t.semaphore("tables_loaded")
        link_sem = t.semaphore("tables_step")
        product = t.semaphore("tables_product")
        loads = [(t.ident[:, :], ins["ident"]), (t.bd[:, :, :], ins[f"bd{slots}"]),
                 (t.bz[:, :, :].rearrange("p h r -> p (h r)"), ins[f"bz{slots}"]),
                 (t.diag[:, :], ins[f"diag{slots}"]), (t.rate[:, 0:1], ins["temperature"].broadcast_to([P, 1])),
                 (iota[:, :], ins["iota"].broadcast_to([NL, T]))]
        a = t.systems
        plain = {"wkv": "wkv", "wq": "wq_tok", "res": "res", "ow": "ow", "ew": "w_bias", "mask8": "mask",
                 "attn_bq": "bq", "attn_bk": "bk", "attn_wfq": "wa_q", "attn_wfk": "wa_k", "attn_wfv": "wa_v"}
        weights_loads = [(a[name][tuple(slice(None) for _ in a[name].shape)], ins[source])
                         for name, source in plain.items()]
        weights_loads += [(a[name][:, :], ins[name].broadcast_to([P, M])) for name in ("ln_g", "ln_b", "bv")]
        weights_loads += [(a["x"][C:C + 1, u, :, :].rearrange("p l h -> p (l h)"), ins["one_row"]) for u in range(2)]
        weights = t.semaphore("a_weights")
        mask_ready = t.semaphore("a_mask_ready")
        wa_high = t.semaphore("a_wa_high")
        known = {}

        @block.sync
        def _(sy):
            for dst, src in loads:
                sy.dma_start(dst, src).then_inc(loaded, 16)

        @block.scalar
        def _(act):
            for dst, src in weights_loads:
                act.dma_start(dst, src).then_inc(weights, 16)
            act.wait_ge(weights, 16 * len(weights_loads))
            for n in "qkv":
                act.activation(a["attn_w" + n][:, 0, :, :], a["attn_wf" + n][:, :, :], ACT.Copy).then_inc(wa_high, 1)
            act.wait_ge(mask_ready, 2)
            act.activation(a["ew"][:, :, :], a["maskf"][:, :, :], ACT.Exp)

        @block.gpsimd
        def _(po):
            po.memset(a["va"][:, :, :, :, DA:R], 1.0)
            for k, n in enumerate("qkv"):
                po.wait_ge(wa_high, k + 1)
                po.tensor_tensor(a["attn_w" + n][:, 1, :, :], a["attn_wf" + n][:, :, :],
                                 a["attn_w" + n][:, 0, :, :], ALU.subtract)

        @block.vector
        def _(ve):
            n = [0]

            def link(instruction):
                n[0] += 1
                instruction.then_inc(link_sem, 1)
                ve.wait_ge(link_sem, n[0])

            ve.memset(a["st"][:, :, :], 0.0)
            link(ve.memset(t.gather[:, :, :], 0.0))
            ve.wait_ge(loaded, 16 * len(loads))
            ve.tensor_copy(a["bd"][:, :, :], t.bd[:, 0:a["bd"].shape[1], :])
            link(ve.reciprocal(t.rate[:, 1:2], t.rate[:, 0:1]))
            link(ve.tensor_scalar(t.rate[:, 0:1], t.rate[:, 1:2], -1.0, None, ALU.mult))
            link(ve.tensor_scalar(pick[:, :], iota[:, 0:NL], rank[:, 0:1], first[:, 0:1], ALU.is_equal, ALU.mult))
            link(ve.tensor_copy(spread[:, :, :], pick[:, 0:slots].unsqueeze(1).broadcast_to([NL, hpc, slots])))
            link(ve.tensor_scalar(hot[:, :], iota[:, :], token[:, 0:1], None, ALU.is_equal))
            link(ve.tensor_copy(both[:, 0:1], count[:, 1:2]))
            link(ve.memset(both[:, 1:2], 1.0))
            known["all"] = n[0]
            ve.wait_ge(product, 1)
            for c in range(NT):
                link(ve.tensor_copy(t.gather[:, c, 0:slots], t.banks[1][:, c * slots:(c + 1) * slots]))
            link(ve.tensor_copy(t.reg[:, 0:2], t.banks[2][:, 0:2]))
            link(ve.tensor_scalar(t.reg[:, 2:3], t.reg[:, 0:1], 1.0, None, ALU.max))
            link(ve.reciprocal(t.reg[:, 3:4], t.reg[:, 2:3]))
            link(ve.tensor_scalar(t.reg[:, 2:3], t.reg[:, 3:4], REG, t.reg[:, 1:2], ALU.mult, ALU.mult))
            link(ve.tensor_scalar(t.reg[:, 3:4], t.reg[:, 1:2], -1.0, 1.0, ALU.mult, ALU.add))
            link(ve.tensor_tensor(t.reg[:, 2:3], t.reg[:, 2:3], t.reg[:, 3:4], ALU.add))
            link(ve.tensor_scalar(t.regd[:, :], t.diag[:, :], t.reg[:, 2:3], None, ALU.mult))
            ve.wait_ge(weights, 16 * len(weights_loads))
            ve.tensor_copy(a["maskf"][:, :, :], a["mask8"][:, :, :].bitcast(U8)).then_inc(mask_ready, 1)
            ve.wait_ge(mask_ready, 1)
            ve.tensor_tensor(a["maskf"][:, :, :], a["maskf"][:, :, :], a["ew"][:, :, :], ALU.mult)\
                .then_inc(mask_ready, 1)

        @block.tensor
        def _(pe):
            pe.wait_ge(link_sem, known["all"])
            pe.matmul(t.banks[2][:, 0:2], spread[:, :, :].rearrange("p h k -> p (h k)"), both[:, :],
                      start=True, stop=True)
            for c in range(NT):
                mm = pe.matmul(t.banks[1][:, c * slots:(c + 1) * slots], hot[:, c * P:(c + 1) * P],
                               pick[:, 0:slots], start=True, stop=True, skip_group_check=True)
            mm.then_inc(product, 1)


def count_tokens(nc, ins, banks, marks, number):
    with ExitStack() as ctx, nc.Block() as block:
        def sb(name, shape, dt=F32):
            return ctx.enter_context(nc.sbuf_tensor("count_" + name, shape, dt))

        idx_row, idx_col = sb("idx_row", [NL, NL], I32), sb("idx_col", [NL, 1], I32)
        row_f, neg_r = sb("row_f", [NL, NL]), sb("neg_r", [NL, NL])
        neg_c = sb("neg_c", [NL, 1])
        tri = sb("tri", [NL, 2, NL])
        same = sb("same", [NL, 2, NL])
        ones = sb("ones", [NL, 1])
        token, count, first, rank = (marks[n] for n in ("token", "count", "first", "rank"))
        loaded = ctx.enter_context(nc.semaphore("count_loaded"))
        link_sem = ctx.enter_context(nc.semaphore("count_step"))
        summed = ctx.enter_context(nc.semaphore("count_summed"))
        idle(block, "scalar", "gpsimd")
        known = {}

        @block.sync
        def _(sy):
            sy.dma_start(idx_row[:, :], ins["idx"].broadcast_to([NL, NL])).then_inc(loaded, 16)
            sy.dma_start(idx_col[:, :], ins["idx"].rearrange("a n -> n a")).then_inc(loaded, 16)
            sy.dma_start(tri[:, :, :], ins["tri"]).then_inc(loaded, 16)

        @block.vector
        def _(ve):
            n = [0]

            def link(instruction):
                n[0] += 1
                instruction.then_inc(link_sem, 1)
                ve.wait_ge(link_sem, n[0])

            link(ve.memset(ones[:, :], 1.0))
            ve.wait_ge(loaded, 48)
            for raw, f, neg in ((idx_row, row_f, neg_r), (idx_col, token, neg_c)):
                link(ve.tensor_copy(f[:, :], raw[:, :]))
                link(ve.tensor_scalar(neg[:, :], f[:, :], 0.0, float(T), ALU.is_lt, ALU.mult))
                link(ve.tensor_tensor(f[:, :], f[:, :], neg[:, :], ALU.add))
                link(ve.tensor_scalar(f[:, :], f[:, :], 0.0, float(T - 1), ALU.max, ALU.min))
            link(ve.tensor_scalar(same[:, 1, :], row_f[:, :], token[:, 0:1], None, ALU.is_equal))
            link(ve.tensor_tensor(same[:, 0, :], same[:, 1, :], tri[:, 0, :], ALU.mult))
            link(ve.tensor_reduce(count[:, :], same[:, :, :], AX_X, ALU.add))
            link(ve.tensor_scalar(first[:, :], count[:, 0:1], 0.0, None, ALU.is_equal))
            known["first"] = n[0]
            ve.wait_ge(summed, 1)
            ve.tensor_copy(number[:, :], banks[0][0:1, 0:1])
            ve.tensor_copy(rank[:, :], banks[1][0:NL, 0:1])

        @block.tensor
        def _(pe):
            pe.wait_ge(link_sem, known["first"])
            pe.matmul(banks[1][0:NL, 0:1], tri[:, 1, :], first[:, :], start=True, stop=True)
            pe.matmul(banks[0][0:1, 0:1], ones[:, :], first[:, :], start=True, stop=True).then_inc(summed, 1)


RSQRT_STEPS = 18
RSQRT_SEED = 0x5F3759DF


def inverse_deviation(ve, x, ST, RS, made, part):
    y, neg, v, w, total, gap = (RS[:, i, :] for i in range(6))
    n = [(0, 8, 14)[part]]

    def follow(back=1):
        if back and n[0]:
            ve.wait_ge(made.sem, made.upto(x, n[0] - back))
        n[0] += 1
        return ve

    if part == 0:
        follow().tensor_tensor(total, ST[:, :, 1], ST[:, :, 4], ALU.add).then_inc(made.sem, 1)
        follow(0).tensor_tensor(gap, ST[:, :, 1], ST[:, :, 4], ALU.subtract).then_inc(made.sem, 1)
        follow(0).tensor_tensor(v, ST[:, :, 2], ST[:, :, 5], ALU.add).then_inc(made.sem, 1)
        follow(2).scalar_tensor_tensor(out=gap, in0=gap, scalar=0.25, in1=gap, op0=ALU.mult, op1=ALU.mult)\
            .then_inc(made.sem, 1)
        follow(2).tensor_scalar(v, v, 1.0 / M, EPS, ALU.mult, ALU.add).then_inc(made.sem, 1)
        follow().tensor_tensor(v, v, gap, ALU.add).then_inc(made.sem, 1)
        follow().tensor_scalar(w.bitcast(I32), v.bitcast(I32), 1, None, ALU.logical_shift_right)\
            .then_inc(made.sem, 1)
        follow().tensor_scalar(y.bitcast(I32), w.bitcast(I32), -1, RSQRT_SEED, ALU.mult, ALU.add)\
            .then_inc(made.sem, 1)
    for _ in range((0, 2, 1)[part]):
        follow().tensor_tensor(w, y, y, ALU.mult).then_inc(made.sem, 1)
        follow().scalar_tensor_tensor(out=w, in0=w, scalar=-0.5, in1=v, op0=ALU.mult, op1=ALU.mult)\
            .then_inc(made.sem, 1)
        follow().scalar_tensor_tensor(out=y, in0=w, scalar=1.5, in1=y, op0=ALU.add, op1=ALU.mult)\
            .then_inc(made.sem, 1)
    if part == 2:
        follow().scalar_tensor_tensor(out=neg, in0=total, scalar=-0.5, in1=y, op0=ALU.mult, op1=ALU.mult)\
            .then_inc(made.sem, 1)


def product(pe, out, operands, start, stop):
    passes = [(a[:, u], b[:, v]) for a, b in operands for u, v in ((0, 0), (0, 1), (1, 0))]
    for n, (a, b) in enumerate(passes):
        mm = pe.matmul(out, a, b, start=start and n == 0, stop=stop and n == len(passes) - 1)
    return mm


def systems_tensors(nc, ctx, slots):
    CPO = HA * slots // P // 2
    shapes = {"wkv": [C + 1, 2 * C], "wq": [C + 1, C],
              "res": [C + 1, HT, P],
              "ow": [P, 2, M], "ew": [P, 2, L],
              "mask8": [P, 2, L // 4],
              "maskf": [P, 2, L], "ln_g": [P, M], "ln_b": [P, M], "bv": [P, M],
              "x": [C + 1, 2, L, HT],
              "bd": [P, CPO, P],
              "st": [P, 2 + NT, 6],
              "va": [P, 2, NT, HA, R]}
    for n in "qkv":
        shapes["attn_w" + n] = [P, 2, 2, M]
        shapes["attn_wf" + n] = [P, 2, M]
    for n in "qk":
        shapes["attn_b" + n] = [P, 2]
    types = {"mask8": I32, "bd": FR} | {"attn_w" + n: FR for n in "qkv"}
    return {n: ctx.enter_context(nc.sbuf_tensor(f"a_{n}_{slots}", shape, types.get(n, F32)))
            for n, shape in shapes.items()}


def systems_phase(nc, ins, t, slots, spill):
    hpc = P // slots
    CH = HA // hpc
    CPO = CH // 2
    TL = T + slots
    TB = max(1, CH * P // 512)
    TW = CH * P // TB
    ZB = 1 if slots == SMALL else 2
    CZ = CH // ZB
    sfx = f"_{slots}"
    with ExitStack() as ctx, nc.Block() as block:
        def sb(name, shape, dt=F32):
            return ctx.enter_context(nc.sbuf_tensor("a_" + name + sfx, shape, dt))

        def sem(name):
            return t.semaphore("a_" + name)

        a = t.systems
        wkv, wq, res, ow, ew, ln_g, ln_b, bv, X, BD, ST, VA = (
            a[n] for n in ("wkv", "wq", "res", "ow", "ew", "ln_g", "ln_b", "bv", "x", "bd", "st", "va"))
        wa = {n: a["attn_w" + n] for n in "qkv"}
        ba = {n: a["attn_b" + n] for n in "qk"}
        EK = sb("ek", [P, 2, 2, 2, M])
        EQ = sb("eq", [P, 2, 2, L])
        DE = sb("de", [P, 2, L])
        YT = sb("yt", [P, 2, 2, L])
        RS = sb("rs", [P, 6, 2 + NT])
        H0 = sb("h0", [P, 2, M])
        H = sb("h", [P, 2, NT, M])
        XN = sb("xn", [P, 2, NT, M])
        XT = sb("xt", [P, 2, 2, TL], FR)
        KT, QT = sb("kt", [P, 2, 2, TL], FR), sb("qt", [P, 2, 2, T], FR)
        KW, QW = sb("kw", [P, 2, TL]), sb("qw", [P, 2, T])
        KS, QS = sb("ks", [P, 2, 2, TL], FR), sb("qs", [P, 2, 2, T], FR)
        LL = sb("ll", [P, 2, CH, P], FR)
        LN = sb("ln", [P, CH])
        LD = sb("ld", [P, CH, slots])
        CK = sb("ck", [P, 2, TL])
        PK = sb("pk", [P, 2, CH, TL])
        PQ = sb("pq", [P, 2, CH, T])
        PN = sb("pn", [P, NT, CH * P])
        ZM = sb("zm", [P, CZ, hpc, R])
        Z = sb("z", [P, 2, CH, R])
        W = sb("w", [P, 2, CH, slots])

        order = ([("kv", 0, 0), ("kv", 1, 0), ("q", 0, 0), ("den", 0, 0), ("num", 0, 0)]
                 + [("cq", i, 3) for i in range(CH)] + [("t", i, 3) for i in range(NT * TB)]
                 + [("xt", 0, 2), ("xt", 1, 2)] + [("z", i, 3) for i in range(ZB)]
                 + [("ak", 0, 2), ("ak", 1, 2), ("aq", 0, 2), ("aq", 1, 2), ("h", 0, 0)]
                 + [("v", i, 2) for i in range(NT)] + [("ck", i, 2) for i in range(CH)])
        per = {stage: sum(1 for job in order if job[0] == stage) for stage, _, _ in order}
        ready = {s: Signal(sem("ready_" + s), n) for s, n in per.items()}
        free = {s: Signal(sem("free_" + s), n) for s, n in per.items()}
        h0_made = free["h"] = Signal(sem("h0_made"), 2)
        ring = Ring(order, free, t.banks, own={"den": (5,), "num": (6,), "h": (7,)}, shared=range(5))
        x_loaded = [sem(f"x_loaded{i}") for i in range(2)]
        txt_loaded = [sem(f"txt_loaded{i}") for i in range(2)]
        h_stored = [sem(f"h_stored{i}") for i in range(2)]
        pq_stored = [sem(f"pq_stored{i}") for i in range(2)]
        z_stored = [sem(f"z_stored{i}") for i in range(2)]
        w_stored = [sem(f"w_stored{i}") for i in range(2)]
        ek_made = Signal(sem("ek_made"), 2)
        de_made = Signal(sem("de_made"), 2)
        stat1 = Signal(sem("stat1"), 2)
        rs_made = Signal(sem("rs_made"), RSQRT_STEPS)
        hg_made = Signal(sem("hg_made"), 2)
        h_made = Signal(sem("h_made"), 2)
        stat2 = Signal(sem("stat2"), NT)
        xn_made = Signal(sem("xn_made"), NT)
        xt_high = Signal(sem("xt_high"), 2)
        high = {"ak": Signal(sem("k_high"), 2), "aq": Signal(sem("q_high"), 2)}
        square_high = {"ak": Signal(sem("ks_high"), 2), "aq": Signal(sem("qs_high"), 2)}
        square_low = {"ak": Signal(sem("ks_low"), 2), "aq": Signal(sem("qs_low"), 2)}
        ln_made = Signal(sem("ln_made"), CH)
        ll_made = Signal(sem("ll_made"), 2 * CH)
        pk_made = Signal(sem("pk_made"), CH)
        pq_made = Signal(sem("pq_made"), CH)
        zr_made = Signal(sem("zr_made"), ZB)
        z_made = Signal(sem("z_made"), ZB)
        w0_made = Signal(sem("w0_made"), 1)
        w_made = Signal(sem("w_made"), 1)

        @block.sync
        def _(sy):
            def load_x(x):
                if x.follows(2):
                    sy.wait_ge(ready["h"].sem, ready["h"].upto(x, back=2))
                sy.dma_start(X[0:C, x.par, :, :].rearrange("p l h -> p (l h)"),
                             ins["x"][bass.ds(x.s, 1)].rearrange("n c l -> c (n l)")).then_inc(x_loaded[x.par], 16)

            def load_txt(x):
                if x.follows(2):
                    sy.wait_ge(h_stored[x.par], dma_count(x, back=2))
                if x.follows(2):
                    sy.wait_ge(xn_made.sem, xn_made.upto(x, back=2))
                sy.dma_start(H[:, x.par, 2, :], ins["txt"][bass.ds(x.s, 1)].rearrange("n p m -> p (n m)"))\
                    .then_inc(txt_loaded[x.par], 16)

            def store_h(x):
                sy.wait_ge(h_made.sem, h_made.upto(x))
                sy.dma_start(spill.h[bass.ds(x.s, 1)].rearrange("n p k -> p (n k)"),
                             H[:, x.par, :, :].rearrange("p c m -> p (c m)")).then_inc(h_stored[x.par], 16)

            def store_pq(x):
                sy.wait_ge(pq_made.sem, pq_made.upto(x))
                sy.dma_start(spill.pq[bass.ds(x.s, 1)].rearrange("n p k -> p (n k)"),
                             PQ[:, x.par, :, :].rearrange("p c m -> p (c m)")).then_inc(pq_stored[x.par], 16)

            def store_w(x):
                rows = bass.ds(x.s * (HA * slots), HA * slots)
                sy.wait_ge(w_made.sem, w_made.upto(x))
                sy.dma_start(spill.w[rows, :].rearrange("(q p) k -> p q k", p=P), W[:, x.par, :, :])\
                    .then_inc(w_stored[x.par], 16)

            def store_z(x):
                rows = bass.ds(x.s * (HA * slots), HA * slots)
                sy.wait_ge(z_made.sem, z_made.upto(x))
                sy.dma_start(spill.z[rows, :].rearrange("(q p) k -> p q k", p=P), Z[:, x.par, :, :])\
                    .then_inc(z_stored[x.par], 16)

            pipeline(sy, [(1, load_txt), (5, store_z), (0, load_x), (2, store_h), (4, store_w), (4, store_pq)],
                     peel=8)
            for stored in (h_stored, pq_stored, z_stored, w_stored):
                for i in range(2):
                    sy.wait_ge(stored[i], 16 * N // 2)

        @block.tensor
        def _(pe):
            def kv(i):
                def step(x):
                    pe.wait_ge(x_loaded[x.par], dma_count(x))
                    ring.wait(pe, "kv", i, x)
                    o = ring.bank("kv", i)[:, :].rearrange("p (a n) -> p a n", a=2)
                    for h in range(HT):
                        mm = pe.matmul(o[:, :, h * C:(h + 1) * C], X[:, x.par, i * P:(i + 1) * P, h],
                                       wkv[:, :].rearrange("p (a n) -> p a n", a=2), start=True, stop=True,
                                       skip_group_check=True)
                    mm.then_inc(ready["kv"].sem, 1)
                return step

            def q(i):
                def step(x):
                    ring.wait(pe, "q", i, x)
                    for h in range(HT):
                        mm = pe.matmul(ring.bank("q")[(h % 2) * C:(h % 2 + 1) * C, (h // 2) * L:(h // 2 + 1) * L],
                                       wq[:, :], X[:, x.par, :, h], start=True, stop=True, skip_group_check=True)
                    mm.then_inc(ready["q"].sem, 1)
                return step

            def mix(stage, which):
                def step(x):
                    if which:
                        pe.wait_ge(free["kv"].sem, free["kv"].upto(x))
                    else:
                        pe.wait_ge(ek_made.sem, ek_made.upto(x))
                    ring.wait(pe, stage, 0, x)
                    for hp in range(2):
                        for sc in range(2):
                            mm = pe.matmul(ring.bank(stage)[:, hp * L:(hp + 1) * L],
                                           EK[:, x.par, sc, which, hp * P:(hp + 1) * P], ew[:, sc, :],
                                           start=(sc == 0), stop=(sc == 1), skip_group_check=True)
                    mm.then_inc(ready[stage].sem, 1)
                return step

            def h(i):
                def step(x):
                    ring.wait(pe, "h", i, x)
                    for tc in range(2):
                        for hh in range(HT):
                            own = slice(tc * M + hh // 2 * P, tc * M + (hh // 2 + 1) * P)
                            pe.matmul(ring.bank("h")[:, own], X[:, x.par, tc * P:(tc + 1) * P, hh], res[:, hh, :],
                                      start=(tc == 0 and hh == 0), stop=False, skip_group_check=True)
                    pe.wait_ge(free["num"].sem, free["num"].upto(x))
                    for tc in range(2):
                        for hp in range(2):
                            mm = pe.matmul(ring.bank("h")[:, tc * M:(tc + 1) * M],
                                           YT[:, x.par, hp, tc * P:(tc + 1) * P], ow[:, hp, :],
                                           start=False, stop=(hp == 1), skip_group_check=True)
                    mm.then_inc(ready["h"].sem, 1)
                return step

            def xt(i):
                def step(x):
                    pe.wait_ge(xn_made.sem, xn_made.upto(x))
                    ring.wait(pe, "xt", i, x)
                    o = ring.bank("xt", i)
                    for c in range(NT):
                        pe.transpose(o[:, c * P:(c + 1) * P], XN[:, x.par, c, i * P:(i + 1) * P], t.ident[:, :])
                    for c in range(NT):
                        mm = pe.matmul(o[:, T:T + P], XN[:, x.par, c, i * P:(i + 1) * P], t.gather[:, c, :],
                                       start=(c == 0), stop=(c == NT - 1), skip_group_check=True)
                    mm.then_inc(ready["xt"].sem, 1)
                return step

            def project(stage, i):
                w, width = (wa["k"], TL) if stage == "ak" else (wa["q"], T)

                def step(x):
                    pe.wait_ge(free["xt"].sem, free["xt"].upto(x))
                    ring.wait(pe, stage, i, x, ("xt",))
                    mm = product(pe, ring.bank(stage, i)[:, 0:width],
                                 [(w[:, :, kc, i * P:(i + 1) * P], XT[:, :, kc, 0:width]) for kc in range(2)],
                                 True, True)
                    mm.then_inc(ready[stage].sem, 1)
                return step

            def v(i):
                def step(x):
                    ring.wait(pe, "v", i, x)
                    mm = product(pe, ring.bank("v", i)[:, 0:M],
                                 [(XT[:, :, kc, i * P:(i + 1) * P], wa["v"][:, :, kc, :]) for kc in range(2)],
                                 True, True)
                    mm.then_inc(ready["v"].sem, 1)
                return step

            def distance(stage, i):
                src, sq, width, made = (KT, KS, TL, "ak") if stage == "ck" else (QT, QS, T, "aq")

                def step(x):
                    pe.wait_ge(free[made].sem, free[made].upto(x))
                    pe.wait_ge(ll_made.sem, ll_made.upto(x))
                    ring.wait(pe, stage, i, x, (made,))
                    o = ring.bank(stage, i)[:, 0:width]
                    product(pe, o, [(LL[:, :, i, :], src[:, :, i // CPO, 0:width])], True, False)
                    pe.wait_ge(square_low[made].sem, square_low[made].upto(x, i // CPO))
                    pe.matmul(o, BD[:, i % CPO, :], sq[:, 0, i // CPO, 0:width], start=False, stop=False)
                    pe.matmul(o, BD[:, i % CPO, :], sq[:, 1, i // CPO, 0:width], start=False, stop=True)\
                        .then_inc(ready[stage].sem, 1)
                return step

            def turned(i):
                c, b = i // TB, i % TB

                def step(x):
                    pe.wait_ge(pk_made.sem, pk_made.upto(x))
                    ring.wait(pe, "t", i, x)
                    for n in range(TW // P):
                        mm = pe.transpose(ring.bank("t", i)[:, n * P:(n + 1) * P],
                                          PK[:, x.par, b * (TW // P) + n, c * P:(c + 1) * P], t.ident[:, :])
                    mm.then_inc(ready["t"].sem, 1)
                return step

            def z(i):
                def step(x):
                    pe.wait_ge(free["t"].sem, free["t"].upto(x))
                    pe.wait_ge(free["v"].sem, free["v"].upto(x))
                    ring.wait(pe, "z", i, x, ("v", "t",))
                    for n in range(CZ):
                        c = i * CZ + n
                        for k in range(NT):
                            mm = pe.matmul(ring.bank("z", i)[:, n * hpc * R:(n + 1) * hpc * R],
                                           PN[:, k, c * P:(c + 1) * P],
                                           VA[:, x.par, k, c * hpc:(c + 1) * hpc, :].rearrange("p h r -> p (h r)"),
                                           start=(k == 0), stop=(k == NT - 1), skip_group_check=True)
                    mm.then_inc(ready["z"].sem, 1)
                return step

            step_of = {"kv": kv, "q": q, "h": h, "xt": xt, "v": v, "t": turned, "z": z,
                       "den": lambda i: mix("den", 0), "num": lambda i: mix("num", 1)}
            step_of |= {s: (lambda i, s=s: project(s, i)) for s in ("ak", "aq")}
            step_of |= {s: (lambda i, s=s: distance(s, i)) for s in ("ck", "cq")}
            pipeline(pe, [(skew, step_of[stage](i)) for stage, i, skew in order], peel=6)

        @block.scalar
        def _(act):
            def exp_k(x):
                for i in range(2):
                    act.wait_ge(ready["kv"].sem, ready["kv"].upto(x, i))
                    if x.follows(2):
                        act.wait_ge(ready["num"].sem, ready["num"].upto(x, back=2))
                    act.activation(EK[:, x.par, i, 0, :], ring.bank("kv", i)[:, 0:M], ACT.Exp).then_inc(ek_made.sem, 1)

            def exp_q(x):
                act.wait_ge(ready["q"].sem, ready["q"].upto(x))
                if x.follows(2):
                    act.wait_ge(free["den"].sem, free["den"].upto(x, back=2))
                act.activation(EQ[:, x.par, :, :].rearrange("p a l -> p (a l)"), ring.bank("q")[:, :], ACT.Exp,
                               scale=-1.0).then_inc(free["q"].sem, 1)

            def norm1(x):
                act.wait_ge(rs_made.sem, rs_made.upto(x))
                if x.follows(1):
                    act.wait_ge(hg_made.sem, hg_made.upto(x, back=1))
                for i in range(2):
                    act.activation(H0[:, i, :], ring.bank("h")[:, i * M:(i + 1) * M], ACT.Identity,
                                   bias=RS[:, 1, i:i + 1], scale=RS[:, 0, i:i + 1]).then_inc(h0_made.sem, 1)

            def norm2(x):
                act.wait_ge(rs_made.sem, rs_made.upto(x, back=-1))
                if x.follows(2):
                    act.wait_ge(ready["xt"].sem, ready["xt"].upto(x, back=2))
                for i in range(NT):
                    act.activation(XN[:, x.par, i, :], H[:, x.par, i, :], ACT.Identity,
                                   bias=RS[:, 1, 2 + i:3 + i], scale=RS[:, 0, 2 + i:3 + i]).then_inc(xn_made.sem, 1)

            def take_xt(x):
                for i in range(2):
                    act.wait_ge(ready["xt"].sem, ready["xt"].upto(x, i))
                    if x.follows(1):
                        act.wait_ge(ready["v"].sem, ready["v"].upto(x, back=1))
                    act.activation(XT[:, 0, i, :], ring.bank("xt", i)[:, 0:TL], ACT.Copy).then_inc(xt_high.sem, 1)

            def take(stage):
                dst, whole, square = (KT, KW, KS) if stage == "ak" else (QT, QW, QS)
                bias, width, used = (ba["k"], TL, "ck") if stage == "ak" else (ba["q"], T, "cq")

                def step(x):
                    for i in range(2):
                        act.wait_ge(ready[stage].sem, ready[stage].upto(x, i))
                        if x.follows(1):
                            act.wait_ge(ready[used].sem, ready[used].upto(x, back=1))
                        if x.follows(1):
                            act.wait_ge(ll_made.sem, ll_made.upto(x, back=1))
                        if x.follows(1):
                            act.wait_ge(square_low[stage].sem, square_low[stage].upto(x, back=1))
                        src = ring.bank(stage, i)[:, 0:width]
                        act.activation(dst[:, 0, i, :], src, ACT.Identity, bias=bias[:, i:i + 1])\
                            .then_inc(high[stage].sem, 1)
                        act.activation(whole[:, i, :], src, ACT.Square, bias=bias[:, i:i + 1])
                        act.activation(square[:, 0, i, :], src, ACT.Square, bias=bias[:, i:i + 1])\
                            .then_inc(square_high[stage].sem, 1)
                return step

            def kernels_k(x):
                for i in range(CH):
                    act.wait_ge(free["ck"].sem, free["ck"].upto(x, i))
                    if x.follows(2):
                        act.wait_ge(ready["t"].sem, ready["t"].upto(x, back=2))
                    if x.follows(2):
                        act.wait_ge(w0_made.sem, w0_made.upto(x, back=2))
                    act.activation(PK[:, x.par, i, :], CK[:, i % 2, :], ACT.Exp, scale=t.rate[:, 0:1])\
                        .then_inc(pk_made.sem, 1)

            def kernels_q(x):
                for i in range(CH):
                    act.wait_ge(free["cq"].sem, free["cq"].upto(x, i))
                    if x.follows(2):
                        act.wait_ge(pq_stored[x.par], dma_count(x, back=2))
                    act.activation(PQ[:, x.par, i, :], CK[:, i % 2, 0:T], ACT.Exp, scale=t.rate[:, 0:1])\
                        .then_inc(pq_made.sem, 1)

            if CH == 2:
                pipeline(act, [(0, exp_k), (0, exp_q), (2, norm2), (3, kernels_k), (1, norm1), (2, take_xt),
                               (3, kernels_q), (2, take("ak")), (2, take("aq"))], peel=6)
            else:
                pipeline(act, [(0, exp_k), (0, exp_q), (2, norm2), (1, norm1), (3, kernels_q), (2, take_xt),
                               (2, take("ak")), (2, take("aq")), (2, kernels_k)], peel=6)

        @block.gpsimd
        def _(po):
            def affine(x):
                if x.follows(2):
                    po.wait_ge(xn_made.sem, xn_made.upto(x, back=2))
                if x.follows(2):
                    po.wait_ge(h_stored[x.par], dma_count(x, back=2))
                for i in range(2):
                    po.wait_ge(h0_made.sem, h0_made.upto(x, i))
                    po.tensor_tensor(H[:, x.par, i, :], H0[:, i, :], ln_g[:, :], ALU.mult).then_inc(hg_made.sem, 1)
                for i in range(2):
                    po.wait_ge(hg_made.sem, hg_made.upto(x, i))
                    if i == 1:
                        po.wait_ge(txt_loaded[x.par], dma_count(x))
                    po.tensor_tensor(H[:, x.par, i, :], H[:, x.par, i, :], ln_b[:, :], ALU.add).then_inc(h_made.sem, 1)

            def system(x):
                po.wait_ge(pk_made.sem, pk_made.upto(x))
                if x.follows(2):
                    po.wait_ge(w_stored[x.par], dma_count(x, back=2))
                po.tensor_tensor(W[:, x.par, :, :], PK[:, x.par, :, T:TL],
                                 t.reg[:, 1:2].unsqueeze(1).broadcast_to([P, CH, slots]), ALU.mult)\
                    .then_inc(w0_made.sem, 1)
                po.wait_ge(w0_made.sem, w0_made.upto(x))
                po.tensor_tensor(W[:, x.par, :, :], W[:, x.par, :, :],
                                 t.regd[:, :].unsqueeze(1).broadcast_to([P, CH, slots]), ALU.add).then_inc(w_made.sem, 1)

            def low_square(stage):
                whole, square, used = (KW, KS, "ck") if stage == "ak" else (QW, QS, "cq")

                def step(x):
                    for i in range(2):
                        po.wait_ge(square_high[stage].sem, square_high[stage].upto(x, i))
                        if x.follows(1):
                            po.wait_ge(ready[used].sem, ready[used].upto(x, back=1))
                        po.tensor_tensor(square[:, 1, i, :], whole[:, i, :], square[:, 0, i, :], ALU.subtract)\
                            .then_inc(square_low[stage].sem, 1)
                return step

            pipeline(po, [(1, affine), (3, system), (2, low_square("ak")), (2, low_square("aq"))], peel=6)

        @block.vector
        def _(ve):
            def v_exp_k(i):
                def step(x):
                    ve.wait_ge(ek_made.sem, ek_made.upto(x, i))
                    if x.follows(2):
                        ve.wait_ge(ready["num"].sem, ready["num"].upto(x, back=2))
                    ve.tensor_tensor(EK[:, x.par, i, 1, :], EK[:, x.par, i, 0, :], ring.bank("kv", i)[:, M:2 * M],
                                     ALU.mult).then_inc(free["kv"].sem, 1)
                return step

            def denominator(x):
                ve.wait_ge(ready["den"].sem, ready["den"].upto(x))
                ve.wait_ge(free["q"].sem, free["q"].upto(x))
                if x.follows(1):
                    ve.wait_ge(free["num"].sem, free["num"].upto(x, back=1))
                ve.scalar_tensor_tensor(out=DE[:, :, :], in0=EQ[:, x.par, :, :], scalar=1.0,
                                        in1=ring.bank("den")[:, :].rearrange("p (a l) -> p a l", a=2),
                                        op0=ALU.add, op1=ALU.mult).then_inc(free["den"].sem, 1)

            def inverse(i):
                def step(x):
                    ve.wait_ge(free["den"].sem, free["den"].upto(x))
                    ve.reciprocal(DE[:, i, :], DE[:, i, :]).then_inc(de_made.sem, 1)
                return step

            def y(x):
                ve.wait_ge(de_made.sem, de_made.upto(x))
                ve.wait_ge(ready["num"].sem, ready["num"].upto(x))
                if x.follows(2):
                    ve.wait_ge(ready["h"].sem, ready["h"].upto(x, back=2))
                ve.tensor_tensor(YT[:, x.par, :, :], DE[:, :, :],
                                 ring.bank("num")[:, :].rearrange("p (a l) -> p a l", a=2), ALU.mult)\
                    .then_inc(free["num"].sem, 1)

            def stats_before(x):
                if isinstance(x.s, int) and x.s == 0:
                    return
                if x.follows(1):
                    ve.wait_ge(h_made.sem, h_made.upto(x, back=1))
                for i in range(NT):
                    ve.bn_stats(ST[:, 2 + i, :], H[:, 1 - x.par, i, :]).then_inc(stat2.sem, 1)

            def stats(part):
                def step(x):
                    if part == 0:
                        if not (isinstance(x.s, int) and x.s == N):
                            ve.wait_ge(ready["h"].sem, ready["h"].upto(x))
                            for i in range(2):
                                ve.bn_stats(ST[:, i, :], ring.bank("h")[:, i * M:(i + 1) * M])\
                                    .then_inc(stat1.sem, 1)
                            ve.wait_ge(stat1.sem, stat1.upto(x))
                        if x.follows(1):
                            ve.wait_ge(stat2.sem, stat2.upto(x, back=1))
                        if x.follows(1):
                            ve.wait_ge(free["h"].sem, free["h"].upto(x, back=1))
                        if x.follows(2):
                            ve.wait_ge(xn_made.sem, xn_made.upto(x, back=2))
                    inverse_deviation(ve, x, ST, RS, rs_made, part)
                return step

            def low_xt(x):
                for i in range(2):
                    ve.wait_ge(xt_high.sem, xt_high.upto(x, i))
                    if x.follows(1):
                        ve.wait_ge(ready["v"].sem, ready["v"].upto(x, back=1))
                    ve.tensor_tensor(XT[:, 1, i, :], ring.bank("xt", i)[:, 0:TL], XT[:, 0, i, :], ALU.subtract)\
                        .then_inc(free["xt"].sem, 1)

            def low(stage):
                dst, bias, width, used = (KT, ba["k"], TL, "ck") if stage == "ak" else (QT, ba["q"], T, "cq")

                def step(x):
                    for i in range(2):
                        ve.wait_ge(high[stage].sem, high[stage].upto(x, i))
                        ve.wait_ge(square_high[stage].sem, square_high[stage].upto(x, i))
                        if x.follows(1):
                            ve.wait_ge(ready[used].sem, ready[used].upto(x, back=1))
                        ve.scalar_tensor_tensor(out=dst[:, 1, i, :], in0=ring.bank(stage, i)[:, 0:width],
                                                scalar=bias[:, i:i + 1], in1=dst[:, 0, i, :],
                                                op0=ALU.add, op1=ALU.subtract).then_inc(free[stage].sem, 1)
                return step

            def landmarks(x):
                ve.wait_ge(free["ak"].sem, free["ak"].upto(x))
                if x.follows(1):
                    ve.wait_ge(ready["cq"].sem, ready["cq"].upto(x, back=1))
                for u in range(2):
                    for i in range(CH):
                        ve.scalar_tensor_tensor(
                            out=LL[:, u, i, :].rearrange("p (h k) -> p h k", h=hpc),
                            in0=KT[:, u, i // CPO, T:TL].unsqueeze(1).broadcast_to([P, hpc, slots]), scalar=-2.0,
                            in1=t.bd[:, i % CPO, :].rearrange("p (h k) -> p h k", h=hpc),
                            op0=ALU.mult, op1=ALU.mult).then_inc(ll_made.sem, 1)

            def take_v(i):
                def step(x):
                    ve.wait_ge(ready["v"].sem, ready["v"].upto(x, i))
                    if x.follows(2):
                        ve.wait_ge(ready["z"].sem, ready["z"].upto(x, back=2))
                    ve.tensor_tensor(VA[:, x.par, i, :, 0:DA],
                                     ring.bank("v", i)[:, 0:M].rearrange("p (h d) -> p h d", h=HA),
                                     bv[:, :].rearrange("p (h d) -> p h d", h=HA), ALU.add).then_inc(free["v"].sem, 1)
                return step

            def clamp(stage):
                width = TL if stage == "ck" else T

                def step(x):
                    for i in range(CH):
                        ve.wait_ge(ready[stage].sem, ready[stage].upto(x, i))
                        if stage == "ck":
                            ve.tensor_tensor_reduce(LD[:, i, :], ring.bank(stage, i)[:, T:TL], t.diag[:, :], 1.0, 0.0,
                                                    ALU.mult, ALU.add, LN[:, i:i + 1]).then_inc(ln_made.sem, 1)
                            ve.wait_ge(ln_made.sem, ln_made.upto(x, i))
                        if i >= 2:
                            made = pk_made if stage == "ck" else pq_made
                            ve.wait_ge(made.sem, made.upto(x, i - 2))
                        elif stage == "ck":
                            if x.follows(1):
                                ve.wait_ge(pq_made.sem, pq_made.upto(x, CH - 2 + i, back=1))
                        else:
                            ve.wait_ge(pk_made.sem, pk_made.upto(x, CH - 2 + i))
                        ve.tensor_scalar(CK[:, i % 2, 0:width], ring.bank(stage, i)[:, 0:width], LN[:, i:i + 1], 0.0,
                                         ALU.subtract, ALU.max).then_inc(free[stage].sem, 1)
                return step

            def take_turned(x):
                for i in range(NT * TB):
                    ve.wait_ge(ready["t"].sem, ready["t"].upto(x, i))
                    if x.follows(1):
                        ve.wait_ge(ready["z"].sem, ready["z"].upto(x, back=1))
                    ve.tensor_copy(PN[:, i // TB, i % TB * TW:(i % TB + 1) * TW], ring.bank("t", i)[:, 0:TW])\
                        .then_inc(free["t"].sem, 1)

            def right_sides(x):
                for i in range(ZB):
                    ve.wait_ge(ready["z"].sem, ready["z"].upto(x, i))
                    if i:
                        ve.wait_ge(zr_made.sem, zr_made.upto(x, i - 1))
                    else:
                        if x.follows(1):
                            ve.wait_ge(zr_made.sem, zr_made.upto(x, back=1))
                    ve.tensor_tensor(ZM[:, :, :, :],
                                     ring.bank("z", i)[:, 0:CZ * hpc * R].rearrange("p (c h r) -> p c h r", c=CZ, h=hpc),
                                     t.bz[:, :, :].unsqueeze(1).broadcast_to([P, CZ, hpc, R]), ALU.mult)\
                        .then_inc(free["z"].sem, 1)
                    ve.wait_ge(free["z"].sem, free["z"].upto(x, i))
                    if x.follows(2):
                        ve.wait_ge(z_stored[x.par], dma_count(x, back=2))
                    own = Z[:, x.par, i * CZ:(i + 1) * CZ, :]
                    ve.tensor_reduce(own, ZM[:, :, :, :].rearrange("p c h r -> p c r h"), AX_X, ALU.add)\
                        .then_inc(zr_made.sem, 1)
                    ve.wait_ge(zr_made.sem, zr_made.upto(x, i))
                    ve.tensor_scalar(own, own, t.reg[:, 1:2], None, ALU.mult).then_inc(z_made.sem, 1)

            after, at_once = ([(3, clamp("ck"))], []) if CH == 2 else ([], [(2, clamp("ck"))])
            pipeline(ve, [(0, v_exp_k(0)), (0, v_exp_k(1)), (1, stats(2), 1)] + after + [
                (0, denominator), (3, clamp("cq")), (3, take_turned), (2, low_xt), (0, inverse(0)),
                (0, inverse(1)), (0, y), (0, stats_before, 1), (2, low("ak")), (3, right_sides),
                (2, landmarks), (2, low("aq")), (2, take_v(0)), (2, take_v(1)), (2, take_v(2)),
                (0, stats(0), 1), (0, stats(1), 1)] + at_once, peel=6)


def solve_phase(nc, ins, t, slots, spill):
    GB = N * HA // P if slots == SMALL else 1
    TURNS = N * HA // P // GB
    HALVES = 2 if GB % 2 == 0 else 1
    GH = GB // HALVES
    halves = [slice(h * GH, (h + 1) * GH) for h in range(HALVES)]
    rows = slots + R
    sfx = f"_{slots}"
    with ExitStack() as ctx, nc.Block() as block:
        def sb(name, shape, dt=F32):
            return ctx.enter_context(nc.sbuf_tensor("s_" + name + sfx, shape, dt))

        def sem(name):
            return t.semaphore("s_" + name)

        A = sb("a", [P, GB, rows, slots])
        ZL = sb("zl", [P, GB, slots, R])
        YO = sb("yo", [P, GB, slots, R])
        DI = sb("di", [P, GB, slots])
        ROW = sb("row", [P, GB, slots])
        PR = sb("pr", [P, GB, rows, slots]) if slots == SMALL else \
            sb("pr", [P, GB, (rows + 1) * (rows + 1) // 4])
        RD = sb("rd", [P, GB, rows])
        loaded = sem("loaded")
        moved = sem("moved")
        stored = sem("stored")
        link_sems = [sem(f"step{h}") for h in range(HALVES)]
        idle(block, "tensor")

        def part(g, m, j):
            if slots == SMALL:
                return PR[:, g, 0:m, 0:j]
            return PR[:, g, 0:m * j].rearrange("p g (m j) -> p g m j", j=j)

        wo = sb("wo", [P, 2, M])
        w1 = sb("w1", [P, 2, F])
        w2 = sb("w2", [P, FC, M + GE])
        lora_b = sb("lora_b", [3 * G3, F + M])
        weights = sem("weights")
        high = sem("high")
        low_made = sem("low_made")
        loads = [(w1[:, :, :], ins["w1"]), (w2[:, :, :], ins["w2"]), (wo[:, :, :], ins["wo"]),
                 (lora_b[:, :], ins["lora_b"]), (t.bo[:, :], ins["bo"].broadcast_to([P, M])),
                 (t.r1[:, :, :], ins["r1"])]
        splits = [(w1[:, :, :], t.w1[:, 0, :, :], t.w1[:, 1, :, :]), (w2[:, :, :], t.w2[:, 0, :, :], t.w2[:, 1, :, :]),
                  (wo[:, :, :], t.wo[:, 0, :, :], t.wo[:, 1, :, :])]
        STEPS = 9 * slots - 6
        w_sys = spill.w.rearrange("(g p k) j -> p g (k j)", p=P, k=slots)
        z_sys = spill.z.rearrange("(g p k) r -> p g (k r)", p=P, k=slots)
        y_sys = spill.y.rearrange("(g p k) r -> p g (k r)", p=P, k=slots)

        @block.sync
        def _(sy):
            def load(turn):
                sy.dma_start(A[:, :, 0:slots, :].rearrange("p g k j -> p g (k j)"),
                             w_sys[:, bass.ds(turn * GB, GB), :]).then_inc(loaded, 16)
                sy.dma_start(ZL[:, :, :, :].rearrange("p g k r -> p g (k r)"),
                             z_sys[:, bass.ds(turn * GB, GB), :]).then_inc(loaded, 16)

            def store(turn):
                sy.wait_ge(moved, turn * HALVES + HALVES)
                sy.dma_start(y_sys[:, bass.ds(turn * GB, GB), :],
                             YO[:, :, :, :].rearrange("p g k r -> p g (k r)")).then_inc(stored, 16)

            load(0)
            for dst, src in loads:
                sy.dma_start(dst, src).then_inc(weights, 16)
            store(0)
            if TURNS > 1:
                with sy.Fori(1, TURNS) as turn:
                    sy.wait_ge(stored, turn * 16)
                    load(turn)
                    store(turn)
            sy.wait_ge(stored, TURNS * 16)

        @block.scalar
        def _(act):
            act.wait_ge(weights, 16 * len(loads))
            for whole, hi, lo in splits:
                act.activation(hi, whole, ACT.Copy).then_inc(high, 1)
            act.activation(t.lora_b[:, :], lora_b[:, :], ACT.Copy).then_inc(high, 1)

        @block.gpsimd
        def _(po):
            for n, (whole, hi, lo) in enumerate(splits):
                po.wait_ge(high, n + 1)
                po.tensor_tensor(lo, whole, hi, ALU.subtract).then_inc(low_made, 1)
                po.wait_ge(low_made, n + 1)
            po.wait_ge(high, len(splits) + 1)
            low = slice(G3, 2 * G3)
            po.tensor_tensor(t.lora_b[low, :], lora_b[low, :], t.lora_b[low, :], ALU.subtract)

        @block.vector
        def _(ve):
            def batch(turn):
                n = [0] * HALVES

                def follow(h):
                    if n[h]:
                        ve.wait_ge(link_sems[h], turn * STEPS + n[h])
                    n[h] += 1
                    return ve

                ve.wait_ge(loaded, turn * 32 + 32)
                for h, g in enumerate(halves):
                    follow(h).tensor_copy(A[:, g, slots:rows, :], ZL[:, g, :, :].rearrange("p g k r -> p g r k"))\
                        .then_inc(link_sems[h], 1)
                for j in range(slots):
                    m = rows - j
                    if j:
                        for h, g in enumerate(halves):
                            follow(h).tensor_tensor(ROW[:, g, 0:j], A[:, g, j, 0:j], DI[:, g, 0:j], ALU.mult)\
                                .then_inc(link_sems[h], 1)
                        for h, g in enumerate(halves):
                            follow(h).tensor_tensor(part(g, m, j), A[:, g, j:rows, 0:j],
                                                    ROW[:, g, 0:j].unsqueeze(2).broadcast_to([P, GH, m, j]), ALU.mult)\
                                .then_inc(link_sems[h], 1)
                        for h, g in enumerate(halves):
                            follow(h).tensor_reduce(RD[:, g, 0:m], part(g, m, j), AX_X, ALU.add)\
                                .then_inc(link_sems[h], 1)
                        for h, g in enumerate(halves):
                            follow(h).tensor_tensor(A[:, g, j:rows, j], A[:, g, j:rows, j], RD[:, g, 0:m],
                                                    ALU.subtract).then_inc(link_sems[h], 1)
                    for h, g in enumerate(halves):
                        follow(h).reciprocal(DI[:, g, j:j + 1], A[:, g, j, j:j + 1]).then_inc(link_sems[h], 1)
                for i in reversed(range(slots)):
                    m = slots - 1 - i
                    if m:
                        for h, g in enumerate(halves):
                            follow(h).tensor_tensor(part(g, R, m), A[:, g, slots:rows, i + 1:slots],
                                                    A[:, g, i + 1:slots, i].unsqueeze(2).broadcast_to([P, GH, R, m]),
                                                    ALU.mult).then_inc(link_sems[h], 1)
                        for h, g in enumerate(halves):
                            follow(h).tensor_reduce(RD[:, g, 0:R], part(g, R, m), AX_X, ALU.add)\
                                .then_inc(link_sems[h], 1)
                        for h, g in enumerate(halves):
                            follow(h).tensor_tensor(A[:, g, slots:rows, i], A[:, g, slots:rows, i], RD[:, g, 0:R],
                                                    ALU.subtract).then_inc(link_sems[h], 1)
                    for h, g in enumerate(halves):
                        follow(h).tensor_tensor(A[:, g, slots:rows, i], A[:, g, slots:rows, i],
                                                DI[:, g, i:i + 1].broadcast_to([P, GH, R]), ALU.mult)\
                            .then_inc(link_sems[h], 1)
                assert set(n) == {STEPS}, (n, STEPS)
                for h, g in enumerate(halves):
                    ve.wait_ge(link_sems[h], turn * STEPS + STEPS)
                    ve.tensor_copy(YO[:, g, :, :], A[:, g, slots:rows, :].rearrange("p g r k -> p g k r"))\
                        .then_inc(moved, 1)

            if TURNS == 1:
                batch(0)
            else:
                with ve.Fori(0, TURNS) as turn:
                    batch(turn)


def output_phase(nc, ins, out, t, slots, spill):
    hpc = P // slots
    CH = HA // hpc
    sfx = f"_{slots}"
    with ExitStack() as ctx, nc.Block() as block:
        def sb(name, shape, dt=F32):
            return ctx.enter_context(nc.sbuf_tensor("b_" + name + sfx, shape, dt))

        def sem(name):
            return t.semaphore("b_" + name)

        wo, w1, w2, lo_b, bo, r1 = t.wo, t.w1, t.w2, t.lora_b, t.bo, t.r1
        PQ = sb("pq", [P, 2, CH, T])
        YL = sb("yl", [P, 2, CH, R])
        YY = sb("yy", [P, 2, CH, hpc, R])
        NM = sb("nm", [P, NT, HA])
        NR = sb("nr", [P, NT, HA])
        O = sb("o", [P, NT, M])
        OT = sb("ot", [P, 2, 2, T], FR)
        H = sb("h", [P, 2, NT, M])
        H2 = sb("h2", [P, 2, NT, M])
        ST, RS = sb("st", [P, NT, 6]), sb("rs", [P, 6, NT])
        XN = sb("xn", [P, NT, M])
        XF = sb("xf", [P, 2, T])
        XT = sb("xt", [P, 2, 2, 2, T], FR)
        HID = sb("hid", [P, 2, 2, FC, T], FR)
        gate_buffers = [{n: sb(f"{n}{i}", shape) for n, shape in
                         (("mx", [P, NT]), ("d", [P, NT, E]), ("e", [P, NT, E]), ("sum", [P, NT]),
                          ("rec", [P, NT]), ("gate", [P, NT, E]), ("zg", [P, NT, 3, G3]))} for i in range(2)]
        ZT = [sb(f"zt{i}", [3 * G3, T], FR) for i in range(2)]
        OUT = sb("out", [P, 2, NT, M])

        order = ([("ot", 0, 1), ("ot", 1, 1), ("hid", 0, 2), ("hid", 1, 2), ("g2", 0, 3), ("hid", 2, 2)]
                 + [("w", i, 1) for i in range(NT)] + [("hid", i, 2) for i in range(3, FC)]
                 + [("y", 0, 2), ("xt", 0, 1), ("xt", 1, 1), ("y", 1, 2)] + [("o", i, 0) for i in range(NT)]
                 + [("r", 0, 1), ("y", 2, 2), ("g1", 0, 1)])
        per = {stage: sum(1 for job in order if job[0] == stage) for stage, _, _ in order}
        ready = {s: Signal(sem("ready_" + s), n) for s, n in per.items()}
        free = {s: Signal(sem("free_" + s), n) for s, n in per.items()}
        ring = Ring(order, free, t.banks, own={"y": (5, 6, 7), "g1": (4,)}, shared=range(5))
        ones_set = sem("ones_set")
        pq_loaded = [sem(f"pq_loaded{i}") for i in range(2)]
        y_loaded = [sem(f"y_loaded{i}") for i in range(2)]
        h_loaded = [sem(f"h_loaded{i}") for i in range(2)]
        out_stored = [sem(f"out_stored{i}") for i in range(2)]
        yy_made = Signal(sem("yy_made"), 1)
        hb_made = Signal(sem("hb_made"), 1)
        norm_made = Signal(sem("norm_made"), 2 * NT)
        stat = Signal(sem("stat"), NT)
        rs_made = Signal(sem("rs_made"), RSQRT_STEPS)
        xn_made = Signal(sem("xn_made"), NT)
        ot_high = Signal(sem("ot_high"), 2)
        xf_made = Signal(sem("xf_made"), 2)
        xt_high = Signal(sem("xt_high"), 2)
        hid_high = Signal(sem("hid_high"), FC)
        zt_high = [Signal(sem(f"zt_high{i}"), 1) for i in range(2)]
        lora_added = Signal(sem("lora_added"), NT)
        logits = [Signal(sem("logits0"), 2), Signal(sem("logits1"), 2 * NT)]
        exps = [Signal(sem(f"exps{i}"), 1) for i in range(2)]
        gates = [Signal(sem(f"gates{i}"), 3) for i in range(2)]
        gated = [free["r"], Signal(sem("gated1"), NT)]

        @block.sync
        def _(sy):
            def load(x):
                if x.follows(2):
                    sy.wait_ge(yy_made.sem, yy_made.upto(x, back=2))
                sy.dma_start(YL[:, x.par, :, :],
                             spill.y[bass.ds(x.s * (HA * slots), HA * slots), :].rearrange("(q p) r -> p q r", p=P))\
                    .then_inc(y_loaded[x.par], 16)
                if x.follows(2):
                    sy.wait_ge(ready["o"].sem, ready["o"].upto(x, back=2))
                sy.dma_start(PQ[:, x.par, :, :].rearrange("p c m -> p (c m)"),
                             spill.pq[bass.ds(x.s, 1)].rearrange("n p k -> p (n k)")).then_inc(pq_loaded[x.par], 16)
                if x.follows(2):
                    sy.wait_ge(free["w"].sem, free["w"].upto(x, back=2))
                sy.dma_start(H[:, x.par, :, :].rearrange("p c m -> p (c m)"),
                             spill.h[bass.ds(x.s, 1)].rearrange("n p k -> p (n k)")).then_inc(h_loaded[x.par], 16)

            def store(x):
                sy.wait_ge(free["y"].sem, free["y"].upto(x))
                sy.dma_start(out[bass.ds(x.s, 1)].rearrange("n (c p) m -> p (n c) m", p=P), OUT[:, x.par, :, :])\
                    .then_inc(out_stored[x.par], 16)

            pipeline(sy, [(3, store), (0, load)], peel=6)
            for i in range(2):
                sy.wait_ge(out_stored[i], 16 * N // 2)

        @block.tensor
        def _(pe):
            def o(i):
                def step(x):
                    pe.wait_ge(pq_loaded[x.par], dma_count(x))
                    pe.wait_ge(yy_made.sem, yy_made.upto(x))
                    ring.wait(pe, "o", i, x)
                    for c in range(CH):
                        mm = pe.matmul(ring.bank("o", i)[:, c * hpc * R:(c + 1) * hpc * R],
                                       PQ[:, x.par, c, i * P:(i + 1) * P],
                                       YY[:, x.par, c, :, :].rearrange("p h r -> p (h r)"), start=True, stop=True,
                                       skip_group_check=True)
                    mm.then_inc(ready["o"].sem, 1)
                return step

            def turn(stage, i, src, made):
                def step(x):
                    pe.wait_ge(made.sem, made.upto(x))
                    ring.wait(pe, stage, i, x)
                    for c in range(NT):
                        mm = pe.transpose(ring.bank(stage, i)[:, c * P:(c + 1) * P], src[:, c, i * P:(i + 1) * P],
                                          t.ident[:, :])
                    mm.then_inc(ready[stage].sem, 1)
                return step

            def w(i):
                def step(x):
                    pe.wait_ge(free["ot"].sem, free["ot"].upto(x))
                    ring.wait(pe, "w", i, x, ("ot",))
                    mm = product(pe, ring.bank("w", i)[:, 0:M],
                                 [(OT[:, :, kc, i * P:(i + 1) * P], wo[:, :, kc, :]) for kc in range(2)], True, True)
                    mm.then_inc(ready["w"].sem, 1)
                return step

            def r(i):
                def step(x):
                    pe.wait_ge(free["xt"].sem, free["xt"].upto(x))
                    ring.wait(pe, "r", i, x, ("xt",))
                    for c in range(NT):
                        for kc in range(2):
                            mm = pe.matmul(ring.bank("r")[:, c * P:(c + 1) * P],
                                           XF[:, kc, c * P:(c + 1) * P], r1[:, kc, :],
                                           start=(kc == 0), stop=(kc == 1), skip_group_check=True)
                    mm.then_inc(ready["r"].sem, 1)
                return step

            def g(n):
                stage = ("g1", "g2")[n]

                def step(x):
                    pe.wait_ge(gated[n].sem, gated[n].upto(x))
                    ring.wait(pe, stage, 0, x)
                    for c in range(NT):
                        mm = pe.transpose(ring.bank(stage)[0:3 * G3, c * P:(c + 1) * P],
                                          gate_buffers[n]["zg"][:, c, :, :].rearrange("p u g -> p (u g)"),
                                          t.ident[:, :])
                    mm.then_inc(ready[stage].sem, 1)
                return step

            def hid(i):
                def step(x):
                    pe.wait_ge(free["xt"].sem, free["xt"].upto(x))
                    ring.wait(pe, "hid", i, x, ("xt",))
                    own = slice(i * P, (i + 1) * P)
                    product(pe, ring.bank("hid", i)[:, 0:T],
                            [(w1[:, :, kc, own], XT[:, x.par, :, kc, :]) for kc in range(2)], True, False)
                    pe.wait_ge(free["g1"].sem, free["g1"].upto(x))
                    pe.matmul(ring.bank("hid", i)[:, 0:T], lo_b[:, own], ZT[0][:, :], start=False, stop=True)\
                        .then_inc(ready["hid"].sem, 1)
                return step

            def y(i):
                def step(x):
                    ring.wait(pe, "y", i, x)
                    for f in range(FC):
                        if i == 0:
                            pe.wait_ge(free["hid"].sem, free["hid"].upto(x, f))
                        mm = product(pe, ring.bank("y", i)[:, 0:M + GE],
                                     [(HID[:, x.par, :, f, i * P:(i + 1) * P], w2[:, :, f, :])],
                                     f == 0, f == FC - 1)
                    mm.then_inc(ready["y"].sem, 1)
                return step

            def lora(x):
                pe.wait_ge(free["g2"].sem, free["g2"].upto(x))
                for i in range(NT):
                    pe.matmul(ring.bank("y", i)[:, 0:M], ZT[1][:, i * P:(i + 1) * P], lo_b[:, F:F + M], start=False,
                              stop=True, skip_group_check=True).then_inc(lora_added.sem, 1)

            step_of = {"o": o, "ot": lambda i: turn("ot", i, O, free["o"]), "w": w,
                       "xt": lambda i: turn("xt", i, XN, xn_made), "r": r, "y": y,
                       "g1": lambda i: g(0), "g2": lambda i: g(1), "hid": hid}
            stages = [(skew, step_of[stage](i)) for stage, i, skew in order]
            stages.insert(7, (3, lora))
            pipeline(pe, stages, peel=6)

        @block.scalar
        def _(act):
            def take_g(n):
                def step(x):
                    stage = ("g1", "g2")[n]
                    act.wait_ge(ready[stage].sem, ready[stage].upto(x))
                    if x.follows(1):
                        used = (ready["hid"], lora_added)[n]
                        act.wait_ge(used.sem, used.upto(x, back=1))
                    act.activation(ZT[n][:, :], ring.bank(stage)[0:3 * G3, 0:T], ACT.Copy).then_inc(zt_high[n].sem, 1)
                return step

            def take_ot(x):
                for i in range(2):
                    act.wait_ge(ready["ot"].sem, ready["ot"].upto(x, i))
                    if x.follows(1):
                        act.wait_ge(ready["w"].sem, ready["w"].upto(x, back=1))
                    act.activation(OT[:, 0, i, :], ring.bank("ot", i)[:, 0:T], ACT.Copy).then_inc(ot_high.sem, 1)

            def take_xt(x):
                for i in range(2):
                    act.wait_ge(ready["xt"].sem, ready["xt"].upto(x, i))
                    if x.follows(2):
                        act.wait_ge(ready["hid"].sem, ready["hid"].upto(x, back=2))
                    act.activation(XT[:, x.par, 0, i, :], ring.bank("xt", i)[:, 0:T], ACT.Copy)\
                        .then_inc(xt_high.sem, 1)
                for i in range(2):
                    if x.follows(1):
                        act.wait_ge(ready["r"].sem, ready["r"].upto(x, back=1))
                    act.activation(XF[:, i, :], ring.bank("xt", i)[:, 0:T], ACT.Copy).then_inc(xf_made.sem, 1)

            def relu(i):
                def step(x):
                    act.wait_ge(ready["hid"].sem, ready["hid"].upto(x, i))
                    if x.follows(2):
                        act.wait_ge(ready["y"].sem, ready["y"].upto(x, back=2))
                    act.activation(HID[:, x.par, 0, i, :], ring.bank("hid", i)[:, 0:T], ACT.Relu)\
                        .then_inc(hid_high.sem, 1)
                return step

            def norm(x):
                act.wait_ge(rs_made.sem, rs_made.upto(x))
                if x.follows(1):
                    act.wait_ge(ready["xt"].sem, ready["xt"].upto(x, back=1))
                for i in range(NT):
                    act.activation(XN[:, i, :], H2[:, x.par, i, :], ACT.Identity, bias=RS[:, 1, i:i + 1],
                                   scale=RS[:, 0, i:i + 1]).then_inc(xn_made.sem, 1)

            def exp(n):
                def step(x):
                    b = gate_buffers[n]
                    act.wait_ge(logits[n].sem, logits[n].upto(x))
                    if x.follows(1):
                        act.wait_ge(gates[n].sem, gates[n].upto(x, 2, back=1))
                    act.activation(b["e"][:, :, :], b["d"][:, :, :], ACT.Exp).then_inc(exps[n].sem, 1)
                return step

            pipeline(act, [(1, take_ot), (2, relu(0)), (2, relu(1)), (3, take_g(1)), (2, relu(2)), (2, relu(3)),
                           (2, relu(4)), (2, relu(5)), (2, relu(6)), (2, relu(7)), (1, norm), (1, take_xt),
                           (1, exp(0)), (1, take_g(0)), (2, exp(1))], peel=6)

        @block.gpsimd
        def _(po):
            for n in range(2):
                po.memset(gate_buffers[n]["zg"][:, :, :, ER + 1:G3], 0.0).then_inc(ones_set, 1)
                po.memset(gate_buffers[n]["zg"][:, :, :, ER:ER + 1], 1.0).then_inc(ones_set, 1)
            def spread(x):
                po.wait_ge(y_loaded[x.par], dma_count(x))
                if x.follows(2):
                    po.wait_ge(ready["o"].sem, ready["o"].upto(x, back=2))
                po.tensor_tensor(YY[:, x.par, :, :, :], YL[:, x.par, :, :].unsqueeze(2).broadcast_to([P, CH, hpc, R]),
                                 t.bz[:, :, :].unsqueeze(1).broadcast_to([P, CH, hpc, R]), ALU.mult)\
                    .then_inc(yy_made.sem, 1)

            def add_bias(x):
                po.wait_ge(h_loaded[x.par], dma_count(x))
                po.tensor_tensor(H[:, x.par, :, :], H[:, x.par, :, :], bo[:, :].unsqueeze(1).broadcast_to([P, NT, M]),
                                 ALU.add).then_inc(hb_made.sem, 1)

            pipeline(po, [(0, spread), (0, add_bias)], peel=6)

        @block.vector
        def _(ve):
            ve.wait_ge(ones_set, 4)

            def divide(i):
                def step(x):
                    ve.wait_ge(ready["o"].sem, ready["o"].upto(x, i))
                    b = ring.bank("o", i)[:, 0:HA * R].rearrange("p (h r) -> p h r", h=HA)
                    ve.tensor_scalar(NM[:, i, :], b[:, :, DA], 1e-10, None, ALU.max).then_inc(norm_made.sem, 1)
                    ve.wait_ge(norm_made.sem, norm_made.upto(x, 2 * i))
                    ve.reciprocal(NR[:, i, :], NM[:, i, :]).then_inc(norm_made.sem, 1)
                    ve.wait_ge(norm_made.sem, norm_made.upto(x, 2 * i + 1))
                    if x.follows(1):
                        ve.wait_ge(ready["ot"].sem, ready["ot"].upto(x, back=1))
                    ve.tensor_tensor(O[:, i, :].rearrange("p (h d) -> p h d", h=HA), b[:, :, 0:DA],
                                     NR[:, i, :].unsqueeze(2).broadcast_to([P, HA, DA]), ALU.mult)\
                        .then_inc(free["o"].sem, 1)
                return step

            def finish(x):
                for i in range(NT):
                    ve.wait_ge(lora_added.sem, lora_added.upto(x, i))
                    if x.follows(2):
                        ve.wait_ge(out_stored[x.par], dma_count(x, back=2))
                    ve.tensor_tensor(OUT[:, x.par, i, :], H2[:, x.par, i, :], ring.bank("y", i)[:, 0:M], ALU.add)\
                        .then_inc(free["y"].sem, 1)

            def low_hid(i):
                def step(x):
                    ve.wait_ge(hid_high.sem, hid_high.upto(x, i))
                    if x.follows(2):
                        ve.wait_ge(ready["y"].sem, ready["y"].upto(x, back=2))
                    ve.scalar_tensor_tensor(out=HID[:, x.par, 1, i, :], in0=ring.bank("hid", i)[:, 0:T], scalar=0.0,
                                            in1=HID[:, x.par, 0, i, :], op0=ALU.max, op1=ALU.subtract)\
                        .then_inc(free["hid"].sem, 1)
                return step

            def low_ot(x):
                for i in range(2):
                    ve.wait_ge(ot_high.sem, ot_high.upto(x, i))
                    if x.follows(1):
                        ve.wait_ge(ready["w"].sem, ready["w"].upto(x, back=1))
                    ve.tensor_tensor(OT[:, 1, i, :], ring.bank("ot", i)[:, 0:T], OT[:, 0, i, :], ALU.subtract)\
                        .then_inc(free["ot"].sem, 1)

            def low_xt(x):
                for i in range(2):
                    ve.wait_ge(xf_made.sem, xf_made.upto(x, i))
                    ve.wait_ge(xt_high.sem, xt_high.upto(x, i))
                    if x.follows(2):
                        ve.wait_ge(ready["hid"].sem, ready["hid"].upto(x, back=2))
                    ve.tensor_tensor(XT[:, x.par, 1, i, :], ring.bank("xt", i)[:, 0:T], XT[:, x.par, 0, i, :],
                                     ALU.subtract).then_inc(free["xt"].sem, 1)

            def low_zt(n):
                def step(x):
                    stage = ("g1", "g2")[n]
                    ve.wait_ge(zt_high[n].sem, zt_high[n].upto(x))
                    ve.tensor_tensor(ZT[n][2 * G3:3 * G3, :], ring.bank(stage)[2 * G3:3 * G3, 0:T],
                                     ZT[n][2 * G3:3 * G3, :], ALU.subtract).then_inc(free[stage].sem, 1)
                return step

            def residual(part):
                def step(x):
                    if part == 0:
                        ve.wait_ge(hb_made.sem, hb_made.upto(x))
                        if x.follows(2):
                            ve.wait_ge(free["y"].sem, free["y"].upto(x, back=2))
                        for i in range(NT):
                            ve.wait_ge(ready["w"].sem, ready["w"].upto(x, i))
                            ve.tensor_tensor(H2[:, x.par, i, :], H[:, x.par, i, :], ring.bank("w", i)[:, 0:M],
                                             ALU.add).then_inc(free["w"].sem, 1)
                        for i in range(NT):
                            ve.wait_ge(free["w"].sem, free["w"].upto(x, i))
                            ve.bn_stats(ST[:, i, :], H2[:, x.par, i, :]).then_inc(stat.sem, 1)
                        ve.wait_ge(stat.sem, stat.upto(x))
                        if x.follows(1):
                            ve.wait_ge(xn_made.sem, xn_made.upto(x, back=1))
                    inverse_deviation(ve, x, ST, RS, rs_made, part)
                return step

            def shift(n):
                def step(x):
                    b = gate_buffers[n]
                    if x.follows(1):
                        ve.wait_ge(exps[n].sem, exps[n].upto(x, back=1))
                    if n == 0:
                        ve.wait_ge(ready["r"].sem, ready["r"].upto(x))
                        p = ring.bank("r")[:, 0:NT * P].rearrange("p (c g) -> p c g", c=NT)[:, :, ER:GATED]
                        ve.tensor_reduce(b["mx"][:, :], p, AX_X, ALU.max).then_inc(logits[n].sem, 1)
                        ve.wait_ge(logits[n].sem, logits[n].upto(x, 0))
                        ve.tensor_tensor(b["d"][:, :, :], p, b["mx"][:, :].unsqueeze(2).broadcast_to([P, NT, E]),
                                         ALU.subtract).then_inc(logits[n].sem, 1)
                        return
                    for i in range(NT):
                        ve.wait_ge(ready["y"].sem, ready["y"].upto(x, i))
                        p = ring.bank("y", i)[:, M + ER:M + GATED]
                        ve.tensor_reduce(b["mx"][:, i:i + 1], p, AX_X, ALU.max).then_inc(logits[n].sem, 1)
                        ve.wait_ge(logits[n].sem, logits[n].upto(x, 2 * i))
                        ve.tensor_scalar(b["d"][:, i, :], p, b["mx"][:, i:i + 1], None, ALU.subtract)\
                            .then_inc(logits[n].sem, 1)
                return step

            def gate(n):
                def step(x):
                    b = gate_buffers[n]
                    ve.wait_ge(exps[n].sem, exps[n].upto(x))
                    ve.tensor_reduce(b["sum"][:, :], b["e"][:, :, :], AX_X, ALU.add).then_inc(gates[n].sem, 1)
                    ve.wait_ge(gates[n].sem, gates[n].upto(x, 0))
                    ve.reciprocal(b["rec"][:, :], b["sum"][:, :]).then_inc(gates[n].sem, 1)
                    ve.wait_ge(gates[n].sem, gates[n].upto(x, 1))
                    ve.scalar_tensor_tensor(out=b["gate"][:, :, :], in0=b["e"][:, :, :], scalar=1.0 / RK,
                                            in1=b["rec"][:, :].unsqueeze(2).broadcast_to([P, NT, E]),
                                            op0=ALU.mult, op1=ALU.mult).then_inc(gates[n].sem, 1)
                    ve.wait_ge(gates[n].sem, gates[n].upto(x, 2))
                    if x.follows(1):
                        ve.wait_ge(ready[("g1", "g2")[n]].sem, ready[("g1", "g2")[n]].upto(x, back=1))
                    for i in range(NT):
                        p = ring.bank("r")[:, i * P:i * P + ER] if n == 0 else ring.bank("y", i)[:, M:M + ER]
                        zg = ve.tensor_tensor(
                            b["zg"][:, i, :, 0:ER].rearrange("p u (e r) -> p u e r", e=E),
                            p.rearrange("p (e r) -> p e r", e=E).unsqueeze(1).broadcast_to([P, 3, E, RK]),
                            b["gate"][:, i, :].unsqueeze(1).unsqueeze(3).broadcast_to([P, 3, E, RK]), ALU.mult)
                        if n or i == NT - 1:
                            zg.then_inc(gated[n].sem, 1)
                return step

            pipeline(ve, [(1, low_ot), (2, low_hid(0)), (2, low_hid(1)), (3, low_zt(1)), (2, low_hid(2)),
                          (3, finish), (1, residual(0)), (2, low_hid(3)), (2, low_hid(4)), (1, residual(1)),
                          (1, residual(2)), (2, low_hid(5)), (2, low_hid(6)), (2, low_hid(7)), (1, low_xt),
                          (0, divide(0)), (0, divide(1)), (0, divide(2)), (1, shift(0)), (1, gate(0)),
                          (2, shift(1)), (1, low_zt(0)), (2, gate(1))], peel=6)


class Tables:

    def __init__(self, banks, marks, semaphore):
        self.banks, self.marks, self.semaphore = banks, marks, semaphore


class Spill:
    pass


def computation(nc, ins, out, banks, marks, semaphore, slots):
    hpc = P // slots
    CH = HA // hpc
    with ExitStack() as ctx:
        def sb(name, shape):
            return ctx.enter_context(nc.sbuf_tensor(f"{name}_{slots}", shape, F32))

        t, spill = Tables(banks, marks, semaphore), Spill()
        t.ident = sb("ident", [P, P])
        t.bd = sb("bd", [P, CH // 2, P])
        t.bz = sb("bz", [P, hpc, R])
        t.diag = sb("diag", [P, slots])
        t.gather = sb("gather", [P, NT, P])
        t.reg = sb("reg", [P, 4])
        t.regd = sb("regd", [P, slots])
        t.rate = sb("rate", [P, 2])
        spill.h = nc.dram_tensor(f"h_spill_{slots}", (N, P, NT * M), F32, kind="Internal").ap()
        spill.pq = nc.dram_tensor(f"pq_spill_{slots}", (N, P, CH * T), F32, kind="Internal").ap()
        spill.w = nc.dram_tensor(f"w_spill_{slots}", (N * HA * slots, slots), F32, kind="Internal").ap()
        spill.z = nc.dram_tensor(f"z_spill_{slots}", (N * HA * slots, R), F32, kind="Internal").ap()
        spill.y = nc.dram_tensor(f"y_spill_{slots}", (N * HA * slots, R), F32, kind="Internal").ap()
        with ExitStack() as scope:
            t.systems = systems_tensors(nc, scope, slots)
            landmark_tables(nc, ins, slots, t)
            systems_phase(nc, ins, t, slots, spill)

        def parts(name, shape):
            return ctx.enter_context(nc.sbuf_tensor(f"{name}_{slots}", shape, FR))

        t.wo = parts("wo", [P, 2, 2, M])
        t.w1 = parts("w1", [P, 2, 2, F])
        t.w2 = parts("w2", [P, 2, FC, M + GE])
        t.bo, t.r1 = sb("bo", [P, M]), sb("r1", [P, 2, P])
        t.lora_b = parts("lora_b", [3 * G3, F + M])
        solve_phase(nc, ins, t, slots, spill)
        output_phase(nc, ins, out, t, slots, spill)


def build(nc, ins, out):
    with ExitStack() as ctx:
        banks = [ctx.enter_context(nc.psum_tensor(f"bank{i}", [P, 512], F32)) for i in range(NB)]
        number = ctx.enter_context(nc.sbuf_tensor("number", [1, 1], I32))
        marks = {name: ctx.enter_context(nc.sbuf_tensor("marks_" + name, [NL, width], F32))
                 for name, width in (("token", 1), ("count", 2), ("first", 1), ("rank", 1))}
        count_tokens(nc, ins, banks, marks, number)
        semaphores = {}

        def semaphore(name):
            if name not in semaphores:
                semaphores[name] = ctx.enter_context(nc.semaphore(name))
            return semaphores[name]

        tokens = nc.values_load(number[0:1, 0:1], min_val=1, max_val=NL)
        with nc.If(tokens <= SMALL):
            computation(nc, ins, out, banks, marks, semaphore, SMALL)
        with nc.Else():
            computation(nc, ins, out, banks, marks, semaphore, NL)


def kernel(x, txt, L0_tok_Wq_w, L0_tok_Wq_b, L0_tok_Wk_w, L0_tok_Wk_b, L0_tok_Wv_w, L0_tok_Wv_b, L0_tok_w_bias,
           L0_tok_out_w, L0_tok_out_b, L0_tok_ln_g, L0_tok_ln_b, L0_tok_local_mask, L0_attn_Wq, L0_attn_bq,
           L0_attn_Wk, L0_attn_bk, L0_attn_Wv, L0_attn_bv, L0_attn_Wo, L0_attn_bo, L0_attn_temperature,
           L0_attn_landmark_idx, L0_ffn_W1, L0_ffn_b1, L0_ffn_A1, L0_ffn_B1, L0_ffn_R1, L0_ffn_W2, L0_ffn_b2,
           L0_ffn_A2, L0_ffn_B2, L0_ffn_R2):
    import concourse.bacc as _bacc
    from concourse.bass_utils import run_bass_kernel_spmd as _run

    a = np.asarray

    def rows(w):
        w = a(w)
        return w.reshape(w.shape[0] // P, P, w.shape[1]).transpose(1, 0, 2)

    def experts(w):
        w = a(w)
        return w.transpose(1, 0, 2).reshape(w.shape[1], -1)

    one = np.ones((1, L * HT), np.float32)
    res = np.zeros((C + 1, HT, P), np.float32)
    for h in range(HT):
        own = slice(h % 2 * C, (h % 2 + 1) * C)
        res[:C, h, own], res[C, h, own] = np.eye(C), a(L0_tok_out_b)[h * C:(h + 1) * C]
    low = np.tril(np.ones((NL, NL), np.float32), -1)
    arrays = {
        "x": a(x).reshape(N, C, L * HT),
        "txt": a(txt),
        "wkv": np.concatenate([np.concatenate([a(L0_tok_Wk_w).T, a(L0_tok_Wv_w).T], 1),
                               np.concatenate([a(L0_tok_Wk_b), a(L0_tok_Wv_b)])[None]], 0),
        "wq_tok": np.concatenate([a(L0_tok_Wq_w).T, a(L0_tok_Wq_b)[None]], 0),
        "res": res,
        "ow": rows(L0_tok_out_w),
        "w_bias": rows(a(L0_tok_w_bias).T),
        "mask": rows(a(L0_tok_local_mask).T).copy().view(np.int32),
        "ln_g": a(L0_tok_ln_g)[None], "ln_b": a(L0_tok_ln_b)[None], "one_row": one,
        "wa_q": rows(a(L0_attn_Wq).T), "wa_k": rows(a(L0_attn_Wk).T), "wa_v": rows(a(L0_attn_Wv).T),
        "bq": a(L0_attn_bq).reshape(2, P).T, "bk": a(L0_attn_bk).reshape(2, P).T, "bv": a(L0_attn_bv)[None],
        "wo": rows(a(L0_attn_Wo).T), "bo": a(L0_attn_bo)[None],
        "temperature": a(L0_attn_temperature).reshape(1, 1), "idx": a(L0_attn_landmark_idx).reshape(1, NL),
        "w1": rows(L0_ffn_W1), "r1": rows(
            np.concatenate([experts(L0_ffn_A1), a(L0_ffn_R1), np.zeros((M, P - GATED), np.float32)], 1)),
        "w2": rows(np.concatenate([a(L0_ffn_W2), experts(L0_ffn_A2), a(L0_ffn_R2),
                                   np.zeros((F, GE - GATED), np.float32)], 1)),
        "lora_b": np.tile(np.concatenate([np.concatenate([a(L0_ffn_B1).reshape(ER, F), a(L0_ffn_B2).reshape(ER, M)], 1),
                                          np.concatenate([a(L0_ffn_b1), a(L0_ffn_b2)])[None],
                                          np.zeros((G3 - ER - 1, F + M), np.float32)], 0), (3, 1)),
        "ident": np.eye(P, dtype=np.float32), "tri": np.stack([low, low.T], 1),
        "iota": np.arange(T, dtype=np.float32)[None],
    }
    for slots in (SMALL, NL):
        arrays[f"bd{slots}"], arrays[f"bz{slots}"], arrays[f"diag{slots}"] = constants(slots)
    nc = _bacc.Bacc("TRN2", target_bir_lowering=False, num_devices=1)
    ins = {}
    feeds = {}
    for name, array in arrays.items():
        array = np.ascontiguousarray(array)
        feeds[f"in_{name}"] = array
        ins[name] = nc.dram_tensor(f"in_{name}", array.shape, mybir.dt.from_np(array.dtype), kind="ExternalInput").ap()
    out = nc.dram_tensor("out", (N, T, M), F32, kind="ExternalOutput").ap()
    build(nc, ins, out)
    return _run(nc, [feeds], core_ids=[0]).results[0]["out"]
```
